# Optimizing a Trainium2 kernel written in Bass

```python
import numpy as np
import jax
import jax.numpy as jnp

def _softmax(x, axis=-1):
    return jax.nn.softmax(x, axis=axis)

def _gelu(x):
    return jax.nn.gelu(x, approximate=True)

def _silu(x):
    return jax.nn.silu(x)

def _sigmoid(x):
    return jax.nn.sigmoid(x)

def _layernorm(x, axis=-1, eps=1e-05):
    m = jnp.mean(x, axis=axis, keepdims=True)
    v = jnp.var(x, axis=axis, keepdims=True)
    return (x - m) / jnp.sqrt(v + eps)

def _scatter_add(tgt, idx, src, axis=0):
    return tgt.at[idx].add(src)

def _segment_sum(src, seg, n):
    return jax.ops.segment_sum(src, seg, n)
kernel_name = 'mk_xattn_seq_d2_seqx_r4_09ae41'

def setup_inputs(seed: int=0):
    np.random.seed(seed)
    _w = jnp.asarray

    def _rec_inputs():
        import jax
        import jax.numpy as jnp
        _rk = jax.random.key(seed)
        x = 7.22e-05 + 1 * jax.random.normal(jax.random.fold_in(_rk, 1), (2, 1024, 256), jnp.float32)
        _lenS = 1024 - jax.random.randint(jax.random.fold_in(_rk, 7), (2,), 0, max(1, 1024 // 4) + 1, jnp.int32)
        _lenS2 = 77 - jax.random.randint(jax.random.fold_in(_rk, 8), (2,), 0, max(1, 77 // 4) + 1, jnp.int32)
        _ctx_1024P = jax.random.normal(jax.random.fold_in(_rk, 11), (2, 16, 256), jnp.float32)
        _ctx_1024c = jax.random.dirichlet(jax.random.fold_in(_rk, 511), 0.3 * jnp.ones((16,), jnp.float32), (2, 77))
        _ctx_1024t = jnp.einsum('bsk,bkd->bsd', _ctx_1024c, _ctx_1024P)
        _ctx_1024t = _ctx_1024t * jax.lax.rsqrt(jnp.mean(jnp.square(_ctx_1024t)) + 1e-12) * 0.953939
        ctx_1024 = 0.00208318 + 0.999174 * (_ctx_1024t + 0.3 * jax.random.normal(jax.random.fold_in(_rk, 611), (2, 77, 256), jnp.float32))
        return (x, ctx_1024)
    x, ctx_1024 = _rec_inputs()

    def _L0_xattn_setup():
        import jax, jax.numpy as jnp
        import numpy as np
        from functools import partial
        HEADS = 16
        DIM_HEAD = 64
        SCALE = DIM_HEAD ** (-0.5)
        MAX_ALLOWABLE = 256 * 256 * 8
        EPS = 1e-05

        def ln32(x, scale, bias):
            x32 = x.astype(jnp.float32)
            mean = jnp.mean(x32, axis=-1, keepdims=True)
            var = jnp.mean(jnp.square(x32 - mean), axis=-1, keepdims=True)
            y = (x32 - mean) * jax.lax.rsqrt(var + EPS) * scale.astype(jnp.float32) + bias.astype(jnp.float32)
            return y.astype(x.dtype)

        def heads_to_batch(t):
            b, s, d = t.shape
            return t.reshape(b, s, HEADS, d // HEADS).transpose(0, 2, 1, 3).reshape(b * HEADS, s, d // HEADS)

        def batch_to_heads(t):
            bh, s, dh = t.shape
            return t.reshape(bh // HEADS, HEADS, s, dh).transpose(0, 2, 1, 3).reshape(bh // HEADS, s, dh * HEADS)

        def _max_pow2(n):
            i = 1
            while n % 2 == 0:
                i *= 2
                n //= 2
            return i

        def sdpa(q, k, v):
            scores = jnp.einsum('bid,bjd->bij', q, k) * SCALE
            probs = jax.nn.softmax(scores, axis=2)
            return jnp.einsum('bij,bjd->bid', probs, v)

        def lowmem_attention(q, k, v):
            dimprod = q.shape[0] * q.shape[1] * k.shape[1]
            true_divisor = dimprod / MAX_ALLOWABLE
            if true_divisor < 1:
                n_splits = 1
            elif true_divisor >= q.shape[0]:
                n_splits = q.shape[0]
            else:
                nearest_pow2 = 2 ** np.round(np.log2(true_divisor))
                n_splits = int(min(_max_pow2(q.shape[0]), nearest_pow2))
            nq, nk, nv = [h.reshape(n_splits, h.shape[0] // n_splits, h.shape[-2], h.shape[-1]) for h in (q, k, v)]
            outs = jax.lax.scan(lambda c, a: (None, sdpa(*a)), None, (nq, nk, nv))[1]
            return outs.reshape(-1, outs.shape[-2], outs.shape[-1])

        def attention(x, ctx, Wq, Wkv, Wo, bo):
            q = x @ Wq
            k, v = jnp.split(ctx @ Wkv, 2, axis=-1)
            out = lowmem_attention(heads_to_batch(q), heads_to_batch(k), heads_to_batch(v))
            return batch_to_heads(out) @ Wo + bo

        def geglu_ff(x, Wff1, bff1, Wff2, bff2):
            h = x @ Wff1 + bff1
            lin, gelu = jnp.split(h, 2, axis=-1)
            h = lin * (gelu * jax.nn.sigmoid(1.702 * gelu))
            return h @ Wff2 + bff2
        key = jax.random.key(seed)
        ks = jax.random.split(key, 12)
        B, S, D, CTX = (4, 512, 256, 77)
        s = 0.02
        return {'hidden_states': jax.random.normal(ks[0], (B, S, D), jnp.float32), 'context': jax.random.normal(ks[1], (B, CTX, D), jnp.float32), 'Wq1': jax.random.normal(ks[2], (D, D), jnp.float32) * s, 'Wkv1': jax.random.normal(ks[3], (D, 2 * D), jnp.float32) * s, 'Wo1': jax.random.normal(ks[4], (D, D), jnp.float32) * s, 'bo1': jnp.zeros((D,), jnp.float32), 'Wq2': jax.random.normal(ks[5], (D, D), jnp.float32) * s, 'Wkv2': jax.random.normal(ks[6], (D, 2 * D), jnp.float32) * s, 'Wo2': jax.random.normal(ks[7], (D, D), jnp.float32) * s, 'bo2': jnp.zeros((D,), jnp.float32), 'Wff1': jax.random.normal(ks[8], (D, 8 * D), jnp.float32) * s, 'bff1': jnp.zeros((8 * D,), jnp.float32), 'Wff2': jax.random.normal(ks[9], (4 * D, D), jnp.float32) * s, 'bff2': jnp.zeros((D,), jnp.float32), 'ln1_s': jnp.ones((D,), jnp.float32), 'ln1_b': jnp.zeros((D,), jnp.float32), 'ln2_s': jnp.ones((D,), jnp.float32), 'ln2_b': jnp.zeros((D,), jnp.float32), 'ln3_s': jnp.ones((D,), jnp.float32), 'ln3_b': jnp.zeros((D,), jnp.float32)}
    _L0_xattn_all = _L0_xattn_setup()
    _L0_xattn_in = {k: v for k, v in _L0_xattn_all.items() if k in ('Wq1', 'Wkv1', 'Wo1', 'bo1', 'Wq2', 'Wkv2', 'Wo2', 'bo2', 'Wff1', 'bff1', 'Wff2', 'bff2', 'ln1_s', 'ln1_b', 'ln2_s', 'ln2_b', 'ln3_s', 'ln3_b')}
    del _L0_xattn_all

    def _L1_xattn_setup():
        import jax, jax.numpy as jnp
        import numpy as np
        H = 256
        EPS = 1e-08

        def rms_norm(x, w):
            rms = jax.lax.rsqrt(jnp.mean(x * x, axis=-1, keepdims=True) + EPS)
            return w * (x * rms)
        key = jax.random.key(seed)
        ks = jax.random.split(key, 12)
        B, S = (8, 512)
        scale = 1.0 / np.sqrt(H)
        return {'q': jax.random.normal(ks[0], (B, S, H), jnp.float32), 'k': jax.random.normal(ks[1], (B, S, H), jnp.float32), 'v': jax.random.normal(ks[2], (B, S, H), jnp.float32), 'Wq': jax.random.normal(ks[3], (H, H), jnp.float32) * scale, 'bq': jnp.zeros((H,), jnp.float32), 'Wk': jax.random.normal(ks[4], (H, H), jnp.float32) * scale, 'bk': jnp.zeros((H,), jnp.float32), 'Wv': jax.random.normal(ks[5], (H, H), jnp.float32) * scale, 'bv': jnp.zeros((H,), jnp.float32), 'Wfc': jax.random.normal(ks[6], (H, H), jnp.float32) * scale, 'bfc': jnp.zeros((H,), jnp.float32), 'norm_w': jnp.ones((H,), jnp.float32)}
    _L1_xattn_all = _L1_xattn_setup()
    _L1_xattn_in = {k: v for k, v in _L1_xattn_all.items() if k in ('Wq', 'bq', 'Wk', 'bk', 'Wv', 'bv', 'Wfc', 'bfc', 'norm_w')}
    del _L1_xattn_all
    return {'x': x, 'ctx_1024': ctx_1024, 'L0_xattn_Wq1': _L0_xattn_in['Wq1'], 'L0_xattn_Wkv1': _L0_xattn_in['Wkv1'], 'L0_xattn_Wo1': _L0_xattn_in['Wo1'], 'L0_xattn_bo1': _L0_xattn_in['bo1'], 'L0_xattn_Wq2': _L0_xattn_in['Wq2'], 'L0_xattn_Wkv2': _L0_xattn_in['Wkv2'], 'L0_xattn_Wo2': _L0_xattn_in['Wo2'], 'L0_xattn_bo2': _L0_xattn_in['bo2'], 'L0_xattn_Wff1': _L0_xattn_in['Wff1'], 'L0_xattn_bff1': _L0_xattn_in['bff1'], 'L0_xattn_Wff2': _L0_xattn_in['Wff2'], 'L0_xattn_bff2': _L0_xattn_in['bff2'], 'L0_xattn_ln1_s': _L0_xattn_in['ln1_s'], 'L0_xattn_ln1_b': _L0_xattn_in['ln1_b'], 'L0_xattn_ln2_s': _L0_xattn_in['ln2_s'], 'L0_xattn_ln2_b': _L0_xattn_in['ln2_b'], 'L0_xattn_ln3_s': _L0_xattn_in['ln3_s'], 'L0_xattn_ln3_b': _L0_xattn_in['ln3_b'], 'L1_xattn_Wq': _L1_xattn_in['Wq'], 'L1_xattn_bq': _L1_xattn_in['bq'], 'L1_xattn_Wk': _L1_xattn_in['Wk'], 'L1_xattn_bk': _L1_xattn_in['bk'], 'L1_xattn_Wv': _L1_xattn_in['Wv'], 'L1_xattn_bv': _L1_xattn_in['bv'], 'L1_xattn_Wfc': _L1_xattn_in['Wfc'], 'L1_xattn_bfc': _L1_xattn_in['bfc'], 'L1_xattn_norm_w': _L1_xattn_in['norm_w']}

def reference(x, ctx_1024, L0_xattn_Wq1, L0_xattn_Wkv1, L0_xattn_Wo1, L0_xattn_bo1, L0_xattn_Wq2, L0_xattn_Wkv2, L0_xattn_Wo2, L0_xattn_bo2, L0_xattn_Wff1, L0_xattn_bff1, L0_xattn_Wff2, L0_xattn_bff2, L0_xattn_ln1_s, L0_xattn_ln1_b, L0_xattn_ln2_s, L0_xattn_ln2_b, L0_xattn_ln3_s, L0_xattn_ln3_b, L1_xattn_Wq, L1_xattn_bq, L1_xattn_Wk, L1_xattn_bk, L1_xattn_Wv, L1_xattn_bv, L1_xattn_Wfc, L1_xattn_bfc, L1_xattn_norm_w):
    import jax
    import jax.numpy as jnp

    def _L0_xattn_ref(hidden_states, context, Wq1, Wkv1, Wo1, bo1, Wq2, Wkv2, Wo2, bo2, Wff1, bff1, Wff2, bff2, ln1_s, ln1_b, ln2_s, ln2_b, ln3_s, ln3_b):
        import jax, jax.numpy as jnp
        import numpy as np
        from functools import partial
        HEADS = 16
        DIM_HEAD = 64
        SCALE = DIM_HEAD ** (-0.5)
        MAX_ALLOWABLE = 256 * 256 * 8
        EPS = 1e-05

        def ln32(x, scale, bias):
            x32 = x.astype(jnp.float32)
            mean = jnp.mean(x32, axis=-1, keepdims=True)
            var = jnp.mean(jnp.square(x32 - mean), axis=-1, keepdims=True)
            y = (x32 - mean) * jax.lax.rsqrt(var + EPS) * scale.astype(jnp.float32) + bias.astype(jnp.float32)
            return y.astype(x.dtype)

        def heads_to_batch(t):
            b, s, d = t.shape
            return t.reshape(b, s, HEADS, d // HEADS).transpose(0, 2, 1, 3).reshape(b * HEADS, s, d // HEADS)

        def batch_to_heads(t):
            bh, s, dh = t.shape
            return t.reshape(bh // HEADS, HEADS, s, dh).transpose(0, 2, 1, 3).reshape(bh // HEADS, s, dh * HEADS)

        def _max_pow2(n):
            i = 1
            while n % 2 == 0:
                i *= 2
                n //= 2
            return i

        def sdpa(q, k, v):
            scores = jnp.einsum('bid,bjd->bij', q, k) * SCALE
            probs = jax.nn.softmax(scores, axis=2)
            return jnp.einsum('bij,bjd->bid', probs, v)

        def lowmem_attention(q, k, v):
            dimprod = q.shape[0] * q.shape[1] * k.shape[1]
            true_divisor = dimprod / MAX_ALLOWABLE
            if true_divisor < 1:
                n_splits = 1
            elif true_divisor >= q.shape[0]:
                n_splits = q.shape[0]
            else:
                nearest_pow2 = 2 ** np.round(np.log2(true_divisor))
                n_splits = int(min(_max_pow2(q.shape[0]), nearest_pow2))
            nq, nk, nv = [h.reshape(n_splits, h.shape[0] // n_splits, h.shape[-2], h.shape[-1]) for h in (q, k, v)]
            outs = jax.lax.scan(lambda c, a: (None, sdpa(*a)), None, (nq, nk, nv))[1]
            return outs.reshape(-1, outs.shape[-2], outs.shape[-1])

        def attention(x, ctx, Wq, Wkv, Wo, bo):
            q = x @ Wq
            k, v = jnp.split(ctx @ Wkv, 2, axis=-1)
            out = lowmem_attention(heads_to_batch(q), heads_to_batch(k), heads_to_batch(v))
            return batch_to_heads(out) @ Wo + bo

        def geglu_ff(x, Wff1, bff1, Wff2, bff2):
            h = x @ Wff1 + bff1
            lin, gelu = jnp.split(h, 2, axis=-1)
            h = lin * (gelu * jax.nn.sigmoid(1.702 * gelu))
            return h @ Wff2 + bff2
        x = hidden_states
        x = attention(ln32(x, ln1_s, ln1_b), ln32(x, ln1_s, ln1_b), Wq1, Wkv1, Wo1, bo1) + x
        x = attention(ln32(x, ln2_s, ln2_b), context, Wq2, Wkv2, Wo2, bo2) + x
        x = geglu_ff(ln32(x, ln3_s, ln3_b), Wff1, bff1, Wff2, bff2) + x
        return x

    def _L1_xattn_ref(q, k, v, Wq, bq, Wk, bk, Wv, bv, Wfc, bfc, norm_w):
        import jax, jax.numpy as jnp
        import numpy as np
        H = 256
        EPS = 1e-08

        def rms_norm(x, w):
            rms = jax.lax.rsqrt(jnp.mean(x * x, axis=-1, keepdims=True) + EPS)
            return w * (x * rms)
        Q = jnp.einsum('bsh,oh->bso', q, Wq) + bq
        K = jnp.einsum('bsh,oh->bso', k, Wk) + bk
        V = jnp.einsum('bsh,oh->bso', v, Wv) + bv
        scores = jnp.einsum('bqh,bkh->bqk', Q, K) / jnp.sqrt(jnp.float32(H))
        attn = jax.nn.softmax(scores, axis=-1)
        attn_out = jnp.einsum('bqk,bkh->bqh', attn, V)
        out = jnp.einsum('bsh,oh->bso', attn_out, Wfc) + bfc
        return rms_norm(out + q, norm_w)
    x = _L0_xattn_ref(x, ctx_1024, L0_xattn_Wq1, L0_xattn_Wkv1, L0_xattn_Wo1, L0_xattn_bo1, L0_xattn_Wq2, L0_xattn_Wkv2, L0_xattn_Wo2, L0_xattn_bo2, L0_xattn_Wff1, L0_xattn_bff1, L0_xattn_Wff2, L0_xattn_bff2, L0_xattn_ln1_s, L0_xattn_ln1_b, L0_xattn_ln2_s, L0_xattn_ln2_b, L0_xattn_ln3_s, L0_xattn_ln3_b)
    x = _L1_xattn_ref(x, ctx_1024, ctx_1024, L1_xattn_Wq, L1_xattn_bq, L1_xattn_Wk, L1_xattn_bk, L1_xattn_Wv, L1_xattn_bv, L1_xattn_Wfc, L1_xattn_bfc, L1_xattn_norm_w)
    return x

_drawn_inputs = setup_inputs


def setup_inputs(seed=0):
    import zlib

    import numpy as np

    out = dict(_drawn_inputs(seed))
    spreads = {'L0_xattn_bo1': (0.0, 0.425),
     'L0_xattn_bo2': (0.0, 0.398),
     'L0_xattn_bff1': (0.0, 0.525),
     'L0_xattn_bff2': (0.0, 0.334),
     'L0_xattn_ln1_s': (1.0, 0.6),
     'L0_xattn_ln1_b': (0.0, 0.8),
     'L0_xattn_ln2_s': (1.0, 0.6),
     'L0_xattn_ln2_b': (0.0, 2.0),
     'L0_xattn_ln3_s': (1.0, 0.6),
     'L0_xattn_ln3_b': (0.0, 2.0),
     'L1_xattn_bq': (0.0, 1.452),
     'L1_xattn_bk': (0.0, 2.0),
     'L1_xattn_bv': (0.0, 0.411),
     'L1_xattn_bfc': (0.0, 0.41),
     'L1_xattn_norm_w': (1.0, 0.2)}
    factors = {'L0_xattn_Wq1': 8.0,
     'L0_xattn_Wkv1': 5.247,
     'L0_xattn_Wo1': 5.506,
     'L0_xattn_Wq2': 64.0,
     'L0_xattn_Wkv2': 5.093,
     'L0_xattn_Wo2': 5.126}
    for name, (base, spread) in spreads.items():
        noise = np.random.default_rng([zlib.crc32(name.encode()), seed]).standard_normal(out[name].shape)
        drawn = base * np.exp(spread * noise) if base else spread * noise
        out[name] = jnp.asarray(drawn.astype(out[name].dtype))
    for name, factor in factors.items():
        out[name] = (out[name] * factor).astype(out[name].dtype)
    return out
```

```python
from contextlib import ExitStack

import concourse.bass as bass
from concourse import mybir

F32 = mybir.dt.float32
BF16 = mybir.dt.bfloat16
I32 = mybir.dt.int32
ACT = mybir.ActivationFunctionType
ALU = mybir.AluOpType
AX = mybir.AxisListType

P = 128
B, S, D = 2, 1024, 256
T = B * S
NC = D // P
TILES = T // P
BLK = 512
BLOCKS = T // BLK
TPB = BLK // P
H, DH = 16, 16
HG = 4
GROUPS = B * H // HG
GPB = GROUPS // B
KC = S // P
CTX = 77
CTXP = 96
F = 4 * D
FC = F // P
PARTS = 3
ROWS = 6 * DH
MROW = ROWS
KROWS = ROWS + PARTS
SCALE = 64 ** -0.5
L1_SCALE = 1.0 / 16.0
LN_EPS = 1e-5
RMS_EPS = 1e-8
Q_PART = (0, 0, 0, 1, 1, 2)
K_PART = (0, 1, 2, 0, 1, 0)

COL_LN = 0
COL_FF = 12
COL_BQ, COL_BK, COL_BV = 28, 30, 32
N_COLS = 34
ROW_BO1, ROW_BO2, ROW_BFF2, ROW_W, ROW_BFC = range(5)


def build(nc, a):
    with ExitStack() as ctx:
        def sb(name, shape, dt=F32):
            return ctx.enter_context(nc.sbuf_tensor(name, shape, dt))

        def sem(name):
            return ctx.enter_context(nc.semaphore(name))

        def scratch(name, shape, dt):
            return nc.dram_tensor(name, shape, dt).ap()

        q_d = scratch("q_parts", [GROUPS, PARTS, HG * DH, S], BF16)
        k_d = scratch("k_parts", [GROUPS, PARTS, HG * DH, S], BF16)
        q2_d = scratch("q2_parts", [GROUPS, PARTS, HG * DH, S], BF16)
        k2_d = scratch("k2_parts", [GPB, PARTS, HG * DH, B * CTX], BF16)
        v_d = scratch("v_groups", [GROUPS, P, KC, P], F32)

        x = sb("x", [P, TILES, D])
        tok = sb("tok", [P, TILES, D])
        xT = sb("xT", [P, NC, T])
        wq1, wkv1, wo1 = sb("wq1", [P, NC, D]), sb("wkv1", [P, NC, 2 * D]), sb("wo1", [P, NC, D])
        wq2, wkv2, wo2 = sb("wq2", [P, NC, D]), sb("wkv2", [P, NC, 2 * D]), sb("wo2", [P, NC, D])
        wff1, wff2 = sb("wff1", [P, NC, 2 * F]), sb("wff2", [P, FC, D])
        wql, wkT, wvT, wfcT = (sb(n, [P, NC, D]) for n in ("wql", "wkT", "wvT", "wfcT"))
        ctxT = sb("ctxT", [P, NC, B * CTX])
        cols = sb("cols", [P, N_COLS])
        rows = sb("rows", [P, 5, D])
        ident, identb = sb("ident", [P, P]), sb("identb", [P, P], BF16)
        ones = sb("ones", [P, P])
        bq_wide = sb("bq_wide", [P, NC, P])
        stack = sb("stack", [P, 4, HG, S], BF16)
        qs = stack[:, :, :, :].rearrange("p s h n -> p s (h n)").rearrange("p s (f h n) -> p s f h n", f=2, h=HG)
        k2 = sb("k2", [P, B, H, CTXP], BF16)
        v1 = sb("v1", [P, 2, KC, P])
        attT = v1[:, :, :, :].rearrange("p a b c -> p (a b c)").rearrange("p (r c n) -> p r c n", r=2, c=NC)
        v2 = sb("v2", [P, B, GPB, P])
        vstage = sb("vstage", [P, 2, H, 2 * DH])
        part = sb("part", [P, PARTS, PARTS, BLK], BF16)
        rest = sb("rest", [P, 2, BLK])
        probs = sb("probs", [P, 2, HG, BLK])
        outT = sb("outT", [P, 2, BLK])
        hidT = stack[:, :, :, :].rearrange("p a b c -> p (a b c)").bitcast(F32).rearrange(
            "p (r f n) -> p r f n", r=2, f=FC)
        gate = vstage[:, :, :, :].rearrange("p a h d -> p a (h d)")
        st = sb("st", [P, TPB, 6])
        mv = sb("mv", [P, 2, TPB, 2])
        var, half_var, rstd = (sb(n, [P, 2, TPB]) for n in ("var", "half_var", "rstd"))
        mm = sb("mm", [P, 2, 32])
        mrest = sb("mrest", [P, 2, 32])
        mpart = sb("mpart", [P, 2, PARTS * 32], BF16)
        mT = sb("mT", [P, 2, P], BF16)
        rec = sb("rec", [P, 2, TPB * HG])
        kT, vT, g1, cb = (sb(n, [P, NC, B * CTX]) for n in ("kT", "vT", "g1", "cb"))
        vw = sb("vw", [P, B, D])
        late = probs[:, :, :, :].rearrange("p a b c -> p (a b c)")

        def over(start, r, t, n):
            return late[:, start:start + r * t * n].rearrange("p (r t n) -> p r t n", r=r, t=t)
        o1 = over(0, 2, TPB, D)
        s1 = over(2 * TPB * D, 2, TPB, CTX)
        p1 = over(2 * TPB * (D + CTX), 2, TPB, CTX)
        p1T = sb("p1T", [P, 2, BLK])
        m1, nm1, sum1, r1, ss1 = (sb(n, [P, 2, TPB]) for n in ("m1", "nm1", "sum1", "r1", "ss1"))
        y1 = gate[:, :, :].rearrange("p a b -> p (a b)").rearrange("p (t d) -> p t d", d=D)
        sq = sb("sq", [P, D])

        ps = ctx.enter_context(nc.psum_tensor("ps", [P, 8, BLK], F32))
        ps_b = ps[:, 7, :].bitcast(BF16)
        ST, PV, MISC = 4, 6, 7

        x_in = [sem(f"x_in{i}") for i in range(BLOCKS)]
        w_in = {n: sem(f"{n}_in") for n in ("cols", "rows", "wqkv1", "wo1", "w2", "wo2", "wff", "wl1", "ctx", "k2")}
        k_in = [sem(f"k_in{i}") for i in range(2)]
        q_in = [[sem(f"q_in{h}{i}") for i in range(2)] for h in range(2)]
        v_in = [sem(f"v_in{i}") for i in range(2)]
        m_in = [sem("m_in0"), sem("m_in1")]
        q2_in = [sem(f"q2_in{i}") for i in range(4)]
        m2_in = [sem(f"m2_in{i}") for i in range(4)]
        part_out = [sem(f"part_out{i}") for i in range(PARTS)]
        v_out = [sem(f"v_out{i}") for i in range(2)]
        y_out = [sem("y_out0"), sem("y_out1")]
        pool_step, c_bq = sem("pool_step"), sem("c_bq")
        dve_step = sem("dve_step")
        var_ready, tok_ready = sem("var_ready"), sem("tok_ready")
        turn_full, turn_done = sem("turn_full"), sem("turn_done")
        pj_full, hi_done, rest_done, mid_done, lo_done = (sem(n) for n in ("pj_full", "hi_done", "rest_done", "mid_done", "lo_done"))
        v_full, v_done = sem("v_full"), sem("v_done")
        su_full, su_done = sem("su_full"), sem("su_done")
        s_full, s_red = sem("s_full"), sem("s_red")
        st_full, exp_done = sem("st_full"), sem("exp_done")
        pv_done, out_copied, out_turned = sem("pv_done"), sem("out_copied"), sem("out_turned")
        m_step, m_turned, m_copied = (sem(n) for n in ("m_step", "m_turned", "m_copied"))
        rec_done, att_done = sem("rec_done"), sem("att_done")
        s2_full, s2_red = sem("s2_full"), sem("s2_red")
        y_full, y_added, bias_added = sem("y_full"), sem("y_added"), sem("bias_added")
        ff_full, gate_done, hid_done = sem("ff_full"), sem("gate_done"), sem("hid_done")
        l_full, l_added, l_max, l_exp, l_turned, l_pT, l_pv, l_y, l_sq, l_out = (
            sem(f"l_{n}") for n in ("full", "added", "max", "exp", "turned", "pT", "pv", "y", "sq", "out"))

        block = ctx.enter_context(nc.Block())

        LN1, ATT1, LN2, ATT2, LN3, X3 = range(6)
        LAST_PAIR = GROUPS // 2 - 1

        def num(g):
            return 2 * g[0] + g[1]

        def after(g):
            return (g[0], 1) if g[1] == 0 else (g[0] + 1, 0)

        EARLY = 2
        LEAD = 4

        PROJ = [("k2", o, 0) for o in range(NC)]
        PROJ_1 = len(PROJ)
        PROJ += [(k, o, blk) for blk in range(BLOCKS) for k in "qk" for o in range(NC)]
        PROJ_2 = len(PROJ)
        PROJ += [("q2", o, blk) for blk in range(BLOCKS) for o in range(NC)]

        def width(u):
            return B * CTX if PROJ[u][0] == "k2" else BLK

        @block.sync
        def _(eng):
            def chunks(w):
                return w.rearrange("(c p) n -> p c n", p=P)

            x_v = a["x"].rearrange("b (t p) d -> p (b t) d", p=P)

            def load_x(blk):
                eng.dma_start(x[:, TPB * blk:TPB * blk + TPB, :], x_v[:, TPB * blk:TPB * blk + TPB, :]).then_inc(x_in[blk], 16)

            load_x(0)
            eng.dma_start(cols[:, :], a["cols"]).then_inc(w_in["cols"], 16)
            eng.dma_start(wq1[:, :, :], chunks(a["Wq1"])).then_inc(w_in["wqkv1"], 16)
            eng.dma_start(wkv1[:, :, :], chunks(a["Wkv1"])).then_inc(w_in["wqkv1"], 16)
            for blk in range(1, BLOCKS):
                load_x(blk)
            eng.dma_start(ctxT[:, :, :], chunks(a["ctxT"])).then_inc(w_in["ctx"], 16)
            eng.dma_start(wq2[:, :, :], chunks(a["Wq2"])).then_inc(w_in["w2"], 16)
            eng.dma_start(wkv2[:, :, :], chunks(a["Wkv2"])).then_inc(w_in["w2"], 16)
            for t, n in ((wql, "Wq"), (wkT, "WkT"), (wvT, "WvT"), (wfcT, "WfcT")):
                eng.dma_start(t[:, :, :], chunks(a[n])).then_inc(w_in["wl1"], 16)
            eng.dma_start(rows[:, :, :], a["rows"].partition_broadcast(P)).then_inc(w_in["rows"], 16)
            eng.dma_start(wo1[:, :, :], chunks(a["Wo1"])).then_inc(w_in["wo1"], 16)

            def store_parts(u):
                kind, o, blk = PROJ[u]
                eng.wait_ge(lo_done, u + 1)
                slot = u % PARTS
                for half in range(2):
                    src = part[64 * half:64 * half + 64, slot, :, 0:width(u)]
                    if kind == "k2":
                        dst = k2_d[2 * o + half]
                    else:
                        b, c0 = blk // 2, BLK * (blk % 2)
                        d = {"q": q_d, "k": k_d, "q2": q2_d}[kind]
                        dst = d[GPB * b + 2 * o + half][:, :, c0:c0 + BLK]
                    eng.dma_start(dst.rearrange("i r n -> r i n"), src).then_inc(part_out[slot], 16)

            def parts_stored(upto):
                for slot in range(PARTS):
                    n = len(range(slot, upto, PARTS))
                    eng.wait_ge(part_out[slot], 32 * n)

            def store_v(t):
                eng.wait_ge(v_done, t + 1)
                b, kc = t // KC, t % KC
                eng.dma_start(v_d[GPB * b:GPB * b + GPB, :, kc, :].rearrange("g p n -> p g n"),
                              vstage[:, t % 2, :, :].rearrange("p (g h) d -> p g (h d)", g=GPB)).then_inc(v_out[t % 2], 16)

            def load_stack(dst, src, which, done):
                i = 0
                while i < len(which):
                    n = 1
                    while i + n < len(which) and which[i + n] == which[i]:
                        n += 1
                    for j in range(n):
                        eng.dma_start(dst[DH * (i + j):DH * (i + j) + DH, :, :],
                                      src(which[i]).rearrange("(h r) n -> r h n", r=DH)).then_inc(done, 16)
                    i += n

            def load_group(g):
                G, slot = num(g), g[1]

                def of(d, cut):
                    if isinstance(G, int):
                        return lambda i: d[G, i, :, cut]
                    return lambda i: d[bass.ds(G, 1), i, :, cut].rearrange("o r n -> (o r) n")
                load_stack(stack[:, 2 + slot, :, :], of(k_d, slice(0, S)), K_PART, k_in[slot])
                for h in range(2):
                    cut = slice(BLK * h, BLK * h + BLK)
                    load_stack(qs[:, slot, h, :, :], of(q_d, cut), Q_PART, q_in[h][slot])

            def load_v(g):
                G, slot = num(g), g[1]
                src = v_d[G] if isinstance(G, int) else v_d[bass.ds(G, 1)].rearrange("o p k n -> (o p) k n")
                eng.dma_start(v1[:, slot, :, :], src).then_inc(v_in[slot], 16)

            def load_max(g, half):
                G, slot = num(g), g[1]
                eng.wait_ge(m_copied, 2 * G + half + 1)
                for i in range(PARTS):
                    eng.dma_start(qs[MROW + i:MROW + i + 1, slot, half, :, :].rearrange("o h n -> o (h n)"), mT[32 * i:32 * i + 16, half, :]).then_inc(m_in[half], 16)

            for u in range(PROJ_2):
                store_parts(u)
                blk, i = divmod(u - PROJ_1, 4)
                if u >= PROJ_1 and i == 3:
                    for t in range(TPB * blk, TPB * blk + TPB):
                        store_v(t)
            parts_stored(PROJ_2)
            load_group((0, 0))
            for s in range(2):
                eng.wait_ge(v_out[s], 16 * TILES // 2)
            load_v((0, 0))
            load_group((0, 1))
            load_v((0, 1))
            load_max((0, 0), 0)
            eng.dma_start(wo2[:, :, :], chunks(a["Wo2"])).then_inc(w_in["wo2"], 16)
            eng.dma_start(wff1[:, :, :], chunks(a["Wff1"])).then_inc(w_in["wff"], 16)
            eng.dma_start(wff2[:, :, :], chunks(a["Wff2"])).then_inc(w_in["wff"], 16)

            def self_group(g, loads):
                n = after(g)
                load_max(g, 1)
                if loads is not None:
                    load_max(n, 0)
                if loads:
                    eng.wait_ge(st_full, 64 * num(n))
                    two = (g[0] + 1, g[1])
                    load_group(two)
                    eng.wait_ge(pv_done, 16 * num(n))
                    load_v(two)

            with eng.Fori(0, LAST_PAIR) as gp:
                self_group((gp, 0), True)
                self_group((gp, 1), True)
            self_group((LAST_PAIR, 0), False)
            self_group((LAST_PAIR, 1), None)

            for u in range(PROJ_2, len(PROJ)):
                store_parts(u)
            parts_stored(len(PROJ))

            def load_q2(G):
                slot = G % 4
                for h in range(2):
                    load_stack(qs[:, slot, h, :, :], lambda i: q2_d[G, i, :, BLK * h:BLK * h + BLK], Q_PART, q2_in[slot])

            for G in range(4):
                load_q2(G)
            for G in range(GROUPS):
                eng.wait_ge(m_copied, 2 * GROUPS + G + 1)
                for i in range(PARTS):
                    eng.dma_start(stack[MROW + i:MROW + i + 1, G % 4, :, :].rearrange("o h n -> o (h n)"),
                                  mT[32 * i:32 * i + 32, G % 2, :]).then_inc(m2_in[G % 4], 16)
                if G >= 2 and G + 2 < GROUPS:
                    eng.wait_ge(st_full, 64 * GROUPS + 8 * (G - 1))
                    load_q2(G + 2)

            out_v = a["out"].rearrange("b (t p) d -> p (b t) d", p=P)
            for blk in range(BLOCKS):
                eng.wait_ge(l_out, TPB * (blk + 1))
                eng.dma_start(out_v[:, TPB * blk:TPB * blk + TPB, :], o1[:, blk % 2, :, :]).then_inc(y_out[blk % 2], 16)
            for s in range(2):
                eng.wait_ge(y_out[s], 16 * BLOCKS // 2)

        IDENTS_SET, V_PADS_SET, CONSTS = 4, 6, 15

        @block.gpsimd
        def _(eng):
            done = [0]

            def alone(ins):
                done[0] += 1
                ins.then_inc(pool_step, 1)
                eng.wait_ge(pool_step, done[0])

            for t in (ident, identb):
                alone(eng.memset(t[:, :], 0.0))
                alone(eng.affine_select(out=t[:, :], in_=t[:, :], compare_op=ALU.not_equal, fill=1.0, base=0,
                                        pattern=[[-1, P]], channel_multiplier=1))
            alone(eng.memset(vstage[:, :, :, :], 0.0))
            alone(eng.memset(vstage[:, :, :, DH:DH + 1], 1.0))
            alone(eng.memset(ones[:, :], 1.0))
            alone(eng.memset(mpart[:, :, :], 0.0))
            alone(eng.memset(stack[MROW:MROW + PARTS, 2:4, :, :], 1.0))
            alone(eng.memset(k2[:, :, :, :], 0.0))
            alone(eng.memset(k2[MROW:MROW + PARTS, :, :, 0:CTX], 1.0))
            alone(eng.memset(v2[:, :, :, :], 0.0))
            alone(eng.memset(v2[0:CTX, :, :, :].rearrange("p b g (h d) -> p (b g) h d", h=HG)[:, :, :, DH:DH + 1], 1.0))
            alone(eng.memset(vw[:, :, :], 0.0))
            alone(eng.memset(p1T[:, :, :], 0.0))
            assert done[0] == CONSTS
            eng.wait_ge(w_in["rows"], 16)
            for n, row in enumerate((ROW_BO1, ROW_BO2, ROW_BFF2)):
                for blk in range(BLOCKS):
                    eng.wait_ge(tok_ready, TPB * (BLOCKS * n + blk + 1))
                    xb = x[:, TPB * blk:TPB * blk + TPB, :]
                    eng.tensor_tensor(xb, xb, rows[:, row:row + 1, :].to_broadcast([P, TPB, D]), ALU.add).then_inc(bias_added, 1)
                if n == 0:
                    for slot in range(PARTS):
                        eng.wait_ge(part_out[slot], 32 * len(range(slot, PROJ_2, PARTS)))
                    for b in range(B):
                        for i in range(6):
                            for g in range(GPB):
                                eng.dma_start(k2[DH * i:DH * i + DH, b, HG * g:HG * g + HG, 0:CTX],
                                              k2_d[g, K_PART[i], :, CTX * b:CTX * b + CTX].rearrange("(h r) n -> r h n", r=DH)
                                              ).then_inc(w_in["k2"], 16)

        @block.tensor
        def _(eng):
            def by_group(i, c):
                b, j = divmod(i, KC)
                start = 2 * TPB * P * (NC * b + c) + P * j
                return tok[:, :, :].rearrange("p t d -> p (t d)")[:, start:start + P]

            def turn(phase, blk):
                k = BLOCKS * phase + blk
                if k >= 2:
                    eng.wait_ge(turn_done, 2 * k - 2)
                for c in range(NC):
                    for t in range(TPB):
                        i = TPB * blk + t
                        if c == 0:
                            if phase in (LN1, LN2, LN3):
                                n = (LN1, LN2, LN3).index(phase)
                                eng.wait_ge(tok_ready, TILES * n + i + 1)
                            elif phase == X3:
                                eng.wait_ge(y_added, 2 * TILES + i + 1)
                        src = by_group(i, c) if phase in (ATT1, ATT2) else (x if phase == X3 else tok)[:, i, P * c:P * c + P]
                        mm_ = eng.transpose(ps[:, 2 * (k % 2) + c, P * t:P * t + P], src, ident[:, :])
                    mm_.then_inc(turn_full, 1)

            def turned(phase, blk):
                eng.wait_ge(turn_done, 2 * (BLOCKS * phase + blk) + 2)

            def project(u):
                kind, o, blk = PROJ[u]
                w = {"q": wq1, "k": wkv1, "q2": wq2, "k2": wkv2}[kind]
                src = ctxT if kind == "k2" else xT
                n, c0 = width(u), BLK * blk
                if u >= 2:
                    eng.wait_ge(rest_done, u - 1)
                for c in range(NC):
                    mm_ = eng.matmul(ps[:, 4 + u % 2, 0:n], w[:, c, P * o:P * o + P], src[:, c, c0:c0 + n],
                                     start=(c == 0), stop=(c == NC - 1))
                mm_.then_inc(pj_full, 1)

            def values(t):
                if t >= 2:
                    eng.wait_ge(v_done, t - 1)
                for c in range(NC):
                    mm_ = eng.matmul(ps[:, 6 + t % 2, 0:D], xT[:, c, P * t:P * t + P], wkv1[:, c, D:2 * D],
                                     start=(c == 0), stop=(c == NC - 1))
                mm_.then_inc(v_full, 1)

            eng.sem_inc(out_turned, EARLY)
            eng.wait_ge(pool_step, IDENTS_SET)
            turn(LN1, 0)
            eng.wait_ge(w_in["ctx"], 16)
            eng.wait_ge(w_in["w2"], 32)
            for u in range(PROJ_1):
                project(u)
            eng.wait_ge(w_in["wqkv1"], 32)
            for blk in range(BLOCKS):
                turned(LN1, blk)
                for i in range(4):
                    project(PROJ_1 + 4 * blk + i)
                if blk + 1 < BLOCKS:
                    turn(LN1, blk + 1)
                for t in range(TPB * blk, TPB * blk + TPB):
                    values(t)

            su = [0]

            def setup(m, n, terms):
                k = su[0]
                su[0] += 1
                if k >= 2:
                    eng.wait_ge(su_done, k - 1)
                else:
                    eng.wait_ge(v_done, TILES - 1 + k)
                for i, (lhs, rhs) in enumerate(terms):
                    mm_ = eng.matmul(ps[0:m, 6 + k % 2, 0:n], lhs, rhs, start=(i == 0), stop=(i == len(terms) - 1))
                mm_.then_inc(su_full, 1)

            eng.wait_ge(w_in["wl1"], 64)
            cut = [slice(CTX * b, CTX * b + CTX) for b in range(B)]
            for b in range(B):
                setup(CTX, D, [(ctxT[:, c, cut[b]], wkv2[:, c, D:2 * D]) for c in range(NC)])
            for w in (wkT, wvT):
                for o in range(NC):
                    setup(P, B * CTX, [(w[:, c, P * o:P * o + P], ctxT[:, c, :]) for c in range(NC)])
            eng.wait_ge(su_done, 6)
            eng.wait_ge(c_bq, NC)
            for o in range(NC):
                setup(P, B * CTX, [(wql[:, c, P * o:P * o + P], kT[:, c, :]) for c in range(NC)])
            setup(P, B * CTX, [(bq_wide[:, c, :], kT[:, c, :]) for c in range(NC)])
            eng.wait_ge(w_in["rows"], 16)
            for b in range(B):
                setup(CTX, D, [(vT[:, c, cut[b]], wfcT[:, c, :]) for c in range(NC)]
                      + [(ones[0:1, 0:CTX], rows[0:1, ROW_BFC, :])])
            eng.wait_ge(su_done, 11)
            eng.wait_ge(rest_done, PROJ_2)

            def scores(g, j, first=False):
                G, slot = num(g), g[1]
                half, jj = divmod(j, 8)
                h, t0 = jj // 2, 2 * (jj % 2)
                if j == 0:
                    eng.wait_ge(k_in[slot], 96 * (g[0] + 1))
                if j in (0, 8):
                    eng.wait_ge(q_in[half][slot], 96 * (g[0] + 1))
                for i in range(2):
                    n = 32 * G + 2 * j + i
                    if not (first and n < 2):
                        eng.wait_ge(s_red, n - 1)
                    for kh in range(2):
                        mm_ = eng.matmul(ps[:, 2 * i + kh, :], qs[0:ROWS, slot, half, h, P * (t0 + i):P * (t0 + i) + P],
                                         stack[0:ROWS, 2 + slot, h, BLK * kh:BLK * kh + BLK], start=True, stop=True)
                        if kh == 1:
                            mm_.then_inc(s_full, 1)
                        yield

            def scores_t(g, k, h, first=False):
                G, slot = num(g), g[1]
                half, kc = divmod(k, KC)
                if kc == 0 and h == 0:
                    eng.wait_ge(m_in[half], 48 * (G + 1))
                if not (first and k == 0 and h < 2):
                    eng.wait_ge(exp_done, 64 * G + 4 * k + h - 1)
                eng.matmul(ps[:, ST + h % 2, :], stack[0:KROWS, 2 + slot, h, P * kc:P * kc + P],
                           qs[0:KROWS, slot, half, h, :], start=True, stop=True).then_inc(st_full, 1)

            def weigh(g, k):
                G, slot = num(g), g[1]
                half, kc = divmod(k, KC)
                eng.wait_ge(exp_done, 64 * G + 4 * k + 4)
                if k == 0:
                    eng.wait_ge(v_in[slot], 16 * (g[0] + 1))
                if kc == 0 and not (isinstance(G, int) and G == 0 and half == 0):
                    eng.wait_ge(out_copied, 2 * G + half)
                for h in range(HG):
                    mm_ = eng.matmul(ps[32 * h:32 * h + 32, PV, :], v1[:, slot, kc, 32 * h:32 * h + 32],
                                     probs[:, k % 2, h, :], start=(kc == 0), stop=(kc == KC - 1))
                mm_.then_inc(pv_done, 1)

            def turn_out(e, half, m_before):
                eng.wait_ge(out_copied, e + 1)
                eng.wait_ge(m_copied, m_before)
                for t in range(TPB):
                    mm_ = eng.transpose(ps[:, MISC, P * t:P * t + P], outT[:, half, P * t:P * t + P], ident[:, :])
                mm_.then_inc(out_turned, 1)

            def turn_max(g, half):
                e = 2 * num(g) + half
                eng.wait_ge(m_step, 4 * e + 4)
                eng.wait_ge(att_done, EARLY + e - 1)
                eng.transpose(ps_b[0:96, 0:P], mpart[:, half, :], identb[:, :]).then_inc(m_turned, 1)

            def step(g, k, lead=True, first=False):
                G = num(g)
                lead_g, j = (g, k + 16 - LEAD) if k < LEAD else (after(g), k - LEAD)
                four = scores(lead_g, j) if lead or k < LEAD else iter(())
                for h, n in enumerate((1, 2, 1, 0)):
                    scores_t(g, k, h, first)
                    for _ in range(n):
                        next(four, None)
                if k > 0:
                    weigh(g, k - 1)
                elif not first:
                    weigh(before(g), 15)
                if k == 2 and not first:
                    turn_out(2 * G - 1, 1, 2 * G + 1)
                if k == 5:
                    turn_max(g, 1)
                if k == 10:
                    turn_out(2 * G, 0, 2 * G + 2)
                if k == 13 and lead:
                    turn_max(after(g), 0)

            def before(g):
                return (g[0], 0) if g[1] == 1 else (g[0] - 1, 1)

            def self_group(g, lead=True, first=False):
                for k in range(LEAD, 16):
                    step(g, k, lead, first)
                if lead:
                    for k in range(LEAD):
                        step(after(g), k)

            eng.wait_ge(pool_step, CONSTS)
            for j in range(16 - LEAD):
                for _ in scores((0, 0), j, first=True):
                    pass
                if j == 9:
                    eng.wait_ge(m_step, 4)
                    eng.transpose(ps_b[0:96, 0:P], mpart[:, 0, :], identb[:, :]).then_inc(m_turned, 1)
            for k in range(LEAD):
                step((0, 0), k, first=True)
            with eng.Fori(0, LAST_PAIR) as gp:
                self_group((gp, 0))
                self_group((gp, 1))
            self_group((LAST_PAIR, 0))
            self_group((LAST_PAIR, 1), lead=False)
            weigh((LAST_PAIR, 1), 15)
            eng.wait_ge(att_done, EARLY + 2 * GROUPS - 1)
            turn_out(2 * GROUPS - 1, 1, 2 * GROUPS)

            def project_out(unit0, w, blk):
                turned((ATT1, ATT2)[unit0 // TILES], blk)
                for t in range(TPB):
                    n = unit0 + TPB * blk + t
                    if n >= 2:
                        eng.wait_ge(y_added, n - 1)
                    for c in range(NC):
                        mm_ = eng.matmul(ps[:, 6 + n % 2, 0:D], attT[:, blk % 2, c, P * t:P * t + P], w[:, c, :],
                                         start=(c == 0), stop=(c == NC - 1))
                    mm_.then_inc(y_full, 1)

            def out_and_turn(phase, unit0, w):
                turn(phase, 0)
                for blk in range(BLOCKS):
                    if blk + 1 < BLOCKS:
                        turn(phase, blk + 1)
                    project_out(unit0, w, blk)

            eng.wait_ge(att_done, EARLY + 2 * GROUPS)
            eng.wait_ge(w_in["wo1"], 16)
            eng.wait_ge(exp_done, 64 * GROUPS)
            out_and_turn(ATT1, 0, wo1)
            turn(LN2, 0)
            for blk in range(BLOCKS):
                if blk + 1 < BLOCKS:
                    turn(LN2, blk + 1)
                turned(LN2, blk)
                for o in range(NC):
                    project(PROJ_2 + NC * blk + o)

            def scores_2(G, tiles):
                b, slot = G // GPB, G % 4
                if tiles[0] == 0:
                    eng.wait_ge(q2_in[slot], 192 * (G // 4 + 1))
                for t in tiles:
                    n = KC * G + t
                    if n >= 4:
                        eng.wait_ge(s2_red, n - 3)
                    for h in range(HG):
                        mm_ = eng.matmul(ps[:, n % 4, CTX * h:CTX * h + CTX], qs[0:ROWS, slot, t // TPB, h, P * (t % TPB):P * (t % TPB) + P],
                                         k2[0:ROWS, b, HG * (G % GPB) + h, 0:CTX], start=True, stop=True)
                    mm_.then_inc(s2_full, 1)

            def scores_t2(G, half, pr):
                b, slot = G // GPB, G % 4
                if half == 0 and pr == 0:
                    eng.wait_ge(m2_in[slot], 48 * (G // 4 + 1))
                for i in range(2):
                    h = 2 * pr + i
                    eng.wait_ge(exp_done, 64 * GROUPS + 8 * G + 4 * half + h - 1)
                    eng.matmul(ps[0:CTXP, ST + i, :], k2[0:KROWS, b, HG * (G % GPB) + h, :],
                               qs[0:KROWS, slot, half, h, :], start=True, stop=True).then_inc(st_full, 1)

            def weigh_2(G, half):
                b = G // GPB
                eng.wait_ge(exp_done, 64 * GROUPS + 8 * G + 4 * half + 4)
                eng.wait_ge(out_copied, 2 * GROUPS + 2 * G + half)
                for h in range(HG):
                    mm_ = eng.matmul(ps[32 * h:32 * h + 32, PV, :], v2[0:CTXP, b, G % GPB, 32 * h:32 * h + 32],
                                     probs[0:CTXP, half, h, :], start=True, stop=True)
                mm_.then_inc(pv_done, 1)

            def turn_out_2(G, half):
                e = 2 * GROUPS + 2 * G + half
                eng.wait_ge(out_copied, e + 1)
                eng.wait_ge(att_done, EARLY + e)
                eng.wait_ge(m_copied, 2 * GROUPS + min(G + 2, GROUPS))
                for t in range(TPB):
                    mm_ = eng.transpose(ps[:, MISC, P * t:P * t + P], outT[:, half, P * t:P * t + P], ident[:, :])
                mm_.then_inc(out_turned, 1)

            def turn_max_2(G):
                eng.wait_ge(m_step, 8 * GROUPS + 4 * G + 4)
                eng.wait_ge(att_done, EARLY + 2 * GROUPS + 2 * max(G - 1, 0))
                if G >= 1:
                    eng.wait_ge(m_copied, 2 * GROUPS + G)
                eng.transpose(ps_b[0:96, 0:P], mpart[:, G % 2, :], identb[:, :]).then_inc(m_turned, 1)

            eng.wait_ge(w_in["k2"], 16 * 6 * GPB * B)
            eng.wait_ge(rest_done, len(PROJ))
            eng.wait_ge(turn_done, 2 * BLOCKS * (LN2 + 1))
            eng.wait_ge(y_added, TILES)
            for G in range(2):
                scores_2(G, range(0, 8))
                turn_max_2(G)
            for G in range(GROUPS):
                scores_t2(G, 0, 0)
                scores_t2(G, 0, 1)
                if G + 2 < GROUPS:
                    scores_2(G + 2, range(0, 4))
                weigh_2(G, 0)
                scores_t2(G, 1, 0)
                scores_t2(G, 1, 1)
                if G + 2 < GROUPS:
                    scores_2(G + 2, range(4, 8))
                turn_out_2(G, 0)
                weigh_2(G, 1)
                turn_out_2(G, 1)
                if G + 2 < GROUPS:
                    turn_max_2(G + 2)

            eng.wait_ge(att_done, EARLY + 4 * GROUPS)
            eng.wait_ge(w_in["wo2"], 16)
            eng.wait_ge(exp_done, 72 * GROUPS)
            out_and_turn(ATT2, TILES, wo2)
            for blk in range(BLOCKS):
                turn(LN3, blk)

            def widen(blk):
                for f in range(FC):
                    n = FC * blk + f
                    if n >= 2:
                        eng.wait_ge(hid_done, n - 1)
                    for i, col in enumerate((f, FC + f)):
                        for c in range(NC):
                            mm_ = eng.matmul(ps[:, 2 * (n % 2) + i, :], wff1[:, c, P * col:P * col + P],
                                             xT[:, c, BLK * blk:BLK * blk + BLK], start=(c == 0), stop=(c == NC - 1))
                    mm_.then_inc(ff_full, 1)

            def narrow(blk):
                eng.wait_ge(hid_done, FC * (blk + 1))
                for t in range(TPB):
                    n = 2 * TILES + TPB * blk + t
                    eng.wait_ge(y_added, n - 1)
                    for f in range(FC):
                        mm_ = eng.matmul(ps[:, 6 + n % 2, 0:D], hidT[:, blk % 2, f, P * t:P * t + P], wff2[:, f, :],
                                         start=(f == 0), stop=(f == FC - 1))
                    mm_.then_inc(y_full, 1)

            turned(LN3, BLOCKS - 1)
            eng.wait_ge(w_in["wff"], 32)
            widen(0)
            for blk in range(BLOCKS):
                if blk + 1 < BLOCKS:
                    widen(blk + 1)
                narrow(blk)

            def l1_scores(blk):
                turned(X3, blk)
                if blk >= 2:
                    eng.wait_ge(l_added, blk - 1)
                b = blk // 2
                for t in range(TPB):
                    for c in range(NC):
                        i = TPB * blk + t
                        mm_ = eng.matmul(ps[:, 4 + blk % 2, CTX * t:CTX * t + CTX], xT[:, c, P * i:P * i + P],
                                         g1[:, c, CTX * b:CTX * b + CTX], start=(c == 0), stop=(c == NC - 1))
                mm_.then_inc(l_full, 1)

            def l1_turn(blk):
                eng.wait_ge(l_exp, TPB * (blk + 1))
                if blk >= 1:
                    eng.wait_ge(l_pT, blk)
                for t in range(TPB):
                    mm_ = eng.transpose(ps[0:CTX, blk % 2, P * t:P * t + P], p1[:, blk % 2, t, :], ident[:, :])
                mm_.then_inc(l_turned, 1)

            def l1_weigh(blk):
                eng.wait_ge(l_pT, blk + 1)
                for t in range(TPB):
                    n = TPB * blk + t
                    if n >= 2:
                        eng.wait_ge(l_y, n - 1)
                    mm_ = eng.matmul(ps[:, 6 + n % 2, 0:D], p1T[0:CTXP, blk % 2, P * t:P * t + P],
                                     vw[0:CTXP, blk // 2, :], start=True, stop=True)
                    mm_.then_inc(l_pv, 1)

            eng.wait_ge(hid_done, FC * BLOCKS)
            for blk in range(BLOCKS):
                turn(X3, blk)
            eng.wait_ge(y_added, 3 * TILES)
            for blk in range(BLOCKS):
                l1_scores(blk)
                if blk == 0:
                    turned(X3, BLOCKS - 1)
                if blk >= 1:
                    l1_turn(blk - 1)
                    l1_weigh(blk - 1)
            l1_turn(BLOCKS - 1)
            l1_weigh(BLOCKS - 1)

        @block.scalar
        def _(eng):
            def turn_copy(phase, blk):
                for c in range(NC):
                    k = BLOCKS * phase + blk
                    eng.wait_ge(turn_full, 2 * k + c + 1)
                    src = ps[:, 2 * (k % 2) + c, :]
                    if phase in (ATT1, ATT2):
                        eng.activation(attT[:, blk % 2, c, :], src, ACT.Copy).then_inc(turn_done, 1)
                    elif phase == X3:
                        eng.activation(xT[:, c, BLK * blk:BLK * blk + BLK], src, ACT.Copy).then_inc(turn_done, 1)
                    else:
                        i = COL_LN + 4 * (LN1, LN2, LN3).index(phase)
                        eng.activation(xT[:, c, BLK * blk:BLK * blk + BLK], src, ACT.Identity,
                                       scale=cols[:, i + c:i + c + 1], bias=cols[:, i + 2 + c:i + 3 + c]).then_inc(turn_done, 1)

            def high(u):
                n, slot = width(u), u % PARTS
                eng.wait_ge(pj_full, u + 1)
                if u >= PARTS:
                    eng.wait_ge(part_out[slot], 32 * (u // PARTS))
                eng.activation(part[:, slot, 0, 0:n], ps[:, 4 + u % 2, 0:n], ACT.Copy).then_inc(hi_done, 1)

            def middle(u):
                n = width(u)
                eng.wait_ge(rest_done, u + 1)
                eng.activation(part[:, u % PARTS, 1, 0:n], rest[:, u % 2, 0:n], ACT.Copy).then_inc(mid_done, 1)

            def values(t):
                eng.wait_ge(v_full, t + 1)
                if t >= 2:
                    eng.wait_ge(v_out[t % 2], 16 * (t // 2))
                eng.activation(vstage[:, t % 2, :, 0:DH], ps[:, 6 + t % 2, 0:D].rearrange("p (h d) -> p h d", h=H),
                               ACT.Copy).then_inc(v_done, 1)

            eng.wait_ge(w_in["cols"], 16)
            turn_copy(LN1, 0)
            eng.wait_ge(pool_step, V_PADS_SET)
            for u in range(PROJ_1):
                high(u)
                middle(u)
            for blk in range(BLOCKS):
                for i in range(4):
                    u = PROJ_1 + 4 * blk + i
                    high(u)
                    if i > 0:
                        middle(u - 1)
                middle(PROJ_1 + 4 * blk + 3)
                if blk + 1 < BLOCKS:
                    turn_copy(LN1, blk + 1)
                for t in range(TPB * blk, TPB * blk + TPB):
                    values(t)

            su = [0]

            def setup_done(dst, m, n, bias=None, view=lambda v: v):
                k = su[0]
                su[0] += 1
                eng.wait_ge(su_full, k + 1)
                src = view(ps[0:m, 6 + k % 2, 0:n])
                if bias is None:
                    eng.activation(dst, src, ACT.Copy).then_inc(su_done, 1)
                else:
                    eng.activation(dst, src, ACT.Identity, bias=bias).then_inc(su_done, 1)

            eng.wait_ge(pool_step, CONSTS)
            for b in range(B):
                setup_done(v2[0:CTX, b, :, :].rearrange("p g (h d) -> p (g h) d", h=HG)[:, :, 0:DH], CTX, D,
                           view=lambda v: v.rearrange("p (h d) -> p h d", h=H))
            for dst, c0 in ((kT, COL_BK), (vT, COL_BV)):
                for o in range(NC):
                    setup_done(dst[:, o, :], P, B * CTX, bias=cols[:, c0 + o:c0 + o + 1])
            for o in range(NC):
                setup_done(g1[:, o, :], P, B * CTX)
            setup_done(cb[:, 0, :], P, B * CTX)
            for b in range(B):
                setup_done(vw[0:CTX, b, :], CTX, D)

            def exps(g, k, pr, first=False):
                G = num(g)
                for h in (2 * pr, 2 * pr + 1):
                    eng.wait_ge(st_full, 64 * G + 4 * k + h + 1)
                    if h == 0 and not (first and k < 2):
                        eng.wait_ge(pv_done, 16 * G + k - 1)
                    eng.activation(probs[:, k % 2, h, :], ps[:, ST + h % 2, :], ACT.Exp, scale=SCALE).then_inc(exp_done, 1)

            def out_copy(e, half):
                eng.wait_ge(pv_done, 8 * e + 8)
                eng.wait_ge(out_turned, EARLY + e - 1)
                eng.activation(outT[:, half, :], ps[:, PV, :], ACT.Copy).then_inc(out_copied, 1)

            def max_copy(e, half):
                eng.wait_ge(m_turned, e + 1)
                eng.activation(mT[0:96, half, :], ps_b[0:96, 0:P], ACT.Copy).then_inc(m_copied, 1)

            def step(g, k, lead=True, first=False):
                G = num(g)
                exps(g, k, 0, first)
                if k == 6:
                    max_copy(2 * G + 1, 1)
                if k == 14 and lead:
                    max_copy(2 * G + 2, 0)
                exps(g, k, 1, first)
                if k == 1 and not first:
                    out_copy(2 * G - 1, 1)
                if k == 9:
                    out_copy(2 * G, 0)

            def self_group(g, lead=True):
                for k in range(LEAD, 16):
                    step(g, k, lead)
                if lead:
                    for k in range(LEAD):
                        step(after(g), k)

            max_copy(0, 0)
            for k in range(LEAD):
                step((0, 0), k, first=True)
            with eng.Fori(0, LAST_PAIR) as gp:
                self_group((gp, 0))
                self_group((gp, 1))
            self_group((LAST_PAIR, 0))
            self_group((LAST_PAIR, 1), lead=False)
            out_copy(2 * GROUPS - 1, 1)

            for blk in range(BLOCKS):
                turn_copy(ATT1, blk)
            turn_copy(LN2, 0)
            for blk in range(BLOCKS):
                if blk + 1 < BLOCKS:
                    turn_copy(LN2, blk + 1)
                for o in range(NC):
                    u = PROJ_2 + NC * blk + o
                    high(u)
                    if u > PROJ_2:
                        middle(u - 1)
            middle(len(PROJ) - 1)

            def max_copy_2(G):
                eng.wait_ge(m_turned, 2 * GROUPS + G + 1)
                if G >= 2:
                    eng.wait_ge(m2_in[(G - 2) % 4], 48 * ((G - 2) // 4 + 1))
                eng.activation(mT[0:96, G % 2, :], ps_b[0:96, 0:P], ACT.Copy).then_inc(m_copied, 1)

            def exps_2(G, half, pr):
                for h in (2 * pr, 2 * pr + 1):
                    eng.wait_ge(st_full, 64 * GROUPS + 8 * G + 4 * half + h + 1)
                    if h == 0:
                        eng.wait_ge(pv_done, 16 * GROUPS + max(2 * G + half - 1, 0))
                    eng.activation(probs[0:CTXP, half, h, :], ps[0:CTXP, ST + h % 2, :], ACT.Exp, scale=SCALE).then_inc(exp_done, 1)

            def out_copy_2(G, half):
                e = 2 * GROUPS + 2 * G + half
                eng.wait_ge(pv_done, 16 * GROUPS + 2 * G + half + 1)
                eng.wait_ge(out_turned, EARLY + e - 1)
                eng.activation(outT[:, half, :], ps[:, PV, :], ACT.Copy).then_inc(out_copied, 1)

            for G in range(2):
                max_copy_2(G)
            for G in range(GROUPS):
                exps_2(G, 0, 0)
                exps_2(G, 0, 1)
                exps_2(G, 1, 0)
                out_copy_2(G, 0)
                exps_2(G, 1, 1)
                out_copy_2(G, 1)
                if G + 2 < GROUPS:
                    max_copy_2(G + 2)

            for phase in (ATT2, LN3):
                for blk in range(BLOCKS):
                    turn_copy(phase, blk)

            for n in range(FC * BLOCKS):
                f = n % FC
                eng.wait_ge(ff_full, n + 1)
                if n >= 2:
                    eng.wait_ge(hid_done, n - 1)
                i = COL_FF + FC + f
                eng.activation(gate[:, n % 2, :], ps[:, 2 * (n % 2) + 1, :], ACT.Gelu_apprx_sigmoid,
                               bias=cols[:, i:i + 1]).then_inc(gate_done, 1)

            def l1_exps(blk):
                eng.wait_ge(l_max, 2 * (blk + 1))
                s = blk % 2
                if blk >= 2:
                    eng.wait_ge(l_turned, blk - 1)
                for t in range(TPB):
                    eng.activation(p1[:, s, t, :], s1[:, s, t, :], ACT.Exp, scale=L1_SCALE, bias=nm1[:, s, t:t + 1],
                                   accum_out=sum1[:, s, t:t + 1]).then_inc(l_exp, 1)

            def l1_squares(blk):
                s = blk % 2
                for t in range(TPB):
                    n = TPB * blk + t
                    eng.wait_ge(l_y, n + 1)
                    if n >= 1:
                        eng.wait_ge(l_sq, n)
                    eng.activation(sq[:, :], y1[:, t, :], ACT.Square, accum_out=ss1[:, s, t:t + 1]).then_inc(l_sq, 1)

            for blk in range(BLOCKS):
                turn_copy(X3, blk)
            for blk in range(BLOCKS):
                l1_exps(blk)
                if blk >= 1:
                    l1_squares(blk - 1)
            l1_squares(BLOCKS - 1)

        @block.vector
        def _(eng):
            steps = [0]

            def link(ins):
                steps[0] += 1
                ins.then_inc(dve_step, 1)
                eng.wait_ge(dve_step, steps[0])

            def inverse_root(s, v, scale, e):
                y, w, h = rstd[:, s, :], var[:, s, :], half_var[:, s, :]
                link(eng.tensor_scalar(w, v, scale, e, ALU.mult, ALU.add))
                link(eng.tensor_scalar(y.bitcast(I32), w.bitcast(I32), -0.5, float(0x5F3759DF), ALU.mult, ALU.add))
                link(eng.tensor_scalar(h, w, -0.5, None, ALU.mult))
                for _ in range(3):
                    link(eng.tensor_tensor(w, y, y, ALU.mult))
                    link(eng.tensor_tensor(w, w, h, ALU.mult))
                    link(eng.scalar_tensor_tensor(out=y, in0=w, scalar=1.5, in1=y, op0=ALU.add, op1=ALU.mult))

            def stats(n, blk, t):
                k = BLOCKS * n + blk
                if k >= 1:
                    eng.wait_ge(var_ready, TPB * (k - 1) + t + 1)
                if k >= 2:
                    eng.wait_ge(tok_ready, TPB * (k - 1))
                link(eng.bn_stats(st[:, t, :], x[:, TPB * blk + t, :]))
                eng.bn_aggr(mv[:, blk % 2, t, :], st[:, t, :]).then_inc(var_ready, 1)

            def norm(n, blk):
                s = blk % 2
                eng.wait_ge(var_ready, TPB * (BLOCKS * n + blk + 1))
                inverse_root(s, mv[:, s, :, 1], 1.0, LN_EPS)
                for t in range(TPB):
                    i = TPB * blk + t
                    eng.tensor_scalar(tok[:, i, :], x[:, i, :], mv[:, s, t, 0:1], rstd[:, s, t:t + 1],
                                      ALU.subtract, ALU.mult).then_inc(tok_ready, 1)

            def remainder(u):
                n = width(u)
                eng.wait_ge(hi_done, u + 1)
                if u >= 2:
                    eng.wait_ge(mid_done, u - 1)
                    eng.wait_ge(lo_done, u - 1)
                eng.tensor_tensor(rest[:, u % 2, 0:n], ps[:, 4 + u % 2, 0:n], part[:, u % PARTS, 0, 0:n],
                                  ALU.subtract).then_inc(rest_done, 1)

            def low(u):
                n = width(u)
                eng.wait_ge(mid_done, u + 1)
                eng.wait_ge(rest_done, u + 1)
                eng.tensor_tensor(part[:, u % PARTS, 2, 0:n], rest[:, u % 2, 0:n], part[:, u % PARTS, 1, 0:n],
                                  ALU.subtract).then_inc(lo_done, 1)

            eng.sem_inc(att_done, EARLY)
            eng.wait_ge(x_in[0], 16)
            for t in range(TPB):
                stats(0, 0, t)
            norm(0, 0)
            eng.wait_ge(pool_step, CONSTS)
            eng.wait_ge(w_in["cols"], 16)
            for c in range(NC):
                eng.tensor_scalar(bq_wide[:, c, :], ones[:, :], cols[:, COL_BQ + c:COL_BQ + c + 1], None,
                                  ALU.mult).then_inc(c_bq, 1)
            for u in range(PROJ_1):
                remainder(u)
                low(u)
            for blk in range(BLOCKS):
                if blk + 1 < BLOCKS:
                    eng.wait_ge(x_in[blk + 1], 16)
                for i in range(4):
                    u = PROJ_1 + 4 * blk + i
                    remainder(u)
                    if i > 0:
                        low(u - 1)
                    if blk + 1 < BLOCKS:
                        if i < 2:
                            stats(0, blk + 1, 2 * i)
                            stats(0, blk + 1, 2 * i + 1)
                        if i == 3:
                            norm(0, blk + 1)
                low(PROJ_1 + 4 * blk + 3)

            def reduce_(g, j):
                G = num(g)
                half, jj = divmod(j, 8)
                h, t0 = jj // 2, 2 * (jj % 2)
                for i in range(2):
                    eng.wait_ge(s_full, 32 * G + 2 * j + i + 1)
                    k = 4 * h + t0 + i
                    eng.tensor_reduce(mm[:, half, k:k + 1], ps[:, 2 * i:2 * i + 2, :], AX.XY, ALU.max).then_inc(s_red, 1)

            def split_max(e, s, n):
                p = mpart[:, s, :].rearrange("p (i n) -> p i n", i=PARTS)[:, :, 0:n]
                eng.tensor_scalar(p[:, 0, :], mm[:, s, 0:n], -1.0, None, ALU.mult).then_inc(m_step, 1)
                eng.wait_ge(m_step, 4 * e + 1)
                eng.scalar_tensor_tensor(out=mrest[:, s, 0:n], in0=mm[:, s, 0:n], scalar=-1.0, in1=p[:, 0, :],
                                         op0=ALU.mult, op1=ALU.subtract).then_inc(m_step, 1)
                eng.wait_ge(m_step, 4 * e + 2)
                eng.tensor_copy(p[:, 1, :], mrest[:, s, 0:n]).then_inc(m_step, 1)
                eng.wait_ge(m_step, 4 * e + 3)
                eng.tensor_tensor(p[:, 2, :], mrest[:, s, 0:n], p[:, 1, :], ALU.subtract).then_inc(m_step, 1)

            def maxima(g, half):
                G = num(g)
                e = 2 * G + half
                eng.wait_ge(s_red, 32 * G + 16 * half + 16)
                split_max(e, half, 16)

            def step(g, k, lead=True, first=False):
                if k < LEAD:
                    reduce_(g, k + 16 - LEAD)
                elif lead:
                    reduce_(after(g), k - LEAD)
                if k == 3:
                    maxima(g, 1)
                    if not first:
                        attended(before(g), 1)
                if k == 11:
                    if lead:
                        maxima(after(g), 0)
                    attended(g, 0)

            def before(g):
                return (g[0], 0) if g[1] == 1 else (g[0] - 1, 1)

            def attended(g, half):
                e = 2 * num(g) + half
                eng.wait_ge(out_turned, EARLY + e + 1)
                v = ps[:, MISC, :].rearrange("p (t h d) -> p t h d", t=TPB, h=HG)
                r = rec[:, half, :].rearrange("p (t h) -> p t h", t=TPB)
                eng.reciprocal(r, v[:, :, :, DH]).then_inc(rec_done, 1)
                eng.wait_ge(rec_done, e + 1)
                pair = g[0] % (GROUPS // 2) if isinstance(g[0], int) else g[0]
                n = TPB * P
                start = 2 * n * pair + n * half
                dst = by_group[:, start:start + n] if isinstance(start, int) else by_group[:, bass.ds(start, n)]
                dst = dst.rearrange("p (t x) -> p t x", t=TPB)[:, :, 64 * g[1]:64 * g[1] + 64].rearrange("p t (h d) -> p t h d", h=HG)
                eng.tensor_tensor(dst, v[:, :, :, 0:DH], r.unsqueeze(3).to_broadcast([P, TPB, HG, DH]), ALU.mult).then_inc(att_done, 1)

            by_group = tok[:, :, :].rearrange("p t d -> p (t d)")

            def self_group(g, lead=True):
                for k in range(LEAD, 16):
                    step(g, k, lead)
                if lead:
                    for k in range(LEAD):
                        step(after(g), k)

            for j in range(16 - LEAD):
                reduce_((0, 0), j)
                if j == 7:
                    maxima((0, 0), 0)
            for k in range(LEAD):
                step((0, 0), k, first=True)
            with eng.Fori(0, LAST_PAIR) as gp:
                self_group((gp, 0))
                self_group((gp, 1))
            self_group((LAST_PAIR, 0))
            self_group((LAST_PAIR, 1), lead=False)
            attended((LAST_PAIR, 1), 1)

            def add(n, i):
                k = TILES * n + i
                eng.wait_ge(y_full, k + 1)
                eng.wait_ge(bias_added, BLOCKS * n + i // TPB + 1)
                eng.tensor_tensor(x[:, i, :], ps[:, 6 + k % 2, 0:D], x[:, i, :], ALU.add).then_inc(y_added, 1)

            def add_and_norm(n):
                for blk in range(BLOCKS):
                    for t in range(TPB):
                        add(n, TPB * blk + t)
                        if t > 0:
                            eng.wait_ge(y_added, TILES * n + TPB * blk + t)
                            stats(n + 1, blk, t - 1)
                    eng.wait_ge(y_added, TILES * n + TPB * blk + TPB)
                    stats(n + 1, blk, TPB - 1)
                    norm(n + 1, blk)

            add_and_norm(0)
            for u in range(PROJ_2, len(PROJ)):
                remainder(u)
                if u > PROJ_2:
                    low(u - 1)
            low(len(PROJ) - 1)

            def reduce_2(G, tiles):
                for t in tiles:
                    n = KC * G + t
                    eng.wait_ge(s2_full, n + 1)
                    dst = mm[:, G % 2, :].rearrange("p (f h t) -> p f h t", f=2, h=HG)[:, t // TPB, :, t % TPB]
                    eng.tensor_reduce(dst, ps[:, n % 4, 0:HG * CTX].rearrange("p (h n) -> p h n", h=HG),
                                      AX.X, ALU.max).then_inc(s2_red, 1)

            def maxima_2(G):
                eng.wait_ge(s2_red, KC * (G + 1))
                split_max(2 * GROUPS + G, G % 2, 32)

            for G in range(2):
                reduce_2(G, range(0, 8))
                maxima_2(G)
            for G in range(GROUPS):
                if G + 2 < GROUPS:
                    reduce_2(G + 2, range(0, 8))
                    maxima_2(G + 2)
                attended((GROUPS // 2 + G // 2, G % 2), 0)
                attended((GROUPS // 2 + G // 2, G % 2), 1)

            add_and_norm(1)

            def hidden(n):
                blk, f = divmod(n, FC)
                eng.wait_ge(gate_done, n + 1)
                eng.scalar_tensor_tensor(out=hidT[:, blk % 2, f, :], in0=ps[:, 2 * (n % 2), :],
                                         scalar=cols[:, COL_FF + f:COL_FF + f + 1], in1=gate[:, n % 2, :],
                                         op0=ALU.add, op1=ALU.mult).then_inc(hid_done, 1)

            for n in range(FC):
                hidden(n)
            for blk in range(BLOCKS):
                if blk + 1 < BLOCKS:
                    for n in range(FC * (blk + 1), FC * (blk + 2)):
                        hidden(n)
                for t in range(TPB):
                    add(2, TPB * blk + t)

            def l1_max(blk):
                s, b = blk % 2, blk // 2
                eng.wait_ge(l_full, blk + 1)
                if blk >= 2:
                    eng.wait_ge(l_exp, TPB * (blk - 1))
                eng.tensor_tensor(s1[:, s, :, :], ps[:, 4 + s, 0:TPB * CTX].rearrange("p (t n) -> p t n", t=TPB),
                                  cb[:, 0:1, CTX * b:CTX * b + CTX].to_broadcast([P, TPB, CTX]), ALU.add).then_inc(l_added, 1)
                eng.wait_ge(l_added, blk + 1)
                eng.tensor_reduce(m1[:, s, :], s1[:, s, :, :], AX.X, ALU.max).then_inc(l_max, 1)
                eng.wait_ge(l_max, 2 * blk + 1)
                eng.tensor_scalar(nm1[:, s, :], m1[:, s, :], -L1_SCALE, None, ALU.mult).then_inc(l_max, 1)

            def l1_probs(blk):
                s = blk % 2
                eng.wait_ge(l_turned, blk + 1)
                eng.tensor_copy(p1T[0:CTX, s, :], ps[0:CTX, s, :]).then_inc(l_pT, 1)
                link(eng.reciprocal(r1[:, s, :], sum1[:, s, :]))

            def l1_residual(blk):
                s = blk % 2
                for t in range(TPB):
                    n = TPB * blk + t
                    eng.wait_ge(l_pv, n + 1)
                    if blk >= 1:
                        eng.wait_ge(l_out, n - TPB + 1)
                    eng.scalar_tensor_tensor(out=y1[:, t, :], in0=ps[:, 6 + n % 2, 0:D], scalar=r1[:, s, t:t + 1],
                                             in1=x[:, n, :], op0=ALU.mult, op1=ALU.add).then_inc(l_y, 1)

            def l1_finish(blk):
                s = blk % 2
                eng.wait_ge(l_sq, TPB * (blk + 1))
                inverse_root(s, ss1[:, s, :], 1.0 / D, RMS_EPS)
                if blk >= 2:
                    eng.wait_ge(y_out[s], 16 * (blk // 2))
                for t in range(TPB):
                    eng.scalar_tensor_tensor(out=o1[:, s, t, :], in0=y1[:, t, :], scalar=rstd[:, s, t:t + 1],
                                             in1=rows[:, ROW_W, :], op0=ALU.mult, op1=ALU.mult).then_inc(l_out, 1)

            for blk in range(BLOCKS):
                l1_max(blk)
                if blk >= 1:
                    l1_probs(blk - 1)
                    l1_residual(blk - 1)
                    l1_finish(blk - 1)
            l1_probs(BLOCKS - 1)
            l1_residual(BLOCKS - 1)
            l1_finish(BLOCKS - 1)


def kernel(**inputs):
    import numpy as np
    import concourse.bacc as bacc
    from concourse.bass_utils import run_bass_kernel_spmd

    v = {k: np.asarray(t) for k, t in inputs.items()}
    l0 = {k[len("L0_xattn_"):]: t for k, t in v.items() if k.startswith("L0_xattn_")}
    l1 = {k[len("L1_xattn_"):]: t for k, t in v.items() if k.startswith("L1_xattn_")}

    def columns(t):
        return t.reshape(-1, P).T

    arrays = {
        "x": v["x"],
        "ctxT": v["ctx_1024"].transpose(2, 0, 1).reshape(D, B * CTX),
        "cols": np.concatenate(
            [columns(l0[n]) for n in ("ln1_s", "ln1_b", "ln2_s", "ln2_b", "ln3_s", "ln3_b", "bff1")]
            + [columns(l1[n]) for n in ("bq", "bk", "bv")], axis=1),
        "rows": np.stack([l0["bo1"], l0["bo2"], l0["bff2"], l1["norm_w"], l1["bfc"]]),
        "Wq": l1["Wq"], "WkT": l1["Wk"].T, "WvT": l1["Wv"].T, "WfcT": l1["Wfc"].T,
    }
    arrays.update({n: l0[n] for n in ("Wq1", "Wkv1", "Wo1", "Wq2", "Wkv2", "Wo2", "Wff1", "Wff2")})
    arrays = {f"in_{n}": np.ascontiguousarray(t) for n, t in arrays.items()}

    nc = bacc.Bacc("TRN2", target_bir_lowering=False, num_devices=1)
    aps = {n[3:]: nc.dram_tensor(n, t.shape, mybir.dt.from_np(t.dtype), kind="ExternalInput").ap()
           for n, t in arrays.items()}
    aps["out"] = nc.dram_tensor("out", (B, S, D), F32, kind="ExternalOutput").ap()
    build(nc, aps)
    result = run_bass_kernel_spmd(nc, [arrays], core_ids=[0])
    return result.results[0]["out"]
```

```python
from contextlib import ExitStack

import concourse.bass as bass
from concourse import mybir

F32 = mybir.dt.float32
BF16 = mybir.dt.bfloat16
I32 = mybir.dt.int32
ACT = mybir.ActivationFunctionType
ALU = mybir.AluOpType
AX = mybir.AxisListType

P = 128
B, S, D = 2, 1024, 256
T = B * S
NC = D // P
TILES = T // P
BLK = 512
BLOCKS = T // BLK
TPB = BLK // P
H, DH = 16, 16
HG = 4
GROUPS = B * H // HG
GPB = GROUPS // B
KC = S // P
CTX = 77
CTXP = 96
F = 4 * D
FC = F // P
PARTS = 3
RING = 5
ROWS = 6 * DH
MROW = ROWS
KROWS = ROWS + PARTS
SCALE = 64 ** -0.5
L1_SCALE = 1.0 / 16.0
LN_EPS = 1e-5
RMS_EPS = 1e-8
Q_PART = (0, 0, 0, 1, 1, 2)
K_PART = (0, 1, 2, 0, 1, 0)
PAIRS = len(Q_PART)
RUNS = PARTS

COL_LN = 0
COL_FF = 12
COL_BQ, COL_BK, COL_BV = 28, 30, 32
N_COLS = 34
ROW_BO1, ROW_BO2, ROW_BFF2, ROW_W, ROW_BFC = range(5)


def build(nc, a):
    with ExitStack() as ctx:
        def sb(name, shape, dt=F32):
            return ctx.enter_context(nc.sbuf_tensor(name, shape, dt))

        def sem(name):
            return ctx.enter_context(nc.semaphore(name))

        def scratch(name, shape, dt):
            return nc.dram_tensor(name, shape, dt).ap()

        q_d, q2_d = (scratch(n, [2, B * NC, PARTS, P, BLK], BF16) for n in ("q_parts", "q2_parts"))
        k_d = scratch("k_parts", [B * NC, PARTS, P, S], BF16)
        k2_d = scratch("k2_parts", [NC, PARTS, P, B * CTX], BF16)
        v_d = scratch("v_groups", [P, KC, GROUPS * P], F32)

        x = sb("x", [P, TILES, D])
        tok = sb("tok", [P, TILES, D])
        xT = sb("xT", [P, NC, T])
        wkv1, wo1 = sb("wkv1", [P, NC, 2 * D]), sb("wo1", [P, NC, D])
        wq2, wkv2, wo2 = sb("wq2", [P, NC, D]), sb("wkv2", [P, NC, 2 * D]), sb("wo2", [P, NC, D])
        wff1, wff2 = sb("wff1", [P, NC, 2 * F]), sb("wff2", [P, FC, D])
        early = sb("early", [P, 5 * NC * D + 4 * 2 * D])
        wql, wkT, wvT, wfcT, wq1 = (early[:, i * NC * D:(i + 1) * NC * D].rearrange("p (c n) -> p c n", c=NC) for i in range(5))
        vstage = early[:, 5 * NC * D:5 * NC * D + 8 * D].rearrange("p (t h d) -> p t h d", t=4, h=H)
        ctxT = sb("ctxT", [P, NC, B * CTX])
        cols = sb("cols", [P, N_COLS])
        rows = sb("rows", [P, 5, D])
        ident, identb = sb("ident", [P, P]), sb("identb", [P, P], BF16)
        ones = sb("ones", [P, P])
        bq_wide = sb("bq_wide", [P, NC, P])
        stack = sb("stack", [P, 4, HG, S], BF16)
        qs = stack[:, :, :, :].rearrange("p s h n -> p s (h n)").rearrange("p s (f h n) -> p s f h n", f=2, h=HG)
        k2 = sb("k2", [P, B, H, CTXP], BF16)
        v1 = sb("v1", [P, 2, KC, P])
        attT = (wkv1, wkv2)
        v2 = sb("v2", [P, B, GPB, P])
        rest = sb("rest", [P, 2, BLK])
        probs = sb("probs", [P, 2, HG, BLK])
        def ring(v):
            return v.bitcast(BF16)[:, 0:RING * PARTS * BLK].rearrange("p (s i n) -> p s i n", s=RING, i=PARTS)
        part_1, part_2 = ring(probs[:, :, :, :].rearrange("p a b c -> p (a b c)")), ring(early[:, :])
        outT = sb("outT", [P, 2, BLK])
        hidT = stack[:, :, :, :].rearrange("p a b c -> p (a b c)").bitcast(F32).rearrange(
            "p (r f n) -> p r f n", r=2, f=FC)
        gate = vstage[:, 0:2, :, :].rearrange("p a h d -> p a (h d)")
        st = sb("st", [P, TPB, 6])
        mv = sb("mv", [P, 2, TPB, 2])
        var, half_var, rstd = (sb(n, [P, 2, TPB]) for n in ("var", "half_var", "rstd"))
        mm = sb("mm", [P, 2, 32])
        mrest = sb("mrest", [P, 2, 32])
        mpart = sb("mpart", [P, 2, PARTS * 32], BF16)
        mT = sb("mT", [P, 2, P], BF16)
        rec = sb("rec", [P, 2, TPB * HG])
        kT, vT, g1, cb = (sb(n, [P, NC, B * CTX]) for n in ("kT", "vT", "g1", "cb"))
        vw = sb("vw", [P, B, D])
        late = probs[:, :, :, :].rearrange("p a b c -> p (a b c)")

        def over(start, r, t, n):
            return late[:, start:start + r * t * n].rearrange("p (r t n) -> p r t n", r=r, t=t)
        o1 = over(0, 2, TPB, D)
        s1 = over(2 * TPB * D, 2, TPB, CTX)
        p1 = over(2 * TPB * (D + CTX), 2, TPB, CTX)
        p1T = sb("p1T", [P, 2, BLK])
        m1, nm1, sum1, r1, ss1 = (sb(n, [P, 2, TPB]) for n in ("m1", "nm1", "sum1", "r1", "ss1"))
        y1 = gate[:, :, :].rearrange("p a b -> p (a b)").rearrange("p (t d) -> p t d", d=D)
        sq = sb("sq", [P, D])

        ps = ctx.enter_context(nc.psum_tensor("ps", [P, 8, BLK], F32))
        ps_b = ps[:, 7, :].bitcast(BF16)
        ST, PV, MISC = 4, 6, 7
        CHAIN = 2

        x_in = [sem(f"x_in{i}") for i in range(BLOCKS)]
        w_in = {n: sem(f"{n}_in") for n in ("cols", "rows", "wqkv1", "wo1", "w2", "wo2", "wff", "wl1", "ctx", "k2")}
        k_in = [sem(f"k_in{i}") for i in range(2)]
        q_in = [[sem(f"q_in{h}{i}") for i in range(2)] for h in range(2)]
        v_in = [sem(f"v_in{i}") for i in range(2)]
        m_in = [sem("m_in0"), sem("m_in1")]
        q2_in = [sem(f"q2_in{i}") for i in range(4)]
        m2_in = [sem(f"m2_in{i}") for i in range(4)]
        part_out = [sem(f"part_out{i}") for i in range(RING)]
        v_out = [sem(f"v_out{i}") for i in range(2)]
        y_out = [sem("y_out0"), sem("y_out1")]
        pool_step, c_bq = sem("pool_step"), sem("c_bq")
        dve_step = sem("dve_step")
        var_ready, tok_ready = sem("var_ready"), sem("tok_ready")
        turn_full, turn_done = sem("turn_full"), sem("turn_done")
        pj_full, hi_done, rest_done, mid_done, lo_done = (sem(n) for n in ("pj_full", "hi_done", "rest_done", "mid_done", "lo_done"))
        v_full, v_done = sem("v_full"), sem("v_done")
        su_full, su_done = sem("su_full"), sem("su_done")
        s_full, s_red = sem("s_full"), sem("s_red")
        st_full, exp_done = sem("st_full"), sem("exp_done")
        pv_done, out_copied, out_turned = sem("pv_done"), sem("out_copied"), sem("out_turned")
        m_step, m_turned, m_copied = (sem(n) for n in ("m_step", "m_turned", "m_copied"))
        rec_done, att_done = sem("rec_done"), sem("att_done")
        s2_full, s2_red = sem("s2_full"), sem("s2_red")
        y_full, y_added, bias_added = sem("y_full"), sem("y_added"), sem("bias_added")
        ff_gate, ff_full, gate_done, hid_done = sem("ff_gate"), sem("ff_full"), sem("gate_done"), sem("hid_done")
        l_full, l_added, l_max, l_exp, l_turned, l_pT, l_pv, l_y, l_sq, l_out = (
            sem(f"l_{n}") for n in ("full", "added", "max", "exp", "turned", "pT", "pv", "y", "sq", "out"))

        block = ctx.enter_context(nc.Block())

        LN1, ATT1, LN2, ATT2, LN3, X3 = range(6)
        LAST_PAIR = GROUPS // 2 - 1

        def num(g):
            return 2 * g[0] + g[1]

        def after(g):
            return (g[0], 1) if g[1] == 0 else (g[0] + 1, 0)

        Q2_SLOT = (0, 2, 1, 3)

        def q2_slot(G, half):
            return qs[:, Q2_SLOT[G % 4], half, :, :]

        TURNS = [(LN1, blk) for blk in range(BLOCKS)]
        TURNS += [(phase, 2 * b + i) for att, ln in ((ATT1, LN2), (ATT2, LN3)) for b in range(B)
                  for phase in (att, ln) for i in range(2)]
        TURNS += [(X3, blk) for blk in range(BLOCKS)]

        def turn_bank(phase, blk, c):
            return 2 * (blk % 2) + c if phase in (LN1, X3) else CHAIN + c

        def out_bank(k):
            return (CHAIN if k < 2 * TILES else 6) + k % 2

        def proj_bank(u):
            return (4 if u < PROJ_2 else CHAIN) + u % 2

        def part(u):
            return (part_1 if u < PROJ_2 else part_2)[:, u % RING, :, 0:width(u)]

        CHAIN_1, CHAIN_2 = 17, 12
        TAIL = (1, 1, 1, 1, 1, 1, 1, 2, 2, 2, 2, 2)
        AHEAD, FIRST_S2 = 6, (0, 1, 0, 1, 0, 1, 0, 1) * 2
        UNITS = 8

        def pieces(G, n):
            if G == 0:
                return 1 if n in (0, 4, 6) else 0
            return 1 if G >= GROUPS - 3 and n % 2 == 0 else 0

        FF_PIECES = (1, 2, 2, 2, 2, 1, 1, 1)
        assert sum(TAIL) == CHAIN_1 == AHEAD + sum(FIRST_S2) + sum(pieces(0, n) for n in range(UNITS))
        assert sum(FF_PIECES) == CHAIN_2 == sum(pieces(G, n) for G in range(1, GROUPS) for n in range(UNITS))

        def ff_bank(n, i):
            return (4, 0)[n % 2] + i

        def st_bank(g, k, h):
            tail = isinstance(g[0], int) and g == (LAST_PAIR, 1) and k >= LEAD
            return (ST, ST + 1, 0, 1)[h] if tail else ST + h % 2

        EARLY = 2
        LEAD = 4

        PROJ = [(k, o, blk) for blk in range(2) for k in "qk" for o in range(NC)]
        PROJ_B0 = len(PROJ)
        PROJ += [("k2", o, 0) for o in range(NC)]
        PROJ_K2 = len(PROJ)
        PROJ += [(k, o, blk) for blk in range(2, BLOCKS) for k in "qk" for o in range(NC)]
        PROJ_2 = len(PROJ)
        PROJ += [("q2", o, blk) for blk in range(BLOCKS) for o in range(NC)]

        FIRST_PAIR = 2
        SETUP_1, SETUP_2 = 6, 5

        def first_of(blk):
            return TPB * blk if blk < 2 else PROJ_K2 + TPB * (blk - 2)

        def width(u):
            return B * CTX if PROJ[u][0] == "k2" else BLK

        def advance(chain, n):
            for _ in range(n):
                next(chain)

        def parts_stored(eng, upto):
            for slot in range(RING):
                eng.wait_ge(part_out[slot], 16 * len(range(slot, upto, RING)))

        @block.sync
        def _(eng):
            def chunks(w):
                return w.rearrange("(c p) n -> p c n", p=P)

            x_v = a["x"].rearrange("b (t p) d -> p (b t) d", p=P)

            def load_x(blk):
                eng.dma_start(x[:, TPB * blk:TPB * blk + TPB, :], x_v[:, TPB * blk:TPB * blk + TPB, :]).then_inc(x_in[blk], 16)

            load_x(0)
            load_x(1)
            eng.dma_start(cols[:, :], a["cols"]).then_inc(w_in["cols"], 16)
            eng.dma_start(wq1[:, :, :], chunks(a["Wq1"])).then_inc(w_in["wqkv1"], 16)
            eng.dma_start(wkv1[:, :, :], chunks(a["Wkv1"])).then_inc(w_in["wqkv1"], 16)
            for blk in range(2, BLOCKS):
                load_x(blk)
            eng.dma_start(ctxT[:, :, :], chunks(a["ctxT"])).then_inc(w_in["ctx"], 16)
            eng.dma_start(wq2[:, :, :], chunks(a["Wq2"])).then_inc(w_in["w2"], 16)
            eng.dma_start(wkv2[:, :, :], chunks(a["Wkv2"])).then_inc(w_in["w2"], 16)
            for t, n in ((wql, "Wq"), (wkT, "WkT"), (wvT, "WvT"), (wfcT, "WfcT")):
                eng.dma_start(t[:, :, :], chunks(a[n])).then_inc(w_in["wl1"], 16)
            eng.dma_start(rows[:, :, :], a["rows"].partition_broadcast(P)).then_inc(w_in["rows"], 16)
            eng.dma_start(wo1[:, :, :], chunks(a["Wo1"])).then_inc(w_in["wo1"], 16)

            def store_parts(u):
                kind, o, blk = PROJ[u]
                eng.wait_ge(lo_done, u + 1)
                slot = u % RING
                if kind == "k2":
                    dst = k2_d[o]
                elif kind == "k":
                    dst = k_d[NC * (blk // 2) + o, :, :, BLK * (blk % 2):BLK * (blk % 2) + BLK]
                else:
                    dst = {"q": q_d, "q2": q2_d}[kind][blk % 2, NC * (blk // 2) + o]
                eng.dma_start(dst.rearrange("i r n -> r i n"), part(u)).then_inc(part_out[slot], 16)

            def store_v(t):
                eng.wait_ge(v_done, t + 2)
                b, kc, pair = t // KC, t % KC, t // 2 % 2
                eng.dma_start(v_d[:, kc:kc + 2, GPB * P * b:GPB * P * b + GPB * P],
                              vstage[:, 2 * pair:2 * pair + 2, :, :].rearrange("p t h d -> p t (h d)")).then_inc(v_out[pair], 16)

            def load_stack(dst, src, heads, which, done):
                i = 0
                while i < PAIRS:
                    rise = int(i + 1 < PAIRS and which[i + 1] > which[i])
                    n = 1
                    while i + n < PAIRS and which[i + n] == which[i] + rise * n:
                        n += 1
                    rows = src[which[i]:which[i] + (n if rise else 1)].rearrange("i (r h) n -> (i r) h n", r=DH)
                    rows = rows[:, heads, :].rearrange("r h n -> r (h n)")
                    if not rise:
                        rows = rows.unsqueeze(0).to_broadcast([n, DH, rows.shape[-1]])
                    eng.dma_start(dst[DH * i:DH * (i + n), :, :].rearrange("r h n -> r (h n)"), rows).then_inc(done, 16)
                    i += n

            def load_group(g):
                pair, slot = g

                def of(d):
                    return d[bass.ds(pair, 1)].rearrange("o i p n -> (o i) p n")
                heads = slice(HG * slot, HG * slot + HG)
                load_stack(stack[:, 2 + slot, :, :], of(k_d), heads, K_PART, k_in[slot])
                for h in range(2):
                    load_stack(qs[:, slot, h, :, :], of(q_d[h]), heads, Q_PART, q_in[h][slot])

            def load_v(g):
                G, slot = num(g), g[1]
                eng.dma_start(v1[:, slot, :, :], v_d[:, :, bass.ds(P * G, P)]).then_inc(v_in[slot], 16)

            def load_max(g, half):
                G, slot = num(g), g[1]
                eng.wait_ge(m_copied, 2 * G + half + 1)
                for i in range(PARTS):
                    eng.dma_start(qs[MROW + i:MROW + i + 1, slot, half, :, :].rearrange("o h n -> o (h n)"), mT[32 * i:32 * i + 16, half, :]).then_inc(m_in[half], 16)

            def v_stored(tiles):
                for s in range(2):
                    eng.wait_ge(v_out[s], 16 * tiles // 4)

            for blk in range(BLOCKS):
                if blk == 2:
                    parts_stored(eng, PROJ_B0)
                    load_group((0, 0))
                    v_stored(KC)
                    load_v((0, 0))
                    for u in range(PROJ_B0, PROJ_K2):
                        store_parts(u)
                for i in range(TPB):
                    store_parts(first_of(blk) + i)
                    if i % 2 == 1:
                        store_v(TPB * blk + i - 1)
                if blk == 2:
                    load_group((0, 1))
                    load_v((0, 1))
            parts_stored(eng, PROJ_2)
            v_stored(TILES)
            load_max((0, 0), 0)
            eng.dma_start(wo2[:, :, :], chunks(a["Wo2"])).then_inc(w_in["wo2"], 16)
            eng.dma_start(wff1[:, :, :], chunks(a["Wff1"])).then_inc(w_in["wff"], 16)
            eng.dma_start(wff2[:, :, :], chunks(a["Wff2"])).then_inc(w_in["wff"], 16)

            def self_group(g, loads):
                n = after(g)
                load_max(g, 1)
                if loads is not None:
                    load_max(n, 0)
                if loads:
                    eng.wait_ge(st_full, 64 * num(n))
                    two = (g[0] + 1, g[1])
                    load_group(two)
                    eng.wait_ge(pv_done, 16 * num(n))
                    load_v(two)

            with eng.Fori(0, LAST_PAIR) as gp:
                self_group((gp, 0), True)
                self_group((gp, 1), True)
            self_group((LAST_PAIR, 0), False)
            self_group((LAST_PAIR, 1), None)

            def load_q2(G):
                for h in range(2):
                    load_stack(q2_slot(G, h), q2_d[h, G // 2], slice(HG * (G % 2), HG * (G % 2) + HG), Q_PART, q2_in[G % 4])

            def load_max_2(G):
                eng.wait_ge(m_copied, 2 * GROUPS + G + 1)
                for i in range(PARTS):
                    eng.dma_start(stack[MROW + i:MROW + i + 1, Q2_SLOT[G % 4], :, :].rearrange("o h n -> o (h n)"),
                                  mT[32 * i:32 * i + 32, G % 2, :]).then_inc(m2_in[G % 4], 16)

            half = PROJ_2 + 2 * NC
            for u in range(PROJ_2, half):
                store_parts(u)
            parts_stored(eng, half)
            load_q2(0)
            load_q2(1)
            eng.wait_ge(st_full, 64 * GROUPS)
            load_q2(2)
            load_q2(3)
            load_max_2(0)
            for u in range(half, len(PROJ)):
                store_parts(u)
            load_max_2(1)
            parts_stored(eng, len(PROJ))
            for G in range(GROUPS):
                if G + 4 < GROUPS:
                    eng.wait_ge(st_full, 64 * GROUPS + UNITS * (G + 1))
                    load_q2(G + 4)
                if G + 2 < GROUPS:
                    load_max_2(G + 2)

            out_v = a["out"].rearrange("b (t p) d -> p (b t) d", p=P)
            for blk in range(BLOCKS):
                eng.wait_ge(l_out, TPB * (blk + 1))
                eng.dma_start(out_v[:, TPB * blk:TPB * blk + TPB, :], o1[:, blk % 2, :, :]).then_inc(y_out[blk % 2], 16)
            for s in range(2):
                eng.wait_ge(y_out[s], 16 * BLOCKS // 2)

        IDENTS_SET, V_PADS_SET, CONSTS = 4, 6, 15

        @block.gpsimd
        def _(eng):
            done = [0]

            def alone(ins):
                done[0] += 1
                ins.then_inc(pool_step, 1)
                eng.wait_ge(pool_step, done[0])

            for t in (ident, identb):
                alone(eng.memset(t[:, :], 0.0))
                alone(eng.affine_select(out=t[:, :], in_=t[:, :], compare_op=ALU.not_equal, fill=1.0, base=0,
                                        pattern=[[-1, P]], channel_multiplier=1))
            alone(eng.memset(vstage[:, :, :, :], 0.0))
            alone(eng.memset(vstage[:, :, :, DH:DH + 1], 1.0))
            alone(eng.memset(ones[:, :], 1.0))
            alone(eng.memset(mpart[:, :, :], 0.0))
            alone(eng.memset(stack[MROW:MROW + PARTS, 2:4, :, :], 1.0))
            alone(eng.memset(k2[:, :, :, :], 0.0))
            alone(eng.memset(k2[MROW:MROW + PARTS, :, :, 0:CTX], 1.0))
            alone(eng.memset(v2[:, :, :, :], 0.0))
            alone(eng.memset(v2[0:CTX, :, :, :].rearrange("p b g (h d) -> p (b g) h d", h=HG)[:, :, :, DH:DH + 1], 1.0))
            alone(eng.memset(vw[:, :, :], 0.0))
            alone(eng.memset(p1T[:, :, :], 0.0))
            assert done[0] == CONSTS
            eng.wait_ge(w_in["rows"], 16)
            for n, row in enumerate((ROW_BO1, ROW_BO2, ROW_BFF2)):
                for blk in range(BLOCKS):
                    eng.wait_ge(tok_ready, TPB * (BLOCKS * n + blk + 1))
                    xb = x[:, TPB * blk:TPB * blk + TPB, :]
                    eng.tensor_tensor(xb, xb, rows[:, row:row + 1, :].to_broadcast([P, TPB, D]), ALU.add).then_inc(bias_added, 1)
                if n == 0:
                    parts_stored(eng, PROJ_K2)
                    for b in range(B):
                        for o in range(NC):
                            for i, p, n in ((0, 0, 3), (3, 0, 2), (5, 0, 1)):
                                eng.dma_start(k2[DH * i:DH * (i + n), b, 8 * o:8 * o + 8, 0:CTX],
                                              k2_d[o, p:p + n, :, CTX * b:CTX * b + CTX].rearrange("i (r h) n -> (i r) h n", r=DH)
                                              ).then_inc(w_in["k2"], 16)

        @block.tensor
        def _(eng):
            def by_group(i, c):
                b, j = divmod(i, KC)
                start = 2 * TPB * P * (NC * b + c) + P * j
                return tok[:, :, :].rearrange("p t d -> p (t d)")[:, start:start + P]

            def turn(phase, blk):
                k = TURNS.index((phase, blk))
                b = blk // 2
                if phase == X3:
                    if blk >= 2:
                        eng.wait_ge(turn_done, 2 * k - 2)
                elif phase != LN1:
                    n = 0 if phase in (ATT1, LN2) else 1
                    eng.wait_ge(turn_done, 2 * k)
                    outs = TILES * n + KC * b + (0 if phase in (ATT1, ATT2) else KC)
                    if outs > 0:
                        eng.wait_ge(y_added, outs)
                    eng.wait_ge(rest_done, len(PROJ) if n else PROJ_2 + 2 * NC * b + (NC * (blk % 2) if phase == LN2 else 0))
                    if phase in (ATT1, ATT2):
                        eng.wait_ge(att_done, EARLY + 2 * GROUPS * n + 2 * GPB * (b + 1))
                elif k >= 2:
                    eng.wait_ge(turn_done, 2 * k - 2)
                for c in range(NC):
                    for t in range(TPB):
                        i = TPB * blk + t
                        if c == 0:
                            if phase in (LN1, LN2, LN3):
                                n = (LN1, LN2, LN3).index(phase)
                                eng.wait_ge(tok_ready, TILES * n + i + 1)
                            elif phase == X3:
                                eng.wait_ge(y_added, 2 * TILES + i + 1)
                        src = by_group(i, c) if phase in (ATT1, ATT2) else (x if phase == X3 else tok)[:, i, P * c:P * c + P]
                        mm_ = eng.transpose(ps[:, turn_bank(phase, blk, c), P * t:P * t + P], src, ident[:, :])
                    mm_.then_inc(turn_full, 1)

            def turned(phase, blk):
                eng.wait_ge(turn_done, 2 * TURNS.index((phase, blk)) + 2)

            def project(u):
                kind, o, blk = PROJ[u]
                w = {"q": wq1, "k": wkv1, "q2": wq2, "k2": wkv2}[kind]
                src = ctxT if kind == "k2" else xT
                n, c0 = width(u), BLK * blk
                if u >= 2:
                    eng.wait_ge(rest_done, u - 1)
                for c in range(NC):
                    mm_ = eng.matmul(ps[:, proj_bank(u), 0:n], w[:, c, P * o:P * o + P], src[:, c, c0:c0 + n],
                                     start=(c == 0), stop=(c == NC - 1))
                mm_.then_inc(pj_full, 1)

            def values(t):
                if t >= 2:
                    eng.wait_ge(v_done, t - 1)
                for c in range(NC):
                    mm_ = eng.matmul(ps[:, 6 + t % 2, 0:D], xT[:, c, P * t:P * t + P], wkv1[:, c, D:2 * D],
                                     start=(c == 0), stop=(c == NC - 1))
                mm_.then_inc(v_full, 1)

            def scores(g, j, first=False):
                G, slot = num(g), g[1]
                half, jj = divmod(j, 8)
                h, t0 = jj // 2, 2 * (jj % 2)
                if j == 0:
                    eng.wait_ge(k_in[slot], 16 * RUNS * (g[0] + 1))
                if j in (0, 8):
                    eng.wait_ge(q_in[half][slot], 16 * RUNS * (g[0] + 1))
                for i in range(2):
                    n = 32 * G + 2 * j + i
                    if not (first and n < 2):
                        eng.wait_ge(s_red, n - 1)
                    for kh in range(2):
                        mm_ = eng.matmul(ps[:, 2 * i + kh, :], qs[0:ROWS, slot, half, h, P * (t0 + i):P * (t0 + i) + P],
                                         stack[0:ROWS, 2 + slot, h, BLK * kh:BLK * kh + BLK], start=True, stop=True)
                        if kh == 1:
                            mm_.then_inc(s_full, 1)
                        yield

            eng.sem_inc(out_turned, EARLY)
            eng.wait_ge(pool_step, IDENTS_SET)
            turn(LN1, 0)
            eng.wait_ge(w_in["wqkv1"], 32)
            for blk in range(2):
                turned(LN1, blk)
                for i in range(TPB):
                    project(first_of(blk) + i)
                    values(TPB * blk + i)
                    if i == 1:
                        turn(LN1, blk + 1)
            turn(LN1, BLOCKS - 1)
            eng.wait_ge(w_in["ctx"], 16)
            eng.wait_ge(w_in["w2"], 32)
            for u in range(PROJ_B0, PROJ_K2):
                project(u)
            turned(LN1, BLOCKS - 1)
            first_scores = (part for j in range(16 - LEAD) for part in scores((0, 0), j, first=True))

            def tile_of_scores():
                for _ in range(2):
                    next(first_scores, None)

            for blk in range(2, BLOCKS):
                for i in range(TPB):
                    project(first_of(blk) + i)
                    if TPB * (blk - 2) + i >= FIRST_PAIR:
                        tile_of_scores()
                    values(TPB * blk + i)
                    if TPB * (blk - 2) + i >= FIRST_PAIR:
                        tile_of_scores()

            su = [0]

            def setup(m, n, terms):
                k = su[0]
                su[0] += 1
                if k >= 2:
                    eng.wait_ge(su_done, k - 1)
                else:
                    eng.wait_ge(v_done, TILES - 1 + k)
                if k == SETUP_1 + 1:
                    eng.wait_ge(m_copied, 1)
                for i, (lhs, rhs) in enumerate(terms):
                    mm_ = eng.matmul(ps[0:m, 6 + k % 2, 0:n], lhs, rhs, start=(i == 0), stop=(i == len(terms) - 1))
                mm_.then_inc(su_full, 1)
                tile_of_scores()

            eng.wait_ge(w_in["wl1"], 64)
            cut = [slice(CTX * b, CTX * b + CTX) for b in range(B)]
            for b in range(B):
                setup(CTX, D, [(ctxT[:, c, cut[b]], wkv2[:, c, D:2 * D]) for c in range(NC)])
            for w in (wkT, wvT):
                for o in range(NC):
                    setup(P, B * CTX, [(w[:, c, P * o:P * o + P], ctxT[:, c, :]) for c in range(NC)])
            eng.wait_ge(su_done, SETUP_1)
            eng.wait_ge(pool_step, CONSTS)
            eng.wait_ge(m_step, 4)
            eng.transpose(ps_b[0:96, 0:P], mpart[:, 0, :], identb[:, :]).then_inc(m_turned, 1)
            eng.wait_ge(c_bq, NC)
            for o in range(NC):
                setup(P, B * CTX, [(wql[:, c, P * o:P * o + P], kT[:, c, :]) for c in range(NC)])
            setup(P, B * CTX, [(bq_wide[:, c, :], kT[:, c, :]) for c in range(NC)])
            eng.wait_ge(w_in["rows"], 16)
            for b in range(B):
                setup(CTX, D, [(vT[:, c, cut[b]], wfcT[:, c, :]) for c in range(NC)]
                      + [(ones[0:1, 0:CTX], rows[0:1, ROW_BFC, :])])
            eng.wait_ge(su_done, SETUP_1 + SETUP_2)
            eng.wait_ge(rest_done, PROJ_2)

            def chain(n, b):
                att, ln, w = ((ATT1, LN2, wo1), (ATT2, LN3, wo2))[n]
                eng.wait_ge(w_in[("wo1", "wo2")[n]], 16)
                if (n, b) == (0, 0):
                    eng.wait_ge(s_red, 32 * GROUPS)
                for blk in (2 * b, 2 * b + 1):
                    turn(att, blk)
                    yield
                turned(att, 2 * b + 1)
                for i in range(KC):
                    k = TILES * n + KC * b + i
                    if i >= 2:
                        eng.wait_ge(y_added, k - 1)
                    t = i % TPB
                    for c in range(NC):
                        mm_ = eng.matmul(ps[:, out_bank(k), 0:D], attT[i // TPB][:, c, P * t:P * t + P], w[:, c, :],
                                         start=(c == 0), stop=(c == NC - 1))
                    mm_.then_inc(y_full, 1)
                    yield
                for blk in (2 * b, 2 * b + 1):
                    turn(ln, blk)
                    yield
                    if n == 0:
                        turned(ln, blk)
                        for o in range(NC):
                            project(PROJ_2 + NC * blk + o)
                            yield
                if n == 0:
                    yield

            def scores_t(g, k, h, first=False):
                G, slot = num(g), g[1]
                half, kc = divmod(k, KC)
                if kc == 0 and h == 0:
                    eng.wait_ge(m_in[half], 48 * (G + 1))
                if st_bank(g, k, 2) == ST:
                    if not (first and k == 0 and h < 2):
                        eng.wait_ge(exp_done, 64 * G + 4 * k + h - 1)
                elif k > LEAD:
                    eng.wait_ge(exp_done, 64 * G + 4 * k + h - 3)
                elif h < 2:
                    eng.wait_ge(exp_done, 64 * G + 4 * k + h - 1)
                else:
                    eng.wait_ge(s_red, 32 * GROUPS)
                eng.matmul(ps[:, st_bank(g, k, h), :], stack[0:KROWS, 2 + slot, h, P * kc:P * kc + P],
                           qs[0:KROWS, slot, half, h, :], start=True, stop=True).then_inc(st_full, 1)

            def weigh(g, k):
                G, slot = num(g), g[1]
                half, kc = divmod(k, KC)
                eng.wait_ge(exp_done, 64 * G + 4 * k + 4)
                if k == 0:
                    eng.wait_ge(v_in[slot], 16 * (g[0] + 1))
                if kc == 0 and not (isinstance(G, int) and G == 0 and half == 0):
                    eng.wait_ge(out_copied, 2 * G + half)
                for h in range(HG):
                    mm_ = eng.matmul(ps[32 * h:32 * h + 32, PV, :], v1[:, slot, kc, 32 * h:32 * h + 32],
                                     probs[:, k % 2, h, :], start=(kc == 0), stop=(kc == KC - 1))
                mm_.then_inc(pv_done, 1)

            def turn_out(e, half, m_before):
                eng.wait_ge(out_copied, e + 1)
                eng.wait_ge(m_copied, m_before)
                for t in range(TPB):
                    mm_ = eng.transpose(ps[:, MISC, P * t:P * t + P], outT[:, half, P * t:P * t + P], ident[:, :])
                mm_.then_inc(out_turned, 1)

            def turn_max(g, half):
                e = 2 * num(g) + half
                eng.wait_ge(m_step, 4 * e + 4)
                eng.wait_ge(att_done, EARLY + e - 1)
                eng.transpose(ps_b[0:96, 0:P], mpart[:, half, :], identb[:, :]).then_inc(m_turned, 1)

            def step(g, k, lead=True, first=False):
                G = num(g)
                lead_g, j = (g, k + 16 - LEAD) if k < LEAD else (after(g), k - LEAD)
                four = scores(lead_g, j) if lead or k < LEAD else iter(())
                for h, n in enumerate((1, 2, 1, 0)):
                    scores_t(g, k, h, first)
                    for _ in range(n):
                        next(four, None)
                if k > 0:
                    weigh(g, k - 1)
                elif not first:
                    weigh(before(g), 15)
                if k == 2 and not first:
                    turn_out(2 * G - 1, 1, 2 * G + 1)
                if k == 5:
                    turn_max(g, 1)
                if k == 10:
                    turn_out(2 * G, 0, 2 * G + 2)
                if k == 13 and lead:
                    turn_max(after(g), 0)

            def before(g):
                return (g[0], 0) if g[1] == 1 else (g[0] - 1, 1)

            def self_group(g, lead=True, chain=None):
                for k in range(LEAD, 16):
                    step(g, k, lead)
                    if not lead:
                        advance(chain, TAIL[k - LEAD])
                if lead:
                    for k in range(LEAD):
                        step(after(g), k)

            for _ in first_scores:
                pass
            for k in range(LEAD):
                step((0, 0), k, first=True)
            with eng.Fori(0, LAST_PAIR) as gp:
                self_group((gp, 0))
                self_group((gp, 1))
            self_group((LAST_PAIR, 0))
            self_group((LAST_PAIR, 1), lead=False, chain=chain(0, 0))
            weigh((LAST_PAIR, 1), 15)
            eng.wait_ge(att_done, EARLY + 2 * GROUPS - 1)
            turn_out(2 * GROUPS - 1, 1, 2 * GROUPS)

            def scores_2(G, t):
                b, slot = G // GPB, Q2_SLOT[G % 4]
                if t == 0:
                    eng.wait_ge(q2_in[G % 4], 2 * 16 * RUNS * (G // 4 + 1))
                n = KC * G + t
                if n >= 2:
                    eng.wait_ge(s2_red, n - 1)
                for h in range(HG):
                    mm_ = eng.matmul(ps[:, n % 2, CTX * h:CTX * h + CTX], qs[0:ROWS, slot, t // TPB, h, P * (t % TPB):P * (t % TPB) + P],
                                     k2[0:ROWS, b, HG * (G % GPB) + h, 0:CTX], start=True, stop=True)
                mm_.then_inc(s2_full, 1)

            def scores_t2(G, n):
                b, (half, h) = G // GPB, divmod(n, HG)
                if n == 0:
                    eng.wait_ge(m2_in[G % 4], 48 * (G // 4 + 1))
                eng.wait_ge(exp_done, 64 * GROUPS + UNITS * G + n - 1)
                eng.matmul(ps[0:CTXP, ST + h % 2, :], k2[0:KROWS, b, HG * (G % GPB) + h, :],
                           qs[0:KROWS, Q2_SLOT[G % 4], half, h, :], start=True, stop=True).then_inc(st_full, 1)

            def weigh_2(G, half):
                b = G // GPB
                eng.wait_ge(exp_done, 64 * GROUPS + UNITS * G + 4 * half + 4)
                eng.wait_ge(out_copied, 2 * GROUPS + 2 * G + half)
                for h in range(HG):
                    mm_ = eng.matmul(ps[32 * h:32 * h + 32, PV, :], v2[0:CTXP, b, G % GPB, 32 * h:32 * h + 32],
                                     probs[0:CTXP, half, h, :], start=True, stop=True)
                mm_.then_inc(pv_done, 1)

            def turn_out_2(G, half):
                e = 2 * GROUPS + 2 * G + half
                eng.wait_ge(out_copied, e + 1)
                if half == 0:
                    eng.wait_ge(att_done, EARLY + e)
                    eng.wait_ge(m_copied, 2 * GROUPS + min(G + 2, GROUPS))
                else:
                    eng.wait_ge(att_done, EARLY + e)
                    eng.wait_ge(m_copied, 2 * GROUPS + min(G + 3, GROUPS))
                for t in range(TPB):
                    mm_ = eng.transpose(ps[:, MISC, P * t:P * t + P], outT[:, half, P * t:P * t + P], ident[:, :])
                mm_.then_inc(out_turned, 1)

            def turn_max_2(G):
                eng.wait_ge(m_step, 8 * GROUPS + 4 * G + 4)
                eng.wait_ge(att_done, EARLY + 2 * GROUPS + max(2 * G - 3, 0))
                eng.transpose(ps_b[0:96, 0:P], mpart[:, G % 2, :], identb[:, :]).then_inc(m_turned, 1)

            def cross_unit(G, n):
                if G < GROUPS:
                    scores_t2(G, n)
                if G + 2 < GROUPS:
                    scores_2(G + 2, n)
                if n == 1 and G >= 1:
                    weigh_2(G - 1, 1)
                if n == 2 and G + 1 < GROUPS:
                    turn_max_2(G + 1)
                if n == 4 and G >= 1:
                    turn_out_2(G - 1, 1)
                if n == 5 and G < GROUPS:
                    weigh_2(G, 0)
                if n == 7 and G < GROUPS:
                    turn_out_2(G, 0)

            after_self = chain(0, 1)
            advance(after_self, AHEAD)
            eng.wait_ge(w_in["k2"], 16 * RUNS * B * NC)
            eng.wait_ge(exp_done, 64 * GROUPS)
            for n, count in enumerate(FIRST_S2):
                G, t = divmod(n, KC)
                scores_2(G, t)
                if (G, t) == (1, 3):
                    turn_max_2(0)
                advance(after_self, count)
            after_cross = chain(1, 0)
            for G in range(GROUPS):
                for n in range(UNITS):
                    cross_unit(G, n)
                    advance(after_self if G == 0 else after_cross, pieces(G, n))
            for n in range(5):
                cross_unit(GROUPS, n)

            def widen(n):
                blk, f = divmod(n, FC)
                if n >= 2:
                    eng.wait_ge(hid_done, n - 1)
                for i in (1, 0):
                    for c in range(NC):
                        col = FC * i + f
                        mm_ = eng.matmul(ps[:, ff_bank(n, i), :], wff1[:, c, P * col:P * col + P],
                                         xT[:, c, BLK * blk:BLK * blk + BLK], start=(c == 0), stop=(c == NC - 1))
                    mm_.then_inc(ff_gate if i else ff_full, 1)

            def narrow(blk):
                eng.wait_ge(hid_done, FC * (blk + 1))
                for t in range(TPB):
                    n = 2 * TILES + TPB * blk + t
                    eng.wait_ge(y_added, n - 1)
                    for f in range(FC):
                        mm_ = eng.matmul(ps[:, out_bank(n), 0:D], hidT[:, blk % 2, f, P * t:P * t + P], wff2[:, f, :],
                                         start=(f == 0), stop=(f == FC - 1))
                    mm_.then_inc(y_full, 1)

            turned(LN3, 1)
            eng.wait_ge(w_in["wff"], 32)
            eng.wait_ge(exp_done, 72 * GROUPS)
            eng.wait_ge(s2_red, KC * GROUPS)
            eng.wait_ge(m_copied, 3 * GROUPS)
            after_cross = chain(1, 1)
            for f in range(FC):
                widen(f)
                advance(after_cross, FF_PIECES[f])
            eng.wait_ge(att_done, EARLY + 4 * GROUPS)
            for blk in range(BLOCKS):
                if blk + 1 < BLOCKS:
                    turned(LN3, blk + 1)
                    for f in range(FC):
                        widen(FC * (blk + 1) + f)
                narrow(blk)

            def l1_scores(blk):
                turned(X3, blk)
                if blk >= 2:
                    eng.wait_ge(l_added, blk - 1)
                b = blk // 2
                for t in range(TPB):
                    for c in range(NC):
                        i = TPB * blk + t
                        mm_ = eng.matmul(ps[:, 4 + blk % 2, CTX * t:CTX * t + CTX], xT[:, c, P * i:P * i + P],
                                         g1[:, c, CTX * b:CTX * b + CTX], start=(c == 0), stop=(c == NC - 1))
                mm_.then_inc(l_full, 1)

            def l1_turn(blk):
                eng.wait_ge(l_exp, TPB * (blk + 1))
                if blk >= 1:
                    eng.wait_ge(l_pT, blk)
                for t in range(TPB):
                    mm_ = eng.transpose(ps[0:CTX, blk % 2, P * t:P * t + P], p1[:, blk % 2, t, :], ident[:, :])
                mm_.then_inc(l_turned, 1)

            def l1_weigh(blk):
                eng.wait_ge(l_pT, blk + 1)
                for t in range(TPB):
                    n = TPB * blk + t
                    if n >= 2:
                        eng.wait_ge(l_y, n - 1)
                    mm_ = eng.matmul(ps[:, 6 + n % 2, 0:D], p1T[0:CTXP, blk % 2, P * t:P * t + P],
                                     vw[0:CTXP, blk // 2, :], start=True, stop=True)
                    mm_.then_inc(l_pv, 1)

            eng.wait_ge(hid_done, FC * BLOCKS)
            for blk in range(BLOCKS):
                turn(X3, blk)
            eng.wait_ge(y_added, 3 * TILES)
            for blk in range(BLOCKS):
                l1_scores(blk)
                if blk == 0:
                    turned(X3, BLOCKS - 1)
                if blk >= 1:
                    l1_turn(blk - 1)
                    l1_weigh(blk - 1)
            l1_turn(BLOCKS - 1)
            l1_weigh(BLOCKS - 1)

        @block.scalar
        def _(eng):
            def turn_copy(phase, blk):
                for c in range(NC):
                    eng.wait_ge(turn_full, 2 * TURNS.index((phase, blk)) + c + 1)
                    src = ps[:, turn_bank(phase, blk, c), :]
                    if phase in (ATT1, ATT2):
                        eng.activation(attT[blk % 2][:, c, :], src, ACT.Copy).then_inc(turn_done, 1)
                    elif phase == X3:
                        eng.activation(xT[:, c, BLK * blk:BLK * blk + BLK], src, ACT.Copy).then_inc(turn_done, 1)
                    else:
                        i = COL_LN + 4 * (LN1, LN2, LN3).index(phase)
                        eng.activation(xT[:, c, BLK * blk:BLK * blk + BLK], src, ACT.Identity,
                                       scale=cols[:, i + c:i + c + 1], bias=cols[:, i + 2 + c:i + 3 + c]).then_inc(turn_done, 1)

            def high(u):
                n, slot = width(u), u % RING
                eng.wait_ge(pj_full, u + 1)
                if u >= RING:
                    eng.wait_ge(part_out[slot], 16 * (u // RING))
                eng.activation(part(u)[:, 0, :], ps[:, proj_bank(u), 0:n], ACT.Copy).then_inc(hi_done, 1)

            def middle(u):
                eng.wait_ge(rest_done, u + 1)
                eng.activation(part(u)[:, 1, :], rest[:, u % 2, 0:width(u)], ACT.Copy).then_inc(mid_done, 1)

            def values(t):
                eng.wait_ge(v_full, t + 1)
                if t >= 4 and t % 2 == 0:
                    eng.wait_ge(v_out[t // 2 % 2], 16 * (t // 4))
                eng.activation(vstage[:, t % 4, :, 0:DH], ps[:, 6 + t % 2, 0:D].rearrange("p (h d) -> p h d", h=H),
                               ACT.Copy).then_inc(v_done, 1)

            eng.wait_ge(w_in["cols"], 16)
            turn_copy(LN1, 0)
            eng.wait_ge(pool_step, V_PADS_SET)
            for blk in range(BLOCKS):
                if blk == 2:
                    turn_copy(LN1, BLOCKS - 1)
                    for u in range(PROJ_B0, PROJ_K2):
                        high(u)
                    for u in range(PROJ_B0, PROJ_K2):
                        middle(u)
                for i in range(TPB):
                    u = first_of(blk) + i
                    high(u)
                    if blk < 2 and i > 0:
                        middle(u - 1)
                    values(TPB * blk + i)
                    if blk >= 2:
                        middle(u)
                    if blk < 2 and i == 1:
                        turn_copy(LN1, blk + 1)
                if blk < 2:
                    middle(first_of(blk) + TPB - 1)

            def max_copy(e, half):
                eng.wait_ge(m_turned, e + 1)
                eng.activation(mT[0:96, half, :], ps_b[0:96, 0:P], ACT.Copy).then_inc(m_copied, 1)

            su = [0]

            def setup_done(dst, m, n, bias=None, view=lambda v: v):
                k = su[0]
                su[0] += 1
                eng.wait_ge(su_full, k + 1)
                src = view(ps[0:m, 6 + k % 2, 0:n])
                if bias is None:
                    eng.activation(dst, src, ACT.Copy).then_inc(su_done, 1)
                else:
                    eng.activation(dst, src, ACT.Identity, bias=bias).then_inc(su_done, 1)

            eng.wait_ge(pool_step, CONSTS)
            for b in range(B):
                setup_done(v2[0:CTX, b, :, :].rearrange("p g (h d) -> p (g h) d", h=HG)[:, :, 0:DH], CTX, D,
                           view=lambda v: v.rearrange("p (h d) -> p h d", h=H))
            for dst, c0 in ((kT, COL_BK), (vT, COL_BV)):
                for o in range(NC):
                    setup_done(dst[:, o, :], P, B * CTX, bias=cols[:, c0 + o:c0 + o + 1])
            max_copy(0, 0)
            for o in range(NC):
                setup_done(g1[:, o, :], P, B * CTX)
            setup_done(cb[:, 0, :], P, B * CTX)
            for b in range(B):
                setup_done(vw[0:CTX, b, :], CTX, D)

            def chain(n, b):
                att, ln = ((ATT1, LN2), (ATT2, LN3))[n]
                for blk in (2 * b, 2 * b + 1):
                    turn_copy(att, blk)
                    yield
                for _ in range(KC):
                    yield
                u = PROJ_2 + 2 * NC * b
                first = u
                for blk in (2 * b, 2 * b + 1):
                    turn_copy(ln, blk)
                    if u > first and n == 0:
                        middle(u - 1)
                    yield
                    if n == 0:
                        for o in range(NC):
                            high(u)
                            if o > 0:
                                middle(u - 1)
                            u += 1
                            yield
                if n == 0:
                    middle(u - 1)
                    yield

            def exps(g, k, pr, first=False):
                G = num(g)
                for h in (2 * pr, 2 * pr + 1):
                    eng.wait_ge(st_full, 64 * G + 4 * k + h + 1)
                    if h == 0 and not (first and k < 2):
                        eng.wait_ge(pv_done, 16 * G + k - 1)
                    eng.activation(probs[:, k % 2, h, :], ps[:, st_bank(g, k, h), :], ACT.Exp, scale=SCALE).then_inc(exp_done, 1)

            def out_copy(e, half):
                eng.wait_ge(pv_done, 8 * e + 8)
                eng.wait_ge(out_turned, EARLY + e - 1)
                eng.activation(outT[:, half, :], ps[:, PV, :], ACT.Copy).then_inc(out_copied, 1)

            def step(g, k, lead=True, first=False):
                G = num(g)
                exps(g, k, 0, first)
                if k == 6:
                    max_copy(2 * G + 1, 1)
                if k == 14 and lead:
                    max_copy(2 * G + 2, 0)
                exps(g, k, 1, first)
                if k == 1 and not first:
                    out_copy(2 * G - 1, 1)
                if k == 9:
                    out_copy(2 * G, 0)

            def self_group(g, lead=True, chain=None):
                for k in range(LEAD, 16):
                    step(g, k, lead)
                    if not lead:
                        advance(chain, TAIL[k - LEAD])
                if lead:
                    for k in range(LEAD):
                        step(after(g), k)

            parts_stored(eng, PROJ_2)
            for s in range(2):
                eng.wait_ge(v_out[s], 16 * TILES // 4)
            for k in range(LEAD):
                step((0, 0), k, first=True)
            with eng.Fori(0, LAST_PAIR) as gp:
                self_group((gp, 0))
                self_group((gp, 1))
            self_group((LAST_PAIR, 0))
            self_group((LAST_PAIR, 1), lead=False, chain=chain(0, 0))
            out_copy(2 * GROUPS - 1, 1)

            def max_copy_2(G):
                eng.wait_ge(m_turned, 2 * GROUPS + G + 1)
                if G >= 2:
                    eng.wait_ge(m2_in[(G - 2) % 4], 48 * ((G - 2) // 4 + 1))
                eng.activation(mT[0:96, G % 2, :], ps_b[0:96, 0:P], ACT.Copy).then_inc(m_copied, 1)

            def exp_2(G, n):
                half, h = divmod(n, HG)
                eng.wait_ge(st_full, 64 * GROUPS + UNITS * G + n + 1)
                if h == 0:
                    eng.wait_ge(pv_done, 16 * GROUPS + max(2 * G + half - 1, 0))
                eng.activation(probs[0:CTXP, half, h, :], ps[0:CTXP, ST + h % 2, :], ACT.Exp, scale=SCALE).then_inc(exp_done, 1)

            def out_copy_2(G, half):
                e = 2 * GROUPS + 2 * G + half
                eng.wait_ge(pv_done, 16 * GROUPS + 2 * G + half + 1)
                eng.wait_ge(out_turned, EARLY + e - 1)
                eng.activation(outT[:, half, :], ps[:, PV, :], ACT.Copy).then_inc(out_copied, 1)

            def cross_unit(G, n):
                if G < GROUPS:
                    exp_2(G, n)
                if n == 2 and G >= 1:
                    out_copy_2(G - 1, 1)
                if n == 3 and G + 1 < GROUPS:
                    max_copy_2(G + 1)
                if n == 6 and G < GROUPS:
                    out_copy_2(G, 0)

            after_self = chain(0, 1)
            advance(after_self, AHEAD)
            for n, count in enumerate(FIRST_S2):
                if divmod(n, KC) == (1, 3):
                    max_copy_2(0)
                advance(after_self, count)
            after_cross = chain(1, 0)
            for G in range(GROUPS):
                for n in range(UNITS):
                    cross_unit(G, n)
                    advance(after_self if G == 0 else after_cross, pieces(G, n))
            for n in range(5):
                cross_unit(GROUPS, n)

            parts_stored(eng, len(PROJ))
            after_cross = chain(1, 1)
            for n in range(FC * BLOCKS):
                f = n % FC
                eng.wait_ge(ff_gate, n + 1)
                if n >= 2:
                    eng.wait_ge(hid_done, n - 1)
                i = COL_FF + FC + f
                eng.activation(gate[:, n % 2, :], ps[:, ff_bank(n, 1), :], ACT.Gelu_apprx_sigmoid,
                               bias=cols[:, i:i + 1]).then_inc(gate_done, 1)
                if n < FC:
                    advance(after_cross, FF_PIECES[n])

            def l1_exps(blk):
                eng.wait_ge(l_max, 2 * (blk + 1))
                s = blk % 2
                if blk >= 2:
                    eng.wait_ge(l_turned, blk - 1)
                for t in range(TPB):
                    eng.activation(p1[:, s, t, :], s1[:, s, t, :], ACT.Exp, scale=L1_SCALE, bias=nm1[:, s, t:t + 1],
                                   accum_out=sum1[:, s, t:t + 1]).then_inc(l_exp, 1)

            def l1_squares(blk):
                s = blk % 2
                for t in range(TPB):
                    n = TPB * blk + t
                    eng.wait_ge(l_y, n + 1)
                    if n >= 1:
                        eng.wait_ge(l_sq, n)
                    eng.activation(sq[:, :], y1[:, t, :], ACT.Square, accum_out=ss1[:, s, t:t + 1]).then_inc(l_sq, 1)

            for blk in range(BLOCKS):
                turn_copy(X3, blk)
            for blk in range(BLOCKS):
                l1_exps(blk)
                if blk >= 1:
                    l1_squares(blk - 1)
            l1_squares(BLOCKS - 1)

        @block.vector
        def _(eng):
            steps = [0]

            def link(ins):
                steps[0] += 1
                ins.then_inc(dve_step, 1)
                eng.wait_ge(dve_step, steps[0])

            def inverse_root(s, v, scale, e):
                y, w, h = rstd[:, s, :], var[:, s, :], half_var[:, s, :]
                link(eng.tensor_scalar(w, v, scale, e, ALU.mult, ALU.add))
                link(eng.tensor_scalar(y.bitcast(I32), w.bitcast(I32), -0.5, float(0x5F3759DF), ALU.mult, ALU.add))
                link(eng.tensor_scalar(h, w, -0.5, None, ALU.mult))
                for _ in range(3):
                    link(eng.tensor_tensor(w, y, y, ALU.mult))
                    link(eng.tensor_tensor(w, w, h, ALU.mult))
                    link(eng.scalar_tensor_tensor(out=y, in0=w, scalar=1.5, in1=y, op0=ALU.add, op1=ALU.mult))

            def stats(n, blk, t):
                k = BLOCKS * n + blk
                if k >= 1:
                    eng.wait_ge(var_ready, TPB * (k - 1) + t + 1)
                if k >= 2:
                    eng.wait_ge(tok_ready, TPB * (k - 1))
                link(eng.bn_stats(st[:, t, :], x[:, TPB * blk + t, :]))
                eng.bn_aggr(mv[:, blk % 2, t, :], st[:, t, :]).then_inc(var_ready, 1)

            def norm(n, blk):
                s = blk % 2
                eng.wait_ge(var_ready, TPB * (BLOCKS * n + blk + 1))
                inverse_root(s, mv[:, s, :, 1], 1.0, LN_EPS)
                for t in range(TPB):
                    i = TPB * blk + t
                    eng.tensor_scalar(tok[:, i, :], x[:, i, :], mv[:, s, t, 0:1], rstd[:, s, t:t + 1],
                                      ALU.subtract, ALU.mult).then_inc(tok_ready, 1)

            def remainder(u):
                n = width(u)
                eng.wait_ge(hi_done, u + 1)
                if u >= 2:
                    eng.wait_ge(mid_done, u - 1)
                    eng.wait_ge(lo_done, u - 1)
                eng.tensor_tensor(rest[:, u % 2, 0:n], ps[:, proj_bank(u), 0:n], part(u)[:, 0, :],
                                  ALU.subtract).then_inc(rest_done, 1)

            def low(u):
                n = width(u)
                eng.wait_ge(mid_done, u + 1)
                eng.wait_ge(rest_done, u + 1)
                eng.tensor_tensor(part(u)[:, 2, :], rest[:, u % 2, 0:n], part(u)[:, 1, :],
                                  ALU.subtract).then_inc(lo_done, 1)

            def reduce_tile(g, j, i):
                G = num(g)
                half, jj = divmod(j, 8)
                h, t0 = jj // 2, 2 * (jj % 2)
                eng.wait_ge(s_full, 32 * G + 2 * j + i + 1)
                k = 4 * h + t0 + i
                eng.tensor_reduce(mm[:, half, k:k + 1], ps[:, 2 * i:2 * i + 2, :], AX.XY, ALU.max).then_inc(s_red, 1)

            def reduce_(g, j):
                for i in range(2):
                    reduce_tile(g, j, i)

            def split_max(e, s, n):
                p = mpart[:, s, :].rearrange("p (i n) -> p i n", i=PARTS)[:, :, 0:n]
                eng.tensor_scalar(p[:, 0, :], mm[:, s, 0:n], -1.0, None, ALU.mult).then_inc(m_step, 1)
                eng.wait_ge(m_step, 4 * e + 1)
                eng.scalar_tensor_tensor(out=mrest[:, s, 0:n], in0=mm[:, s, 0:n], scalar=-1.0, in1=p[:, 0, :],
                                         op0=ALU.mult, op1=ALU.subtract).then_inc(m_step, 1)
                eng.wait_ge(m_step, 4 * e + 2)
                eng.tensor_copy(p[:, 1, :], mrest[:, s, 0:n]).then_inc(m_step, 1)
                eng.wait_ge(m_step, 4 * e + 3)
                eng.tensor_tensor(p[:, 2, :], mrest[:, s, 0:n], p[:, 1, :], ALU.subtract).then_inc(m_step, 1)

            def maxima(g, half):
                G = num(g)
                e = 2 * G + half
                eng.wait_ge(s_red, 32 * G + 16 * half + 16)
                split_max(e, half, 16)

            eng.sem_inc(att_done, EARLY)
            for blk in range(2):
                eng.wait_ge(x_in[blk], 16)
                for t in range(TPB):
                    stats(0, blk, t)
                norm(0, blk)
            for blk in range(2):
                eng.wait_ge(x_in[blk + 2], 16)
                for i in range(TPB):
                    u = first_of(blk) + i
                    remainder(u)
                    if i > 0:
                        low(u - 1)
                    if i < 2:
                        stats(0, blk + 2, 2 * i)
                        stats(0, blk + 2, 2 * i + 1)
                    if i == 2:
                        norm(0, blk + 2)
                low(u)
            for u in range(PROJ_B0, PROJ_K2):
                remainder(u)
                low(u)
            eng.wait_ge(pool_step, CONSTS)
            eng.wait_ge(w_in["cols"], 16)
            for c in range(NC):
                eng.tensor_scalar(bq_wide[:, c, :], ones[:, :], cols[:, COL_BQ + c:COL_BQ + c + 1], None,
                                  ALU.mult).then_inc(c_bq, 1)

            def first_reduces():
                for j in range(16 - LEAD):
                    for i in range(2):
                        reduce_tile((0, 0), j, i)
                        if (j, i) == (7, 1):
                            maxima((0, 0), 0)
                        yield

            first_tiles = first_reduces()
            for blk in range(2, BLOCKS):
                for i in range(TPB):
                    u = first_of(blk) + i
                    remainder(u)
                    if TPB * (blk - 2) + i >= FIRST_PAIR:
                        next(first_tiles)
                    low(u)
                    if TPB * (blk - 2) + i >= FIRST_PAIR:
                        next(first_tiles)

            def add(n, i):
                k = TILES * n + i
                eng.wait_ge(y_full, k + 1)
                eng.wait_ge(bias_added, BLOCKS * n + i // TPB + 1)
                eng.tensor_tensor(x[:, i, :], ps[:, out_bank(k), 0:D], x[:, i, :], ALU.add).then_inc(y_added, 1)

            def chain(n, b):
                for _ in range(2):
                    yield
                for i in range(KC):
                    blk, t = divmod(KC * b + i, TPB)
                    add(n, KC * b + i)
                    if t > 0:
                        eng.wait_ge(y_added, TILES * n + KC * b + i)
                        stats(n + 1, blk, t - 1)
                    if t == TPB - 1:
                        eng.wait_ge(y_added, TILES * n + KC * b + i + 1)
                        stats(n + 1, blk, t)
                        norm(n + 1, blk)
                    yield
                u = PROJ_2 + 2 * NC * b
                for i in range(2):
                    if i > 0 and n == 0:
                        low(u - 1)
                    yield
                    if n == 0:
                        for o in range(NC):
                            remainder(u)
                            if o > 0:
                                low(u - 1)
                            u += 1
                            yield
                if n == 0:
                    low(u - 1)
                    yield

            def step(g, k, lead=True, first=False):
                if k < LEAD:
                    reduce_(g, k + 16 - LEAD)
                elif lead:
                    reduce_(after(g), k - LEAD)
                if k == 3:
                    maxima(g, 1)
                    if not first:
                        attended(before(g), 1)
                if k == 11:
                    if lead:
                        maxima(after(g), 0)
                    attended(g, 0)

            def before(g):
                return (g[0], 0) if g[1] == 1 else (g[0] - 1, 1)

            def attended(g, half):
                e = 2 * num(g) + half
                eng.wait_ge(out_turned, EARLY + e + 1)
                v = ps[:, MISC, :].rearrange("p (t h d) -> p t h d", t=TPB, h=HG)
                r = rec[:, half, :].rearrange("p (t h) -> p t h", t=TPB)
                eng.reciprocal(r, v[:, :, :, DH]).then_inc(rec_done, 1)
                eng.wait_ge(rec_done, e + 1)
                pair = g[0] % (GROUPS // 2) if isinstance(g[0], int) else g[0]
                n = TPB * P
                start = 2 * n * pair + n * half
                dst = by_group[:, start:start + n] if isinstance(start, int) else by_group[:, bass.ds(start, n)]
                dst = dst.rearrange("p (t x) -> p t x", t=TPB)[:, :, 64 * g[1]:64 * g[1] + 64].rearrange("p t (h d) -> p t h d", h=HG)
                eng.tensor_tensor(dst, v[:, :, :, 0:DH], r.unsqueeze(3).to_broadcast([P, TPB, HG, DH]), ALU.mult).then_inc(att_done, 1)

            by_group = tok[:, :, :].rearrange("p t d -> p (t d)")

            def self_group(g, lead=True, chain=None):
                for k in range(LEAD, 16):
                    step(g, k, lead)
                    if not lead:
                        advance(chain, TAIL[k - LEAD])
                if lead:
                    for k in range(LEAD):
                        step(after(g), k)

            for _ in first_tiles:
                pass
            for k in range(LEAD):
                step((0, 0), k, first=True)
            with eng.Fori(0, LAST_PAIR) as gp:
                self_group((gp, 0))
                self_group((gp, 1))
            self_group((LAST_PAIR, 0))
            self_group((LAST_PAIR, 1), lead=False, chain=chain(0, 0))
            attended((LAST_PAIR, 1), 1)

            def reduce_2(G, t):
                n = KC * G + t
                eng.wait_ge(s2_full, n + 1)
                dst = mm[:, G % 2, :].rearrange("p (f h t) -> p f h t", f=2, h=HG)[:, t // TPB, :, t % TPB]
                eng.tensor_reduce(dst, ps[:, n % 2, 0:HG * CTX].rearrange("p (h n) -> p h n", h=HG),
                                  AX.X, ALU.max).then_inc(s2_red, 1)
                if t == KC - 1:
                    eng.wait_ge(s2_red, KC * (G + 1))
                    split_max(2 * GROUPS + G, G % 2, 32)

            def attended_2(G, half):
                attended((GROUPS // 2 + G // 2, G % 2), half)

            def cross_unit(G, n):
                if G + 2 < GROUPS:
                    reduce_2(G + 2, n)
                if n == 0 and G >= 1:
                    attended_2(G - 1, 0)
                if n == 4 and G >= 1:
                    attended_2(G - 1, 1)

            after_self = chain(0, 1)
            advance(after_self, AHEAD)
            for n, count in enumerate(FIRST_S2):
                reduce_2(*divmod(n, KC))
                advance(after_self, count)
            after_cross = chain(1, 0)
            for G in range(GROUPS):
                for n in range(UNITS):
                    cross_unit(G, n)
                    advance(after_self if G == 0 else after_cross, pieces(G, n))
            for n in range(5):
                cross_unit(GROUPS, n)

            def hidden(n):
                blk, f = divmod(n, FC)
                eng.wait_ge(ff_full, n + 1)
                eng.wait_ge(gate_done, n + 1)
                eng.scalar_tensor_tensor(out=hidT[:, blk % 2, f, :], in0=ps[:, ff_bank(n, 0), :],
                                         scalar=cols[:, COL_FF + f:COL_FF + f + 1], in1=gate[:, n % 2, :],
                                         op0=ALU.add, op1=ALU.mult).then_inc(hid_done, 1)

            after_cross = chain(1, 1)
            for n in range(FC):
                hidden(n)
                advance(after_cross, FF_PIECES[n])
            for blk in range(BLOCKS):
                if blk + 1 < BLOCKS:
                    for n in range(FC * (blk + 1), FC * (blk + 2)):
                        hidden(n)
                for t in range(TPB):
                    add(2, TPB * blk + t)

            def l1_max(blk):
                s, b = blk % 2, blk // 2
                eng.wait_ge(l_full, blk + 1)
                if blk >= 2:
                    eng.wait_ge(l_exp, TPB * (blk - 1))
                eng.tensor_tensor(s1[:, s, :, :], ps[:, 4 + s, 0:TPB * CTX].rearrange("p (t n) -> p t n", t=TPB),
                                  cb[:, 0:1, CTX * b:CTX * b + CTX].to_broadcast([P, TPB, CTX]), ALU.add).then_inc(l_added, 1)
                eng.wait_ge(l_added, blk + 1)
                eng.tensor_reduce(m1[:, s, :], s1[:, s, :, :], AX.X, ALU.max).then_inc(l_max, 1)
                eng.wait_ge(l_max, 2 * blk + 1)
                eng.tensor_scalar(nm1[:, s, :], m1[:, s, :], -L1_SCALE, None, ALU.mult).then_inc(l_max, 1)

            def l1_probs(blk):
                s = blk % 2
                eng.wait_ge(l_turned, blk + 1)
                eng.tensor_copy(p1T[0:CTX, s, :], ps[0:CTX, s, :]).then_inc(l_pT, 1)
                link(eng.reciprocal(r1[:, s, :], sum1[:, s, :]))

            def l1_residual(blk):
                s = blk % 2
                for t in range(TPB):
                    n = TPB * blk + t
                    eng.wait_ge(l_pv, n + 1)
                    if blk >= 1:
                        eng.wait_ge(l_out, n - TPB + 1)
                    eng.scalar_tensor_tensor(out=y1[:, t, :], in0=ps[:, 6 + n % 2, 0:D], scalar=r1[:, s, t:t + 1],
                                             in1=x[:, n, :], op0=ALU.mult, op1=ALU.add).then_inc(l_y, 1)

            def l1_finish(blk):
                s = blk % 2
                eng.wait_ge(l_sq, TPB * (blk + 1))
                inverse_root(s, ss1[:, s, :], 1.0 / D, RMS_EPS)
                if blk >= 2:
                    eng.wait_ge(y_out[s], 16 * (blk // 2))
                for t in range(TPB):
                    eng.scalar_tensor_tensor(out=o1[:, s, t, :], in0=y1[:, t, :], scalar=rstd[:, s, t:t + 1],
                                             in1=rows[:, ROW_W, :], op0=ALU.mult, op1=ALU.mult).then_inc(l_out, 1)

            for blk in range(BLOCKS):
                l1_max(blk)
                if blk >= 1:
                    l1_probs(blk - 1)
                    l1_residual(blk - 1)
                    l1_finish(blk - 1)
            l1_probs(BLOCKS - 1)
            l1_residual(BLOCKS - 1)
            l1_finish(BLOCKS - 1)


def kernel(**inputs):
    import numpy as np
    import concourse.bacc as bacc
    from concourse.bass_utils import run_bass_kernel_spmd

    v = {k: np.asarray(t) for k, t in inputs.items()}
    l0 = {k[len("L0_xattn_"):]: t for k, t in v.items() if k.startswith("L0_xattn_")}
    l1 = {k[len("L1_xattn_"):]: t for k, t in v.items() if k.startswith("L1_xattn_")}

    def by_feature(w):
        return w.reshape(D, NC, P // DH, DH).transpose(0, 1, 3, 2).reshape(D, D)

    def columns(t):
        return t.reshape(-1, P).T

    arrays = {
        "x": v["x"],
        "ctxT": v["ctx_1024"].transpose(2, 0, 1).reshape(D, B * CTX),
        "cols": np.concatenate(
            [columns(l0[n]) for n in ("ln1_s", "ln1_b", "ln2_s", "ln2_b", "ln3_s", "ln3_b", "bff1")]
            + [columns(l1[n]) for n in ("bq", "bk", "bv")], axis=1),
        "rows": np.stack([l0["bo1"], l0["bo2"], l0["bff2"], l1["norm_w"], l1["bfc"]]),
        "Wq": l1["Wq"], "WkT": l1["Wk"].T, "WvT": l1["Wv"].T, "WfcT": l1["Wfc"].T,
    }
    arrays.update({n: l0[n] for n in ("Wo1", "Wo2", "Wff1", "Wff2")})
    for n in ("Wq1", "Wq2"):
        arrays[n] = by_feature(l0[n])
    for n in ("Wkv1", "Wkv2"):
        arrays[n] = np.concatenate([by_feature(l0[n][:, :D]), l0[n][:, D:]], axis=1)
    arrays = {f"in_{n}": np.ascontiguousarray(t) for n, t in arrays.items()}

    nc = bacc.Bacc("TRN2", target_bir_lowering=False, num_devices=1)
    aps = {n[3:]: nc.dram_tensor(n, t.shape, mybir.dt.from_np(t.dtype), kind="ExternalInput").ap()
           for n, t in arrays.items()}
    aps["out"] = nc.dram_tensor("out", (B, S, D), F32, kind="ExternalOutput").ap()
    build(nc, aps)
    result = run_bass_kernel_spmd(nc, [arrays], core_ids=[0])
    return result.results[0]["out"]
```

```python
from contextlib import ExitStack

import numpy as np

import concourse.bass as bass
from concourse import mybir

F32 = mybir.dt.float32
F32R = mybir.dt.float32r
BF16 = mybir.dt.bfloat16
I32 = mybir.dt.int32
ACT = mybir.ActivationFunctionType
ALU = mybir.AluOpType
AX = mybir.AxisListType

P = 128
B, S, D = 2, 1024, 256
T = B * S
NC = D // P
TILES = T // P
BLK = 512
BLOCKS = T // BLK
TPB = BLK // P
H, DH = 16, 16
HG = 4
GROUPS = B * H // HG
GPB = GROUPS // B
KC = S // P
CTX = 77
CTXP = 96
F = 4 * D
FC = F // P
PARTS = 3
RING = 5
HID_RING = 4
FF_LAG = 3
ROWS = 6 * DH
MROW = ROWS
KROWS = ROWS + PARTS
SCALE = 64 ** -0.5
L1_SCALE = 1.0 / 16.0
LN_EPS = 1e-5
RMS_EPS = 1e-8
Q_PART = (0, 0, 0, 1, 1, 2)
K_PART = (0, 1, 2, 0, 1, 0)
PAIRS = len(Q_PART)
RUNS = PARTS

COL_LN = 0
COL_FF = 12
COL_BQ, COL_BK, COL_BV = 28, 30, 32
N_COLS = 34
ROW_BO1, ROW_BO2, ROW_BFF2, ROW_W, ROW_BFC = range(5)


def build(nc, a):
    with ExitStack() as ctx:
        ends, sizes = {}, {}

        def sb(name, shape, dt=F32):
            t = ctx.enter_context(nc.sbuf_tensor(name, shape, dt))
            ends[name] = nc.sbuf_base
            sizes[name] = int(np.prod(shape[1:])) * mybir.dt.size(dt)
            return t

        def over(name, old, shape, dt, start=0):
            return nc.alloc_sbuf_tensor_at(name, shape, dt, offset=ends[old] - sizes[old] + start)

        def sem(name):
            return ctx.enter_context(nc.semaphore(name))

        def scratch(name, shape, dt):
            return nc.dram_tensor(name, shape, dt).ap()

        q_d, q2_d = (scratch(n, [2, B * NC, PARTS, P, BLK], BF16) for n in ("q_parts", "q2_parts"))
        k_d = scratch("k_parts", [B * NC, PARTS, P, S], BF16)
        k2_d = scratch("k2_parts", [NC, PARTS, P, B * CTX], BF16)
        v_d = scratch("v_groups", [P, KC, GROUPS * P], F32)

        x = sb("x", [P, TILES, D])
        tok = sb("tok", [P, TILES, D])
        xT = sb("xT", [P, NC, T])
        wkv1, wo1 = sb("wkv1", [P, NC, 2 * D]), sb("wo1", [P, NC, D])
        wq2, wkv2, wo2 = sb("wq2", [P, NC, D]), sb("wkv2", [P, NC, 2 * D]), sb("wo2", [P, NC, D])
        wff1, wff2 = sb("wff1", [P, NC, 2 * F]), sb("wff2", [P, FC, D])
        early = sb("early", [P, 5 * NC * D + 4 * 2 * D])
        wql, wkT, wvT, wfcT, wq1 = (early[:, i * NC * D:(i + 1) * NC * D].rearrange("p (c n) -> p c n", c=NC) for i in range(5))
        vstage = early[:, 5 * NC * D:5 * NC * D + 8 * D].rearrange("p (t h d) -> p t h d", t=4, h=H)
        ctxT = sb("ctxT", [P, NC, B * CTX])
        cols = sb("cols", [P, N_COLS])
        rows = sb("rows", [P, 5, D])
        ident, identb = sb("ident", [P, P]), sb("identb", [P, P], BF16)
        ones = sb("ones", [P, P])
        bq_wide = sb("bq_wide", [P, NC, P])
        stack = sb("stack", [P, 4, HG, S], BF16)
        qs = stack[:, :, :, :].rearrange("p s h n -> p s (h n)").rearrange("p s (f h n) -> p s f h n", f=2, h=HG)
        k2 = sb("k2", [P, B, H, CTXP], BF16)
        v1 = sb("v1", [P, 2, KC, P])
        attT = (wkv1, wkv2)
        v2 = sb("v2", [P, B, GPB, P])
        rest = sb("rest", [P, 2, BLK])
        probs = sb("probs", [P, 2, HG, BLK])
        def ring(v):
            return v.bitcast(BF16)[:, 0:RING * PARTS * BLK].rearrange("p (s i n) -> p s i n", s=RING, i=PARTS)
        part_1, part_2 = ring(probs[:, :, :, :].rearrange("p a b c -> p (a b c)")), ring(early[:, :])
        outT = sb("outT", [P, 2, BLK])
        half_stack = 2 * HG * S * mybir.dt.size(BF16)
        hid_hi = over("hid_hi", "stack", [P, HID_RING, BLK], F32R)
        hid_lo = over("hid_lo", "stack", [P, HID_RING, BLK], F32R, half_stack // 2)
        wff1_hi = over("wff1_hi", "stack", [P, NC, 2, FC, P], F32R, half_stack)
        wff1_lo = over("wff1_lo", "wff1", [P, NC, 2, FC, P], F32R)
        wff1_v = wff1[:, :, :].rearrange("p c (i f n) -> p c i f n", i=2, f=FC)
        wff2_hi, wff2_lo = over("wff2_hi", "v1", [P, FC, D], F32R), over("wff2_lo", "wff2", [P, FC, D], F32R)
        x_hi = [over(f"x_hi{i}", t, [P, NC, BLK], F32R) for i, t in enumerate(("rest", "outT"))]
        x_lo = over("x_lo", "xT", [P, NC, T], F32R)
        hid = k2[:, :, :, :].rearrange("p b h n -> p (b h n)").bitcast(F32)[:, 0:2 * BLK].rearrange("p (r n) -> p r n", r=2)
        gate = vstage[:, 0:2, :, :].rearrange("p a h d -> p a (h d)")
        st = sb("st", [P, TPB, 6])
        mv = sb("mv", [P, 2, TPB, 2])
        var, half_var, rstd = (sb(n, [P, 2, TPB]) for n in ("var", "half_var", "rstd"))
        mm = sb("mm", [P, 2, 32])
        mrest = sb("mrest", [P, 2, 32])
        mpart = sb("mpart", [P, 2, PARTS * 32], BF16)
        mT = sb("mT", [P, 2, P], BF16)
        rec = sb("rec", [P, 2, TPB * HG])
        kT, vT, g1, cb = (sb(n, [P, NC, B * CTX]) for n in ("kT", "vT", "g1", "cb"))
        vw = sb("vw", [P, B, D])
        s1 = probs[:, :, :, :].rearrange("p a b c -> p (a b c)")[:, 0:BLOCKS * TPB * CTX].rearrange(
            "p (r t n) -> p r t n", r=BLOCKS, t=TPB)
        p1T = sb("p1T", [P, BLOCKS, BLK])
        m1, nm1, sum1, r1, ss1, rms, ms, half_ms = (sb(n, [P, BLOCKS, TPB]) for n in ("m1", "nm1", "sum1", "r1", "ss1", "rms", "ms", "half_ms"))
        sq = sb("sq", [P, D])

        ps = ctx.enter_context(nc.psum_tensor("ps", [P, 8, BLK], F32))
        ps_b = ps[:, 7, :].bitcast(BF16)
        ST, PV, MISC = 4, 6, 7
        CHAIN = 2

        x_in = [sem(f"x_in{i}") for i in range(BLOCKS)]
        w_in = {n: sem(f"{n}_in") for n in ("cols", "rows", "wqkv1", "wo1", "w2", "wo2", "wff", "wl1", "ctx", "k2")}
        k_in = [sem(f"k_in{i}") for i in range(2)]
        q_in = [[sem(f"q_in{h}{i}") for i in range(2)] for h in range(2)]
        v_in = [sem(f"v_in{i}") for i in range(2)]
        m_in = [sem("m_in0"), sem("m_in1")]
        q2_in = [[sem(f"q2_in{h}{i}") for i in range(4)] for h in range(2)]
        m2_in = [sem(f"m2_in{i}") for i in range(4)]
        part_out = [sem(f"part_out{i}") for i in range(RING)]
        v_out = [sem(f"v_out{i}") for i in range(2)]
        y_out = sem("y_out")
        pool_step, c_bq = sem("pool_step"), sem("c_bq")
        dve_step = sem("dve_step")
        var_ready, tok_ready = sem("var_ready"), sem("tok_ready")
        turn_full, turn_done = sem("turn_full"), sem("turn_done")
        pj_full, hi_done, rest_done, mid_done, lo_done = (sem(n) for n in ("pj_full", "hi_done", "rest_done", "mid_done", "lo_done"))
        v_full, v_done = sem("v_full"), sem("v_done")
        su_full, su_done = sem("su_full"), sem("su_done")
        w1_hi, w1_lo, w2_split, x_hi_done, x_lo_done, hid_hi_done, hid_lo_done = (
            sem(n) for n in ("w1_hi", "w1_lo", "w2_split", "x_hi_done", "x_lo_done", "hid_hi_done", "hid_lo_done"))
        s_full, s_red = sem("s_full"), sem("s_red")
        st_full, exp_done = sem("st_full"), sem("exp_done")
        pv_done, out_copied, out_turned = sem("pv_done"), sem("out_copied"), sem("out_turned")
        m_step, m_turned, m_copied = (sem(n) for n in ("m_step", "m_turned", "m_copied"))
        rec_done, att_done = sem("rec_done"), sem("att_done")
        s2_full, s2_red = sem("s2_full"), sem("s2_red")
        y_full, y_added, bias_added = sem("y_full"), sem("y_added"), sem("bias_added")
        ff_gate, ff_full, narrowed, gate_done, hid_done = sem("ff_gate"), sem("ff_full"), sem("narrowed"), sem("gate_done"), sem("hid_done")
        l_full, l_added, l_max, l_exp, l_turned, l_pT, l_pv, l_y, l_sq, l_root, l_scaled, l_out, l_last = (
            sem(f"l_{n}") for n in ("full", "added", "max", "exp", "turned", "pT", "pv", "y", "sq", "root", "scaled", "out", "last"))

        block = ctx.enter_context(nc.Block())

        LN1, ATT1, LN2, ATT2, LN3, X3 = range(6)
        LAST_PAIR = GROUPS // 2 - 1

        def num(g):
            return 2 * g[0] + g[1]

        def after(g):
            return (g[0], 1) if g[1] == 0 else (g[0] + 1, 0)

        Q2_SLOT = (0, 2, 1, 3)

        def q2_slot(G, half):
            return qs[:, Q2_SLOT[G % 4], half, :, :]

        TURNS = [(LN1, blk) for blk in range(BLOCKS)]
        TURNS += [(phase, 2 * b + i) for att, ln in ((ATT1, LN2), (ATT2, LN3)) for b in range(B)
                  for phase in (att, ln) for i in range(2)]
        TURNS += [(X3, blk) for blk in range(BLOCKS)]

        def turn_bank(phase, blk, c):
            if phase == LN1:
                return 2 * (blk % 2) + c
            return c if (phase, blk) == (ATT1, BLOCKS - 1) else CHAIN + c

        def out_bank(k):
            return CHAIN + k % 2 if k < 2 * TILES else WIDE[k % TPB]

        def proj_bank(u):
            return (4 if u < PROJ_2 else CHAIN) + u % 2

        def part(u):
            return (part_1 if u < PROJ_2 else part_2)[:, u % RING, :, 0:width(u)]

        CHAIN_1, CHAIN_2 = 17, 12
        TAIL = (1, 1, 1, 1, 1, 2, 1, 2, 1, 2, 2, 2)
        AHEAD, FIRST_S2 = 6, (0, 1, 0, 1, 0, 1, 0, 1) * 2
        UNITS = 8

        def pieces(G, n):
            if G == 0:
                return 1 if n in (1, 3, 5) else 0
            return 1 if G >= GROUPS - 3 and n % 2 == 0 else 0

        FF_PIECES = (1, 2, 2, 2, 2, 1, 1, 1)
        assert sum(TAIL) == CHAIN_1 == AHEAD + sum(FIRST_S2) + sum(pieces(0, n) for n in range(UNITS))
        assert sum(FF_PIECES) == CHAIN_2 == sum(pieces(G, n) for G in range(1, GROUPS) for n in range(UNITS))

        LINEAR, GATE, WIDE = 4, 5, (0, 1, 6, 7)

        def x3_step(n):
            blk, i = divmod(n - FF_LAG - FC, FC)
            return (blk, i) if 0 <= blk < BLOCKS - 1 and n < FC * BLOCKS + FF_LAG else (0, None)

        def chunk_used(eng, n):
            blk, f = divmod(n, FC)
            if f == FC - 1:
                eng.wait_ge(y_full, 2 * TILES + TPB * (blk + 1))
            else:
                eng.wait_ge(narrowed, (FC - 1) * blk + f + 1)

        def st_bank(g, k, h):
            tail = isinstance(g[0], int) and g == (LAST_PAIR, 1) and k >= LEAD
            return (ST, ST + 1, 0, 1)[h] if tail else ST + h % 2

        EARLY = 2
        LEAD = 4

        PROJ = [(k, o, blk) for blk in range(2) for k in "qk" for o in range(NC)]
        PROJ_B0 = len(PROJ)
        PROJ += [("k2", o, 0) for o in range(NC)]
        PROJ_K2 = len(PROJ)
        PROJ += [(k, o, blk) for blk in range(2, BLOCKS) for k in "qk" for o in range(NC)]
        PROJ_2 = len(PROJ)
        PROJ += [("q2", o, blk) for blk in range(BLOCKS) for o in range(NC)]

        FIRST_PAIR = 2
        SETUP_1, SETUP_2 = 6, 5

        def first_of(blk):
            return TPB * blk if blk < 2 else PROJ_K2 + TPB * (blk - 2)

        def width(u):
            return B * CTX if PROJ[u][0] == "k2" else BLK

        def advance(chain, n):
            for _ in range(n):
                next(chain)

        def parts_stored(eng, upto):
            for slot in range(RING):
                eng.wait_ge(part_out[slot], 16 * len(range(slot, upto, RING)))

        @block.sync
        def _(eng):
            def chunks(w):
                return w.rearrange("(c p) n -> p c n", p=P)

            x_v = a["x"].rearrange("b (t p) d -> p (b t) d", p=P)

            def load_x(blk):
                eng.dma_start(x[:, TPB * blk:TPB * blk + TPB, :], x_v[:, TPB * blk:TPB * blk + TPB, :]).then_inc(x_in[blk], 16)

            load_x(0)
            eng.dma_start(cols[:, :], a["cols"]).then_inc(w_in["cols"], 16)
            eng.dma_start(wq1[:, :, :], chunks(a["Wq1"])).then_inc(w_in["wqkv1"], 16)
            eng.dma_start(wkv1[:, :, :], chunks(a["Wkv1"])).then_inc(w_in["wqkv1"], 16)
            for blk in range(1, BLOCKS):
                load_x(blk)
            eng.dma_start(ctxT[:, :, :], chunks(a["ctxT"])).then_inc(w_in["ctx"], 16)
            eng.dma_start(wq2[:, :, :], chunks(a["Wq2"])).then_inc(w_in["w2"], 16)
            eng.dma_start(wkv2[:, :, :], chunks(a["Wkv2"])).then_inc(w_in["w2"], 16)
            for t, n in ((wql, "Wq"), (wkT, "WkT"), (wvT, "WvT"), (wfcT, "WfcT")):
                eng.dma_start(t[:, :, :], chunks(a[n])).then_inc(w_in["wl1"], 16)
            eng.dma_start(rows[:, :, :], a["rows"].partition_broadcast(P)).then_inc(w_in["rows"], 16)
            eng.dma_start(wo1[:, :, :], chunks(a["Wo1"])).then_inc(w_in["wo1"], 16)

            def store_parts(u):
                kind, o, blk = PROJ[u]
                eng.wait_ge(lo_done, u + 1)
                slot = u % RING
                if kind == "k2":
                    dst = k2_d[o]
                elif kind == "k":
                    dst = k_d[NC * (blk // 2) + o, :, :, BLK * (blk % 2):BLK * (blk % 2) + BLK]
                else:
                    dst = {"q": q_d, "q2": q2_d}[kind][blk % 2, NC * (blk // 2) + o]
                eng.dma_start(dst.rearrange("i r n -> r i n"), part(u)).then_inc(part_out[slot], 16)

            def store_v(t):
                eng.wait_ge(v_done, t + 2)
                b, kc, pair = t // KC, t % KC, t // 2 % 2
                eng.dma_start(v_d[:, kc:kc + 2, GPB * P * b:GPB * P * b + GPB * P],
                              vstage[:, 2 * pair:2 * pair + 2, :, :].rearrange("p t h d -> p t (h d)")).then_inc(v_out[pair], 16)

            def load_stack(dst, src, heads, which, done):
                i = 0
                while i < PAIRS:
                    rise = int(i + 1 < PAIRS and which[i + 1] > which[i])
                    n = 1
                    while i + n < PAIRS and which[i + n] == which[i] + rise * n:
                        n += 1
                    rows = src[which[i]:which[i] + (n if rise else 1)].rearrange("i (r h) n -> (i r) h n", r=DH)
                    rows = rows[:, heads, :].rearrange("r h n -> r (h n)")
                    if not rise:
                        rows = rows.unsqueeze(0).to_broadcast([n, DH, rows.shape[-1]])
                    eng.dma_start(dst[DH * i:DH * (i + n), :, :].rearrange("r h n -> r (h n)"), rows).then_inc(done, 16)
                    i += n

            def load_group(g):
                pair, slot = g

                def of(d):
                    return d[bass.ds(pair, 1)].rearrange("o i p n -> (o i) p n")
                heads = slice(HG * slot, HG * slot + HG)
                load_stack(stack[:, 2 + slot, :, :], of(k_d), heads, K_PART, k_in[slot])
                for h in range(2):
                    load_stack(qs[:, slot, h, :, :], of(q_d[h]), heads, Q_PART, q_in[h][slot])

            def load_v(g):
                G, slot = num(g), g[1]
                eng.dma_start(v1[:, slot, :, :], v_d[:, :, bass.ds(P * G, P)]).then_inc(v_in[slot], 16)

            def load_max(g, half):
                G, slot = num(g), g[1]
                eng.wait_ge(m_copied, 2 * G + half + 1)
                eng.dma_start(qs[MROW:KROWS, slot, half, :, :].rearrange("i h n -> i (h n)"),
                              mT[0:PARTS * HG * TPB, half, :]).then_inc(m_in[half], 16)

            def v_stored(tiles):
                for s in range(2):
                    eng.wait_ge(v_out[s], 16 * tiles // 4)

            for blk in range(BLOCKS):
                if blk == 2:
                    parts_stored(eng, PROJ_B0)
                    load_group((0, 0))
                    v_stored(KC)
                    load_v((0, 0))
                    for u in range(PROJ_B0, PROJ_K2):
                        store_parts(u)
                for i in range(TPB):
                    store_parts(first_of(blk) + i)
                    if i % 2 == 1:
                        store_v(TPB * blk + i - 1)
                if blk == 2:
                    load_group((0, 1))
                    load_v((0, 1))
            parts_stored(eng, PROJ_2)
            v_stored(TILES)
            load_max((0, 0), 0)
            eng.dma_start(wo2[:, :, :], chunks(a["Wo2"])).then_inc(w_in["wo2"], 16)
            eng.dma_start(wff1[:, :, :], chunks(a["Wff1"])).then_inc(w_in["wff"], 16)
            eng.dma_start(wff2[:, :, :], chunks(a["Wff2"])).then_inc(w_in["wff"], 16)

            def self_group(g, loads):
                n = after(g)
                load_max(g, 1)
                if loads is not None:
                    load_max(n, 0)
                if loads:
                    eng.wait_ge(st_full, 64 * num(n))
                    two = (g[0] + 1, g[1])
                    load_group(two)
                    eng.wait_ge(pv_done, 16 * num(n))
                    load_v(two)

            with eng.Fori(0, LAST_PAIR) as gp:
                self_group((gp, 0), True)
                self_group((gp, 1), True)
            self_group((LAST_PAIR, 0), False)
            self_group((LAST_PAIR, 1), None)

            def load_q2(G, halves=(0, 1)):
                for h in halves:
                    load_stack(q2_slot(G, h), q2_d[h, G // 2], slice(HG * (G % 2), HG * (G % 2) + HG), Q_PART, q2_in[h][G % 4])

            def load_max_2(G):
                eng.wait_ge(m_copied, 2 * GROUPS + G + 1)
                eng.dma_start(stack[MROW:KROWS, Q2_SLOT[G % 4], :, :].rearrange("i h n -> i (h n)"),
                              mT[0:PARTS * HG * KC, G % 2, :]).then_inc(m2_in[G % 4], 16)

            half = PROJ_2 + 2 * NC
            for u in range(PROJ_2, half):
                store_parts(u)
            parts_stored(eng, half)
            load_q2(0)
            load_q2(1)
            eng.wait_ge(st_full, 64 * GROUPS)
            load_q2(2)
            load_q2(3)
            load_max_2(0)
            for u in range(half, len(PROJ)):
                store_parts(u)
                if u == half + 1:
                    load_max_2(1)
            parts_stored(eng, len(PROJ))
            for G in range(GROUPS):
                if G + 4 < GROUPS:
                    eng.wait_ge(st_full, 64 * GROUPS + UNITS * (G + 1))
                    load_q2(G + 4, (0,))
                if G + 2 < GROUPS:
                    load_max_2(G + 2)
                if G + 4 < GROUPS:
                    load_q2(G + 4, (1,))

            out_v = a["out"].rearrange("b (t p) d -> p (b t) d", p=P)
            for blk in range(BLOCKS):
                if blk < BLOCKS - 1:
                    eng.wait_ge(l_out, TPB * (blk + 1))
                else:
                    eng.wait_ge(l_last, TPB)
                eng.dma_start(out_v[:, TPB * blk:TPB * blk + TPB, :], x[:, TPB * blk:TPB * blk + TPB, :]).then_inc(y_out, 16)
            eng.wait_ge(y_out, 16 * BLOCKS)

        IDENTS_SET, V_PADS_SET, CONSTS = 4, 6, 15

        @block.gpsimd
        def _(eng):
            done = [0]

            def alone(ins):
                done[0] += 1
                ins.then_inc(pool_step, 1)
                eng.wait_ge(pool_step, done[0])

            for t in (ident, identb):
                alone(eng.memset(t[:, :], 0.0))
                alone(eng.affine_select(out=t[:, :], in_=t[:, :], compare_op=ALU.not_equal, fill=1.0, base=0,
                                        pattern=[[-1, P]], channel_multiplier=1))
            alone(eng.memset(vstage[:, :, :, :], 0.0))
            alone(eng.memset(vstage[:, :, :, DH:DH + 1], 1.0))
            alone(eng.memset(ones[:, :], 1.0))
            alone(eng.memset(mpart[:, :, :], 0.0))
            alone(eng.memset(stack[MROW:MROW + PARTS, 2:4, :, :], 1.0))
            alone(eng.memset(k2[:, :, :, :], 0.0))
            alone(eng.memset(k2[MROW:MROW + PARTS, :, :, 0:CTX], 1.0))
            alone(eng.memset(v2[:, :, :, :], 0.0))
            alone(eng.memset(v2[0:CTX, :, :, :].rearrange("p b g (h d) -> p (b g) h d", h=HG)[:, :, :, DH:DH + 1], 1.0))
            alone(eng.memset(vw[:, :, :], 0.0))
            alone(eng.memset(p1T[:, :, :], 0.0))
            assert done[0] == CONSTS
            eng.wait_ge(w_in["rows"], 16)
            for n, row in enumerate((ROW_BO1, ROW_BO2, ROW_BFF2)):
                for blk in range(BLOCKS):
                    eng.wait_ge(tok_ready, TPB * (BLOCKS * n + blk + 1))
                    xb = x[:, TPB * blk:TPB * blk + TPB, :]
                    eng.tensor_tensor(xb, xb, rows[:, row:row + 1, :].to_broadcast([P, TPB, D]), ALU.add).then_inc(bias_added, 1)
                if n == 1:
                    eng.wait_ge(w_in["wff"], 32)
                    eng.wait_ge(pv_done, 16 * GROUPS)
                    for f in range(0, FC, 2):
                        hi, w = wff2_hi[:, f:f + 2, :], wff2[:, f:f + 2, :]
                        eng.tensor_copy(hi, w).then_inc(w2_split, 1)
                        eng.wait_ge(w2_split, f + 1)
                        eng.tensor_tensor(wff2_lo[:, f:f + 2, :], w, hi.bitcast(F32), ALU.subtract).then_inc(w2_split, 1)
                        eng.wait_ge(w2_split, f + 2)
                if n == 0:
                    parts_stored(eng, PROJ_K2)
                    for b in range(B):
                        for o in range(NC):
                            for i, p, n in ((0, 0, 3), (3, 0, 2), (5, 0, 1)):
                                eng.dma_start(k2[DH * i:DH * (i + n), b, 8 * o:8 * o + 8, 0:CTX],
                                              k2_d[o, p:p + n, :, CTX * b:CTX * b + CTX].rearrange("i (r h) n -> (i r) h n", r=DH)
                                              ).then_inc(w_in["k2"], 16)

            for blk in range(BLOCKS - 1):
                for i in range(TPB * blk, TPB * blk + TPB):
                    eng.wait_ge(l_scaled, i + 1)
                    eng.tensor_tensor(x[:, i, :], x[:, i, :], rows[:, ROW_W, :], ALU.mult).then_inc(l_out, 1)

        @block.tensor
        def _(eng):
            def by_group(i, c):
                b, j = divmod(i, KC)
                start = 2 * TPB * P * (NC * b + c) + P * j
                return tok[:, :, :].rearrange("p t d -> p (t d)")[:, start:start + P]

            def turn(phase, blk):
                k = TURNS.index((phase, blk))
                b = blk // 2
                if phase == X3:
                    if blk >= 1:
                        eng.wait_ge(l_added, blk)
                    eng.wait_ge(turn_done, 2 * k)
                elif (phase, blk) == (ATT1, BLOCKS - 1):
                    eng.wait_ge(exp_done, 64 * GROUPS)
                elif phase != LN1:
                    n = 0 if phase in (ATT1, LN2) else 1
                    eng.wait_ge(turn_done, 2 * k)
                    outs = TILES * n + KC * b + (0 if phase in (ATT1, ATT2) else KC)
                    if outs > 0:
                        eng.wait_ge(y_added, outs)
                    eng.wait_ge(rest_done, len(PROJ) if n else PROJ_2 + 2 * NC * b + (NC * (blk % 2) if phase == LN2 else 0))
                    if phase in (ATT1, ATT2):
                        eng.wait_ge(att_done, EARLY + 2 * GROUPS * n + 2 * GPB * (b + 1))
                elif k >= 2:
                    eng.wait_ge(turn_done, 2 * k - 2)
                for c in range(NC):
                    for t in range(TPB):
                        i = TPB * blk + t
                        if c == 0:
                            if phase in (LN1, LN2, LN3):
                                n = (LN1, LN2, LN3).index(phase)
                                eng.wait_ge(tok_ready, TILES * n + i + 1)
                            elif phase == X3:
                                eng.wait_ge(y_added, 2 * TILES + i + 1)
                        src = by_group(i, c) if phase in (ATT1, ATT2) else (x if phase == X3 else tok)[:, i, P * c:P * c + P]
                        mm_ = eng.transpose(ps[:, turn_bank(phase, blk, c), P * t:P * t + P], src, ident[:, :])
                    mm_.then_inc(turn_full, 1)

            def turned(phase, blk):
                eng.wait_ge(turn_done, 2 * TURNS.index((phase, blk)) + 2)

            def project(u):
                kind, o, blk = PROJ[u]
                w = {"q": wq1, "k": wkv1, "q2": wq2, "k2": wkv2}[kind]
                src = ctxT if kind == "k2" else xT
                n, c0 = width(u), BLK * blk
                if u >= 2:
                    eng.wait_ge(rest_done, u - 1)
                for c in range(NC):
                    mm_ = eng.matmul(ps[:, proj_bank(u), 0:n], w[:, c, P * o:P * o + P], src[:, c, c0:c0 + n],
                                     start=(c == 0), stop=(c == NC - 1))
                mm_.then_inc(pj_full, 1)

            def values(t):
                if t >= 2:
                    eng.wait_ge(v_done, t - 1)
                for c in range(NC):
                    mm_ = eng.matmul(ps[:, 6 + t % 2, 0:D], xT[:, c, P * t:P * t + P], wkv1[:, c, D:2 * D],
                                     start=(c == 0), stop=(c == NC - 1))
                mm_.then_inc(v_full, 1)

            def scores(g, j, first=False):
                G, slot = num(g), g[1]
                half, jj = divmod(j, 8)
                h, t0 = jj // 2, 2 * (jj % 2)
                if j == 0:
                    eng.wait_ge(k_in[slot], 16 * RUNS * (g[0] + 1))
                if j in (0, 8):
                    eng.wait_ge(q_in[half][slot], 16 * RUNS * (g[0] + 1))
                for i in range(2):
                    n = 32 * G + 2 * j + i
                    if not (first and n < 2):
                        eng.wait_ge(s_red, n - 1)
                    for kh in range(2):
                        mm_ = eng.matmul(ps[:, 2 * i + kh, :], qs[0:ROWS, slot, half, h, P * (t0 + i):P * (t0 + i) + P],
                                         stack[0:ROWS, 2 + slot, h, BLK * kh:BLK * kh + BLK], start=True, stop=True)
                        if kh == 1:
                            mm_.then_inc(s_full, 1)
                        yield

            eng.sem_inc(out_turned, EARLY)
            eng.wait_ge(pool_step, IDENTS_SET)
            turn(LN1, 0)
            eng.wait_ge(w_in["wqkv1"], 32)
            for blk in range(2):
                turned(LN1, blk)
                for i in range(TPB):
                    project(first_of(blk) + i)
                    values(TPB * blk + i)
                    if i == 1:
                        turn(LN1, blk + 1)
            turn(LN1, BLOCKS - 1)
            eng.wait_ge(w_in["ctx"], 16)
            eng.wait_ge(w_in["w2"], 32)
            for u in range(PROJ_B0, PROJ_K2):
                project(u)
            turned(LN1, BLOCKS - 1)
            first_scores = (part for j in range(16 - LEAD) for part in scores((0, 0), j, first=True))

            def tile_of_scores():
                for _ in range(2):
                    next(first_scores, None)

            for blk in range(2, BLOCKS):
                for i in range(TPB):
                    project(first_of(blk) + i)
                    if TPB * (blk - 2) + i >= FIRST_PAIR:
                        tile_of_scores()
                    values(TPB * blk + i)
                    if TPB * (blk - 2) + i >= FIRST_PAIR:
                        tile_of_scores()

            su = [0]

            def setup(m, n, terms):
                k = su[0]
                su[0] += 1
                if k >= 2:
                    eng.wait_ge(su_done, k - 1)
                else:
                    eng.wait_ge(v_done, TILES - 1 + k)
                if k == SETUP_1 + 1:
                    eng.wait_ge(m_copied, 1)
                for i, (lhs, rhs) in enumerate(terms):
                    mm_ = eng.matmul(ps[0:m, 6 + k % 2, 0:n], lhs, rhs, start=(i == 0), stop=(i == len(terms) - 1))
                mm_.then_inc(su_full, 1)
                tile_of_scores()

            eng.wait_ge(w_in["wl1"], 64)
            cut = [slice(CTX * b, CTX * b + CTX) for b in range(B)]
            for b in range(B):
                setup(CTX, D, [(ctxT[:, c, cut[b]], wkv2[:, c, D:2 * D]) for c in range(NC)])
            for w in (wkT, wvT):
                for o in range(NC):
                    setup(P, B * CTX, [(w[:, c, P * o:P * o + P], ctxT[:, c, :]) for c in range(NC)])
            eng.wait_ge(su_done, SETUP_1)
            eng.wait_ge(pool_step, CONSTS)
            eng.wait_ge(m_step, 4)
            eng.transpose(ps_b[0:96, 0:P], mpart[:, 0, :], identb[:, :]).then_inc(m_turned, 1)
            eng.wait_ge(c_bq, NC)
            for o in range(NC):
                setup(P, B * CTX, [(wql[:, c, P * o:P * o + P], kT[:, c, :]) for c in range(NC)])
            setup(P, B * CTX, [(bq_wide[:, c, :], kT[:, c, :]) for c in range(NC)])
            eng.wait_ge(w_in["rows"], 16)
            for b in range(B):
                setup(CTX, D, [(vT[:, c, cut[b]], wfcT[:, c, :]) for c in range(NC)]
                      + [(ones[0:1, 0:CTX], rows[0:1, ROW_BFC, :])])
            eng.wait_ge(su_done, SETUP_1 + SETUP_2)
            eng.wait_ge(rest_done, PROJ_2)

            def chain(n, b):
                att, ln, w = ((ATT1, LN2, wo1), (ATT2, LN3, wo2))[n]
                eng.wait_ge(w_in[("wo1", "wo2")[n]], 16)
                if (n, b) == (0, 0):
                    eng.wait_ge(s_red, 32 * GROUPS)
                for blk in (2 * b, 2 * b + 1):
                    turn(att, blk)
                    yield
                turned(att, 2 * b + 1)
                for i in range(KC):
                    k = TILES * n + KC * b + i
                    if i >= 2:
                        eng.wait_ge(y_added, k - 1)
                    t = i % TPB
                    for c in range(NC):
                        mm_ = eng.matmul(ps[:, out_bank(k), 0:D], attT[i // TPB][:, c, P * t:P * t + P], w[:, c, :],
                                         start=(c == 0), stop=(c == NC - 1))
                    mm_.then_inc(y_full, 1)
                    yield
                for blk in (2 * b, 2 * b + 1):
                    turn(ln, blk)
                    yield
                    if n == 0:
                        turned(ln, blk)
                        for o in range(NC):
                            project(PROJ_2 + NC * blk + o)
                            yield
                if n == 0:
                    yield

            def scores_t(g, k, h, first=False):
                G, slot = num(g), g[1]
                half, kc = divmod(k, KC)
                if kc == 0 and h == 0:
                    eng.wait_ge(m_in[half], 16 * (G + 1))
                if st_bank(g, k, 2) == ST:
                    if not (first and k == 0 and h < 2):
                        eng.wait_ge(exp_done, 64 * G + 4 * k + h - 1)
                elif k > LEAD:
                    eng.wait_ge(exp_done, 64 * G + 4 * k + h - 3)
                elif h < 2:
                    eng.wait_ge(exp_done, 64 * G + 4 * k + h - 1)
                else:
                    eng.wait_ge(s_red, 32 * GROUPS)
                eng.matmul(ps[:, st_bank(g, k, h), :], stack[0:KROWS, 2 + slot, h, P * kc:P * kc + P],
                           qs[0:KROWS, slot, half, h, :], start=True, stop=True).then_inc(st_full, 1)

            def weigh(g, k):
                G, slot = num(g), g[1]
                half, kc = divmod(k, KC)
                eng.wait_ge(exp_done, 64 * G + 4 * k + 4)
                if k == 0:
                    eng.wait_ge(v_in[slot], 16 * (g[0] + 1))
                if kc == 0 and not (isinstance(G, int) and G == 0 and half == 0):
                    eng.wait_ge(out_copied, 2 * G + half)
                for h in range(HG):
                    mm_ = eng.matmul(ps[32 * h:32 * h + 32, PV, :], v1[:, slot, kc, 32 * h:32 * h + 32],
                                     probs[:, k % 2, h, :], start=(kc == 0), stop=(kc == KC - 1))
                mm_.then_inc(pv_done, 1)

            def turn_out(e, half, m_before):
                eng.wait_ge(out_copied, e + 1)
                eng.wait_ge(m_copied, m_before)
                for t in range(TPB):
                    mm_ = eng.transpose(ps[:, MISC, P * t:P * t + P], outT[:, half, P * t:P * t + P], ident[:, :])
                mm_.then_inc(out_turned, 1)

            def turn_max(g, half):
                e = 2 * num(g) + half
                eng.wait_ge(m_step, 4 * e + 4)
                eng.wait_ge(att_done, EARLY + e - 1)
                eng.transpose(ps_b[0:96, 0:P], mpart[:, half, :], identb[:, :]).then_inc(m_turned, 1)

            def step(g, k, lead=True, first=False):
                G = num(g)
                lead_g, j = (g, k + 16 - LEAD) if k < LEAD else (after(g), k - LEAD)
                four = scores(lead_g, j) if lead or k < LEAD else iter(())
                for h, n in enumerate((3, 1, 0, 0)):
                    scores_t(g, k, h, first)
                    for _ in range(n):
                        next(four, None)
                    if h == 2 and k > 0:
                        weigh(g, k - 1)
                    elif h == 2 and not first:
                        weigh(before(g), 15)
                if k == 1 and not first:
                    turn_out(2 * G - 1, 1, 2 * G + 1)
                if k == 5:
                    turn_max(g, 1)
                if k == 9:
                    turn_out(2 * G, 0, 2 * G + 2)
                if k == 13 and lead:
                    turn_max(after(g), 0)

            def before(g):
                return (g[0], 0) if g[1] == 1 else (g[0] - 1, 1)

            def self_group(g, lead=True, chain=None):
                for k in range(LEAD, 16):
                    step(g, k, lead)
                    if not lead:
                        advance(chain, TAIL[k - LEAD])
                if lead:
                    for k in range(LEAD):
                        step(after(g), k)

            for _ in first_scores:
                pass
            for k in range(LEAD):
                step((0, 0), k, first=True)
            with eng.Fori(0, LAST_PAIR) as gp:
                self_group((gp, 0))
                self_group((gp, 1))
            self_group((LAST_PAIR, 0))
            self_group((LAST_PAIR, 1), lead=False, chain=chain(0, 0))
            weigh((LAST_PAIR, 1), 15)
            eng.wait_ge(att_done, EARLY + 2 * GROUPS - 1)
            turn_out(2 * GROUPS - 1, 1, 2 * GROUPS)

            def scores_2(G, t):
                b, slot = G // GPB, Q2_SLOT[G % 4]
                if t % TPB == 0:
                    eng.wait_ge(q2_in[t // TPB][G % 4], 16 * RUNS * (G // 4 + 1))
                n = KC * G + t
                if n >= 2:
                    eng.wait_ge(s2_red, n - 1)
                for h in range(HG):
                    mm_ = eng.matmul(ps[:, n % 2, CTX * h:CTX * h + CTX], qs[0:ROWS, slot, t // TPB, h, P * (t % TPB):P * (t % TPB) + P],
                                     k2[0:ROWS, b, HG * (G % GPB) + h, 0:CTX], start=True, stop=True)
                mm_.then_inc(s2_full, 1)

            def scores_t2(G, n):
                b, (half, h) = G // GPB, divmod(n, HG)
                if n == 0:
                    eng.wait_ge(m2_in[G % 4], 16 * (G // 4 + 1))
                eng.wait_ge(exp_done, 64 * GROUPS + UNITS * G + n - 1)
                eng.matmul(ps[0:CTXP, ST + h % 2, :], k2[0:KROWS, b, HG * (G % GPB) + h, :],
                           qs[0:KROWS, Q2_SLOT[G % 4], half, h, :], start=True, stop=True).then_inc(st_full, 1)

            def weigh_2(G, half):
                b = G // GPB
                eng.wait_ge(exp_done, 64 * GROUPS + UNITS * G + 4 * half + 4)
                eng.wait_ge(out_copied, 2 * GROUPS + 2 * G + half)
                for h in range(HG):
                    mm_ = eng.matmul(ps[32 * h:32 * h + 32, PV, :], v2[0:CTXP, b, G % GPB, 32 * h:32 * h + 32],
                                     probs[0:CTXP, half, h, :], start=True, stop=True)
                mm_.then_inc(pv_done, 1)

            def turn_out_2(G, half):
                e = 2 * GROUPS + 2 * G + half
                eng.wait_ge(out_copied, e + 1)
                eng.wait_ge(att_done, EARLY + e)
                eng.wait_ge(m_copied, 2 * GROUPS + min(G + 2 + half, GROUPS))
                for t in range(TPB):
                    mm_ = eng.transpose(ps[:, MISC, P * t:P * t + P], outT[:, half, P * t:P * t + P], ident[:, :])
                mm_.then_inc(out_turned, 1)

            def turn_max_2(G):
                eng.wait_ge(m_step, 8 * GROUPS + 4 * G + 4)
                eng.wait_ge(att_done, EARLY + 2 * GROUPS + max(2 * G - 3, 0))
                eng.transpose(ps_b[0:96, 0:P], mpart[:, G % 2, :], identb[:, :]).then_inc(m_turned, 1)

            def cross_unit(G, n):
                if G < GROUPS:
                    scores_t2(G, n)
                if G + 2 < GROUPS:
                    scores_2(G + 2, n)
                if n == 0 and G >= 1:
                    turn_out_2(G - 1, 0)
                if n == 1 and G >= 1:
                    weigh_2(G - 1, 1)
                if n == 2 and G + 1 < GROUPS:
                    turn_max_2(G + 1)
                if n == 5 and G >= 1:
                    turn_out_2(G - 1, 1)
                if n == 5 and G < GROUPS:
                    weigh_2(G, 0)

            after_self = chain(0, 1)
            advance(after_self, AHEAD)
            eng.wait_ge(w_in["k2"], 16 * RUNS * B * NC)
            for n, count in enumerate(FIRST_S2):
                G, t = divmod(n, KC)
                scores_2(G, t)
                if (G, t) == (1, 3):
                    turn_max_2(0)
                advance(after_self, count)
            after_cross = chain(1, 0)
            for G in range(GROUPS):
                for n in range(UNITS):
                    cross_unit(G, n)
                    advance(after_self if G == 0 else after_cross, pieces(G, n))
            for n in range(6):
                cross_unit(GROUPS, n)

            def widen(n):
                blk, f = divmod(n, FC)
                if f == 0:
                    eng.wait_ge(x_lo_done, blk + 1)
                if blk == 0:
                    eng.wait_ge(w1_lo, f + 1)
                xh = x_hi[blk % 2]
                xl = x_lo[:, :, BLK * blk:BLK * blk + BLK]
                for i, bank, read, full in ((1, GATE, gate_done, ff_gate), (0, LINEAR, hid_done, ff_full)):
                    if n >= 1:
                        eng.wait_ge(read, n)
                    for c in range(NC):
                        wh, wl = (w[:, c, i, f, :] for w in (wff1_hi, wff1_lo))
                        eng.matmul(ps[:, bank, :], wh, xh[:, c, :], start=(c == 0), stop=False)
                        eng.matmul(ps[:, bank, :], wh, xl[:, c, :], start=False, stop=False)
                        mm_ = eng.matmul(ps[:, bank, :], wl, xh[:, c, :], start=False, stop=(c == NC - 1))
                    mm_.then_inc(full, 1)

            def narrow(n):
                blk, f = divmod(n, FC)
                eng.wait_ge(hid_lo_done, n + 1)
                if f == 0 and blk > 0:
                    eng.wait_ge(y_added, 2 * TILES + TPB * blk)
                w2h, w2l = wff2_hi[:, f, :], wff2_lo[:, f, :]
                for t in range(TPB):
                    out = ps[:, WIDE[t], 0:D]
                    hh, hl = (v[:, n % HID_RING, P * t:P * t + P] for v in (hid_hi, hid_lo))
                    eng.matmul(out, hh, w2h, start=(f == 0), stop=False)
                    eng.matmul(out, hh, w2l, start=False, stop=False)
                    mm_ = eng.matmul(out, hl, w2h, start=False, stop=(f == FC - 1))
                    if f == FC - 1:
                        mm_.then_inc(y_full, 1)
                if f < FC - 1:
                    mm_.then_inc(narrowed, 1)

            def l1_scores(blk):
                turned(X3, blk)
                b = blk // 2
                for t in range(TPB):
                    for c in range(NC):
                        i = TPB * blk + t
                        mm_ = eng.matmul(ps[:, CHAIN, CTX * t:CTX * t + CTX], xT[:, c, P * i:P * i + P],
                                         g1[:, c, CTX * b:CTX * b + CTX], start=(c == 0), stop=(c == NC - 1))
                mm_.then_inc(l_full, 1)

            def l1_turn(blk):
                eng.wait_ge(l_exp, TPB * (blk + 1))
                if blk >= 2:
                    eng.wait_ge(l_pT, blk - 1)
                for t in range(TPB):
                    mm_ = eng.transpose(ps[0:CTX, LINEAR + blk % 2, P * t:P * t + P], s1[:, blk, t, :], ident[:, :])
                mm_.then_inc(l_turned, 1)

            def l1_weigh(blk):
                eng.wait_ge(l_pT, blk + 1)
                for t in range(TPB):
                    n = TPB * blk + t
                    if blk >= 1:
                        eng.wait_ge(l_y, n - TPB + 1)
                    eng.matmul(ps[:, WIDE[t], 0:D], p1T[0:CTXP, blk, P * t:P * t + P],
                               vw[0:CTXP, blk // 2, :], start=True, stop=True).then_inc(l_pv, 1)

            eng.wait_ge(exp_done, 72 * GROUPS)
            eng.wait_ge(w2_split, FC)
            after_cross = chain(1, 1)
            for n in range(FC * BLOCKS + FF_LAG):
                if n < FC * BLOCKS:
                    widen(n)
                if n < FC:
                    advance(after_cross, FF_PIECES[n])
                if n == FF_LAG:
                    eng.wait_ge(s2_red, KC * GROUPS)
                    eng.wait_ge(out_copied, 4 * GROUPS)
                    eng.wait_ge(att_done, EARLY + 4 * GROUPS)
                if n >= FF_LAG:
                    narrow(n - FF_LAG)
                blk, i = x3_step(n)
                if i == 1:
                    turn(X3, blk)
                if i == 2:
                    l1_scores(blk)

            eng.wait_ge(hid_done, FC * BLOCKS)
            last = BLOCKS - 1
            l1_turn(0)
            l1_turn(1)
            turn(X3, last)
            eng.wait_ge(y_added, 3 * TILES)
            l1_weigh(0)
            l1_scores(last)
            l1_turn(2)
            l1_weigh(1)
            l1_weigh(2)
            l1_turn(last)
            l1_weigh(last)

        @block.scalar
        def _(eng):
            def turn_copy(phase, blk):
                for c in range(NC):
                    eng.wait_ge(turn_full, 2 * TURNS.index((phase, blk)) + c + 1)
                    src = ps[:, turn_bank(phase, blk, c), :]
                    if phase in (ATT1, ATT2):
                        eng.activation(attT[blk % 2][:, c, :], src, ACT.Copy).then_inc(turn_done, 1)
                    elif phase == X3:
                        eng.activation(xT[:, c, BLK * blk:BLK * blk + BLK], src, ACT.Copy).then_inc(turn_done, 1)
                    else:
                        i = COL_LN + 4 * (LN1, LN2, LN3).index(phase)
                        eng.activation(xT[:, c, BLK * blk:BLK * blk + BLK], src, ACT.Identity,
                                       scale=cols[:, i + c:i + c + 1], bias=cols[:, i + 2 + c:i + 3 + c]).then_inc(turn_done, 1)

            def high(u):
                n, slot = width(u), u % RING
                eng.wait_ge(pj_full, u + 1)
                if u >= RING:
                    eng.wait_ge(part_out[slot], 16 * (u // RING))
                eng.activation(part(u)[:, 0, :], ps[:, proj_bank(u), 0:n], ACT.Copy).then_inc(hi_done, 1)

            def middle(u):
                eng.wait_ge(rest_done, u + 1)
                eng.activation(part(u)[:, 1, :], rest[:, u % 2, 0:width(u)], ACT.Copy).then_inc(mid_done, 1)

            def values(t):
                eng.wait_ge(v_full, t + 1)
                if t >= 4 and t % 2 == 0:
                    eng.wait_ge(v_out[t // 2 % 2], 16 * (t // 4))
                eng.activation(vstage[:, t % 4, :, 0:DH], ps[:, 6 + t % 2, 0:D].rearrange("p (h d) -> p h d", h=H),
                               ACT.Copy).then_inc(v_done, 1)

            eng.wait_ge(w_in["cols"], 16)
            turn_copy(LN1, 0)
            eng.wait_ge(pool_step, V_PADS_SET)
            for blk in range(BLOCKS):
                if blk == 2:
                    turn_copy(LN1, BLOCKS - 1)
                    for u in range(PROJ_B0, PROJ_K2):
                        high(u)
                    for u in range(PROJ_B0, PROJ_K2):
                        middle(u)
                for i in range(TPB):
                    u = first_of(blk) + i
                    high(u)
                    if blk < 2 and i > 0:
                        middle(u - 1)
                    values(TPB * blk + i)
                    if blk >= 2:
                        middle(u)
                    if blk < 2 and i == 1:
                        turn_copy(LN1, blk + 1)
                if blk < 2:
                    middle(first_of(blk) + TPB - 1)

            def max_copy(e, half):
                eng.wait_ge(m_turned, e + 1)
                eng.activation(mT[0:96, half, :], ps_b[0:96, 0:P], ACT.Copy).then_inc(m_copied, 1)

            su = [0]

            def setup_done(dst, m, n, bias=None, view=lambda v: v):
                k = su[0]
                su[0] += 1
                eng.wait_ge(su_full, k + 1)
                src = view(ps[0:m, 6 + k % 2, 0:n])
                if bias is None:
                    eng.activation(dst, src, ACT.Copy).then_inc(su_done, 1)
                else:
                    eng.activation(dst, src, ACT.Identity, bias=bias).then_inc(su_done, 1)

            eng.wait_ge(pool_step, CONSTS)
            for b in range(B):
                setup_done(v2[0:CTX, b, :, :].rearrange("p g (h d) -> p (g h) d", h=HG)[:, :, 0:DH], CTX, D,
                           view=lambda v: v.rearrange("p (h d) -> p h d", h=H))
            for dst, c0 in ((kT, COL_BK), (vT, COL_BV)):
                for o in range(NC):
                    setup_done(dst[:, o, :], P, B * CTX, bias=cols[:, c0 + o:c0 + o + 1])
            max_copy(0, 0)
            for o in range(NC):
                setup_done(g1[:, o, :], P, B * CTX)
            setup_done(cb[:, 0, :], P, B * CTX)
            for b in range(B):
                setup_done(vw[0:CTX, b, :], CTX, D)

            def chain(n, b):
                att, ln = ((ATT1, LN2), (ATT2, LN3))[n]
                for blk in (2 * b, 2 * b + 1):
                    turn_copy(att, blk)
                    yield
                for _ in range(KC):
                    yield
                u = PROJ_2 + 2 * NC * b
                first = u
                for blk in (2 * b, 2 * b + 1):
                    turn_copy(ln, blk)
                    if u > first and n == 0:
                        middle(u - 1)
                    yield
                    if n == 0:
                        for o in range(NC):
                            high(u)
                            if o > 0:
                                middle(u - 1)
                            u += 1
                            yield
                if n == 0:
                    middle(u - 1)
                    yield

            def exps(g, k, pr, first=False):
                G = num(g)
                for h in (2 * pr, 2 * pr + 1):
                    eng.wait_ge(st_full, 64 * G + 4 * k + h + 1)
                    if h == 0 and not (first and k < 2):
                        eng.wait_ge(pv_done, 16 * G + k - 1)
                    eng.activation(probs[:, k % 2, h, :], ps[:, st_bank(g, k, h), :], ACT.Exp, scale=SCALE).then_inc(exp_done, 1)

            def out_copy(e, half):
                eng.wait_ge(pv_done, 8 * e + 8)
                eng.wait_ge(out_turned, EARLY + e - 1)
                eng.activation(outT[:, half, :], ps[:, PV, :], ACT.Copy).then_inc(out_copied, 1)

            def step(g, k, lead=True, first=False):
                G = num(g)
                if k == 1 and not first:
                    out_copy(2 * G - 1, 1)
                if k == 9:
                    out_copy(2 * G, 0)
                exps(g, k, 0, first)
                if k == 6:
                    max_copy(2 * G + 1, 1)
                if k == 14 and lead:
                    max_copy(2 * G + 2, 0)
                exps(g, k, 1, first)

            def self_group(g, lead=True, chain=None):
                for k in range(LEAD, 16):
                    step(g, k, lead)
                    if not lead:
                        advance(chain, TAIL[k - LEAD])
                if lead:
                    for k in range(LEAD):
                        step(after(g), k)

            parts_stored(eng, PROJ_2)
            for s in range(2):
                eng.wait_ge(v_out[s], 16 * TILES // 4)
            for k in range(LEAD):
                step((0, 0), k, first=True)
            with eng.Fori(0, LAST_PAIR) as gp:
                self_group((gp, 0))
                self_group((gp, 1))
            self_group((LAST_PAIR, 0))
            self_group((LAST_PAIR, 1), lead=False, chain=chain(0, 0))
            out_copy(2 * GROUPS - 1, 1)

            def w1_high(f):
                eng.activation(wff1_hi[:, :, :, f, :], wff1_v[:, :, :, f, :], ACT.Copy).then_inc(w1_hi, 1)

            def x_high(blk):
                if blk == 0:
                    eng.wait_ge(lo_done, len(PROJ))
                elif blk == 1:
                    eng.wait_ge(out_turned, EARLY + 4 * GROUPS)
                else:
                    eng.wait_ge(ff_full, FC * (blk - 1))
                eng.wait_ge(turn_done, 2 * TURNS.index((LN3, blk)) + 2)
                eng.activation(x_hi[blk % 2][:, :, :], xT[:, :, BLK * blk:BLK * blk + BLK],
                               ACT.Copy).then_inc(x_hi_done, 1)

            def max_copy_2(G):
                eng.wait_ge(m_turned, 2 * GROUPS + G + 1)
                if G >= 2:
                    eng.wait_ge(m2_in[(G - 2) % 4], 16 * ((G - 2) // 4 + 1))
                eng.activation(mT[0:96, G % 2, :], ps_b[0:96, 0:P], ACT.Copy).then_inc(m_copied, 1)

            def exp_2(G, n):
                half, h = divmod(n, HG)
                eng.wait_ge(st_full, 64 * GROUPS + UNITS * G + n + 1)
                if h == 0:
                    eng.wait_ge(pv_done, 16 * GROUPS + max(2 * G + half - 1, 0))
                eng.activation(probs[0:CTXP, half, h, :], ps[0:CTXP, ST + h % 2, :], ACT.Exp, scale=SCALE).then_inc(exp_done, 1)

            def out_copy_2(G, half):
                e = 2 * GROUPS + 2 * G + half
                eng.wait_ge(pv_done, 16 * GROUPS + 2 * G + half + 1)
                eng.wait_ge(out_turned, EARLY + e - 1)
                eng.activation(outT[:, half, :], ps[:, PV, :], ACT.Copy).then_inc(out_copied, 1)

            def cross_unit(G, n):
                if G < GROUPS:
                    exp_2(G, n)
                if n == 2 and G >= 1:
                    out_copy_2(G - 1, 1)
                if n == 3 and G + 1 < GROUPS:
                    max_copy_2(G + 1)
                if n == 6 and G < GROUPS:
                    out_copy_2(G, 0)

            after_self = chain(0, 1)
            advance(after_self, AHEAD)
            for n, count in enumerate(FIRST_S2):
                if divmod(n, KC) == (1, 3):
                    max_copy_2(0)
                advance(after_self, count)
            after_cross = chain(1, 0)
            for G in range(GROUPS):
                for n in range(UNITS):
                    cross_unit(G, n)
                    advance(after_self if G == 0 else after_cross, pieces(G, n))
            for n in range(6):
                cross_unit(GROUPS, n)
                if n == 0:
                    eng.wait_ge(w_in["wff"], 32)
                    eng.wait_ge(st_full, 64 * GROUPS + UNITS * GROUPS)
                    w1_high(0)
                if n == 1:
                    x_high(0)
                if n == 3:
                    w1_high(1)

            def hid_high(n):
                eng.wait_ge(hid_done, n + 1)
                if n >= HID_RING:
                    chunk_used(eng, n - HID_RING)
                eng.activation(hid_hi[:, n % HID_RING, :], hid[:, n % 2, :], ACT.Copy).then_inc(hid_hi_done, 1)

            parts_stored(eng, len(PROJ))
            after_cross = chain(1, 1)
            for n in range(FC * BLOCKS):
                blk, f = divmod(n, FC)
                eng.wait_ge(ff_gate, n + 1)
                if n >= 2:
                    eng.wait_ge(hid_done, n - 1)
                i = COL_FF + FC + f
                eng.activation(gate[:, n % 2, :], ps[:, GATE, :], ACT.Gelu_apprx_sigmoid,
                               bias=cols[:, i:i + 1]).then_inc(gate_done, 1)
                if n >= 1:
                    hid_high(n - 1)
                if n + 2 < FC:
                    w1_high(n + 2)
                if n < FC:
                    advance(after_cross, FF_PIECES[n])
                if f == 4 and blk + 1 < BLOCKS:
                    x_high(blk + 1)
                done, i = x3_step(n)
                if i == 1:
                    turn_copy(X3, done)
            hid_high(FC * BLOCKS - 1)

            def l1_exps(blk):
                eng.wait_ge(l_max, 2 * (blk + 1))
                for t in range(TPB):
                    eng.activation(s1[:, blk, t, :], s1[:, blk, t, :], ACT.Exp, scale=L1_SCALE, bias=nm1[:, blk, t:t + 1],
                                   accum_out=sum1[:, blk, t:t + 1]).then_inc(l_exp, 1)

            def l1_turn_copy(blk):
                eng.wait_ge(l_turned, blk + 1)
                eng.activation(p1T[0:CTX, blk, :], ps[0:CTX, LINEAR + blk % 2, :], ACT.Copy).then_inc(l_pT, 1)

            def l1_squares(blk):
                for t in range(TPB):
                    n = TPB * blk + t
                    eng.wait_ge(l_y, n + 1)
                    if n >= 1:
                        eng.wait_ge(l_sq, n)
                    eng.activation(sq[:, :], x[:, n, :], ACT.Square, accum_out=ss1[:, blk, t:t + 1]).then_inc(l_sq, 1)

            def l1_scale(blk):
                eng.wait_ge(l_root, blk + 1)
                for t in range(TPB):
                    y = x[:, TPB * blk + t, :]
                    eng.activation(y, y, ACT.Copy, scale=rms[:, blk, t:t + 1]).then_inc(l_scaled, 1)

            last = BLOCKS - 1
            for blk in range(last):
                l1_exps(blk)
            l1_turn_copy(0)
            l1_turn_copy(1)
            turn_copy(X3, last)
            l1_turn_copy(2)
            l1_squares(0)
            l1_exps(last)
            l1_squares(1)
            l1_turn_copy(last)
            l1_scale(0)
            l1_squares(2)
            l1_scale(1)
            l1_squares(last)
            l1_scale(2)

        @block.vector
        def _(eng):
            steps = [0]

            def begin(ins):
                steps[0] += 1
                ins.then_inc(dve_step, 1)
                return steps[0]

            def link(ins):
                eng.wait_ge(dve_step, begin(ins))

            under_way = [iter(())]

            def tick():
                next(under_way[0], None)

            def finish_norm():
                for _ in under_way[0]:
                    pass

            def root_steps(v, y, w, h, scale, e, ready=None):
                for out, ops in ((w, (v, scale, e, ALU.mult, ALU.add)), (h, (w, -0.5, None, ALU.mult)),
                                 (y.bitcast(I32), (w.bitcast(I32), -0.5, float(0x5F3759DF), ALU.mult, ALU.add))):
                    at = begin(eng.tensor_scalar(out, *ops))
                    yield
                    eng.wait_ge(dve_step, at)
                for i in range(3):
                    for in0, in1 in ((y, y), (w, h)):
                        at = begin(eng.tensor_tensor(w, in0, in1, ALU.mult))
                        yield
                        eng.wait_ge(dve_step, at)
                    ins = eng.scalar_tensor_tensor(out=y, in0=w, scalar=1.5, in1=y, op0=ALU.add, op1=ALU.mult)
                    if i == 2 and ready is not None:
                        ins.then_inc(ready, 1)
                        return
                    at = begin(ins)
                    yield
                    eng.wait_ge(dve_step, at)

            def stats(n, blk, t):
                k = BLOCKS * n + blk
                if k >= 1:
                    eng.wait_ge(var_ready, TPB * (k - 1) + t + 1)
                if k >= 2:
                    eng.wait_ge(tok_ready, TPB * (k - 1))
                link(eng.bn_stats(st[:, t, :], x[:, TPB * blk + t, :]))
                eng.bn_aggr(mv[:, blk % 2, t, :], st[:, t, :]).then_inc(var_ready, 1)

            def norm_steps(n, blk):
                s = blk % 2
                eng.wait_ge(var_ready, TPB * (BLOCKS * n + blk + 1))
                yield from root_steps(mv[:, s, :, 1], rstd[:, s, :], var[:, s, :], half_var[:, s, :], 1.0, LN_EPS)
                for t in range(TPB):
                    i = TPB * blk + t
                    eng.tensor_scalar(tok[:, i, :], x[:, i, :], mv[:, s, t, 0:1], rstd[:, s, t:t + 1],
                                      ALU.subtract, ALU.mult).then_inc(tok_ready, 1)
                    yield

            def norm(n, blk):
                for _ in norm_steps(n, blk):
                    pass

            def remainder(u):
                n = width(u)
                eng.wait_ge(hi_done, u + 1)
                if u >= 2:
                    eng.wait_ge(mid_done, u - 1)
                    eng.wait_ge(lo_done, u - 1)
                eng.tensor_tensor(rest[:, u % 2, 0:n], ps[:, proj_bank(u), 0:n], part(u)[:, 0, :],
                                  ALU.subtract).then_inc(rest_done, 1)

            def low(u):
                n = width(u)
                eng.wait_ge(mid_done, u + 1)
                eng.wait_ge(rest_done, u + 1)
                eng.tensor_tensor(part(u)[:, 2, :], rest[:, u % 2, 0:n], part(u)[:, 1, :],
                                  ALU.subtract).then_inc(lo_done, 1)

            def reduce_tile(g, j, i):
                G = num(g)
                half, jj = divmod(j, 8)
                h, t0 = jj // 2, 2 * (jj % 2)
                eng.wait_ge(s_full, 32 * G + 2 * j + i + 1)
                k = 4 * h + t0 + i
                eng.tensor_reduce(mm[:, half, k:k + 1], ps[:, 2 * i:2 * i + 2, :], AX.XY, ALU.max).then_inc(s_red, 1)

            def reduce_(g, j):
                for i in range(2):
                    reduce_tile(g, j, i)

            def split_max(e, s, n):
                p = mpart[:, s, 0:PARTS * n].rearrange("p (i n) -> p i n", i=PARTS)
                eng.tensor_scalar(p[:, 0, :], mm[:, s, 0:n], -1.0, None, ALU.mult).then_inc(m_step, 1)
                eng.wait_ge(m_step, 4 * e + 1)
                eng.scalar_tensor_tensor(out=mrest[:, s, 0:n], in0=mm[:, s, 0:n], scalar=-1.0, in1=p[:, 0, :],
                                         op0=ALU.mult, op1=ALU.subtract).then_inc(m_step, 1)
                eng.wait_ge(m_step, 4 * e + 2)
                eng.tensor_copy(p[:, 1, :], mrest[:, s, 0:n]).then_inc(m_step, 1)
                eng.wait_ge(m_step, 4 * e + 3)
                eng.tensor_tensor(p[:, 2, :], mrest[:, s, 0:n], p[:, 1, :], ALU.subtract).then_inc(m_step, 1)

            def maxima(g, half):
                G = num(g)
                e = 2 * G + half
                eng.wait_ge(s_red, 32 * G + 16 * half + 16)
                split_max(e, half, 16)

            eng.sem_inc(att_done, EARLY)
            for blk in range(2):
                eng.wait_ge(x_in[blk], 16)
                for t in range(TPB):
                    stats(0, blk, t)
                norm(0, blk)
            for blk in range(2):
                eng.wait_ge(x_in[blk + 2], 16)
                for i in range(TPB):
                    u = first_of(blk) + i
                    remainder(u)
                    if i > 0:
                        low(u - 1)
                    if i < 2:
                        stats(0, blk + 2, 2 * i)
                        stats(0, blk + 2, 2 * i + 1)
                    if i == 2:
                        norm(0, blk + 2)
                low(u)
            for u in range(PROJ_B0, PROJ_K2):
                remainder(u)
                low(u)
            eng.wait_ge(pool_step, CONSTS)
            eng.wait_ge(w_in["cols"], 16)
            for c in range(NC):
                eng.tensor_scalar(bq_wide[:, c, :], ones[:, :], cols[:, COL_BQ + c:COL_BQ + c + 1], None,
                                  ALU.mult).then_inc(c_bq, 1)

            def first_reduces():
                for j in range(16 - LEAD):
                    for i in range(2):
                        reduce_tile((0, 0), j, i)
                        if (j, i) == (7, 1):
                            maxima((0, 0), 0)
                        yield

            first_tiles = first_reduces()
            for blk in range(2, BLOCKS):
                for i in range(TPB):
                    u = first_of(blk) + i
                    remainder(u)
                    if TPB * (blk - 2) + i >= FIRST_PAIR:
                        next(first_tiles)
                    low(u)
                    if TPB * (blk - 2) + i >= FIRST_PAIR:
                        next(first_tiles)

            def add(n, i):
                k = TILES * n + i
                eng.wait_ge(y_full, k + 1)
                eng.wait_ge(bias_added, BLOCKS * n + i // TPB + 1)
                eng.tensor_tensor(x[:, i, :], ps[:, out_bank(k), 0:D], x[:, i, :], ALU.add).then_inc(y_added, 1)

            def chain(n, b):
                for _ in range(2):
                    yield
                for i in range(KC):
                    blk, t = divmod(KC * b + i, TPB)
                    add(n, KC * b + i)
                    tick()
                    if t > 0:
                        eng.wait_ge(y_added, TILES * n + KC * b + i)
                        stats(n + 1, blk, t - 1)
                        tick()
                    if t == TPB - 1:
                        eng.wait_ge(y_added, TILES * n + KC * b + i + 1)
                        stats(n + 1, blk, t)
                        finish_norm()
                        under_way[0] = norm_steps(n + 1, blk)
                        if n == b or blk % 2 == 1:
                            finish_norm()
                    tick()
                    yield
                    tick()
                u = PROJ_2 + 2 * NC * b
                for i in range(2):
                    if i > 0:
                        finish_norm()
                        if n == 0:
                            low(u - 1)
                    yield
                    if n == 0:
                        for o in range(NC):
                            remainder(u)
                            if o > 0:
                                low(u - 1)
                            u += 1
                            yield
                if n == 0:
                    low(u - 1)
                    yield

            def step(g, k, lead=True, first=False):
                if k < LEAD:
                    reduce_(g, k + 16 - LEAD)
                elif lead:
                    reduce_(after(g), k - LEAD)
                if k == 2 and not first:
                    attended(before(g), 1)
                if k == 3:
                    maxima(g, 1)
                if k == 10:
                    attended(g, 0)
                if k == 11 and lead:
                    maxima(after(g), 0)

            def before(g):
                return (g[0], 0) if g[1] == 1 else (g[0] - 1, 1)

            def attended(g, half):
                e = 2 * num(g) + half
                eng.wait_ge(out_turned, EARLY + e + 1)
                v = ps[:, MISC, :].rearrange("p (t h d) -> p t h d", t=TPB, h=HG)
                r = rec[:, half, :].rearrange("p (t h) -> p t h", t=TPB)
                eng.reciprocal(r, v[:, :, :, DH]).then_inc(rec_done, 1)
                eng.wait_ge(rec_done, e + 1)
                pair = g[0] % (GROUPS // 2) if isinstance(g[0], int) else g[0]
                n = TPB * P
                start = 2 * n * pair + n * half
                dst = by_group[:, start:start + n] if isinstance(start, int) else by_group[:, bass.ds(start, n)]
                dst = dst.rearrange("p (t x) -> p t x", t=TPB)[:, :, 64 * g[1]:64 * g[1] + 64].rearrange("p t (h d) -> p t h d", h=HG)
                eng.tensor_tensor(dst, v[:, :, :, 0:DH], r.unsqueeze(3).to_broadcast([P, TPB, HG, DH]), ALU.mult).then_inc(att_done, 1)

            by_group = tok[:, :, :].rearrange("p t d -> p (t d)")

            def self_group(g, lead=True, chain=None):
                for k in range(LEAD, 16):
                    step(g, k, lead)
                    if not lead:
                        advance(chain, TAIL[k - LEAD])
                if lead:
                    for k in range(LEAD):
                        step(after(g), k)

            for _ in first_tiles:
                pass
            for k in range(LEAD):
                step((0, 0), k, first=True)
            with eng.Fori(0, LAST_PAIR) as gp:
                self_group((gp, 0))
                self_group((gp, 1))
            self_group((LAST_PAIR, 0))
            self_group((LAST_PAIR, 1), lead=False, chain=chain(0, 0))
            attended((LAST_PAIR, 1), 1)

            def w1_low(f):
                lo, w, hi = (v[:, :, :, f, :] for v in (wff1_lo, wff1_v, wff1_hi))
                eng.wait_ge(w1_hi, f + 1)
                eng.tensor_tensor(lo, w, hi.bitcast(F32), ALU.subtract).then_inc(w1_lo, 1)

            def x_low(blk):
                cut = slice(BLK * blk, BLK * blk + BLK)
                eng.wait_ge(x_hi_done, blk + 1)
                eng.tensor_tensor(x_lo[:, :, cut], xT[:, :, cut], x_hi[blk % 2][:, :, :].bitcast(F32), ALU.subtract).then_inc(x_lo_done, 1)

            def reduce_2(G, t):
                n = KC * G + t
                eng.wait_ge(s2_full, n + 1)
                dst = mm[:, G % 2, :].rearrange("p (f h t) -> p f h t", f=2, h=HG)[:, t // TPB, :, t % TPB]
                eng.tensor_reduce(dst, ps[:, n % 2, 0:HG * CTX].rearrange("p (h n) -> p h n", h=HG),
                                  AX.X, ALU.max).then_inc(s2_red, 1)
                tick()
                if t == KC - 1:
                    eng.wait_ge(s2_red, KC * (G + 1))
                    split_max(2 * GROUPS + G, G % 2, 32)

            def attended_2(G, half):
                attended((GROUPS // 2 + G // 2, G % 2), half)
                tick()

            def cross_unit(G, n):
                if G + 2 < GROUPS:
                    reduce_2(G + 2, n)
                if n == 1 and G >= 1:
                    attended_2(G - 1, 0)
                if n == 5 and G >= 1:
                    attended_2(G - 1, 1)

            after_self = chain(0, 1)
            advance(after_self, AHEAD)
            for n, count in enumerate(FIRST_S2):
                reduce_2(*divmod(n, KC))
                advance(after_self, count)
            after_cross = chain(1, 0)
            for G in range(GROUPS):
                for n in range(UNITS):
                    cross_unit(G, n)
                    advance(after_self if G == 0 else after_cross, pieces(G, n))
            for n in range(6):
                cross_unit(GROUPS, n)
                if n == 1:
                    w1_low(0)
                if n == 2:
                    x_low(0)
                if n == 3:
                    w1_low(1)

            def hidden(n):
                f = n % FC
                eng.wait_ge(ff_full, n + 1)
                eng.wait_ge(gate_done, n + 1)
                if n >= 2:
                    eng.wait_ge(hid_hi_done, n - 1)
                    eng.wait_ge(hid_lo_done, n - 1)
                eng.scalar_tensor_tensor(out=hid[:, n % 2, :], in0=ps[:, LINEAR, :],
                                         scalar=cols[:, COL_FF + f:COL_FF + f + 1], in1=gate[:, n % 2, :],
                                         op0=ALU.add, op1=ALU.mult).then_inc(hid_done, 1)

            def hid_low(n):
                eng.wait_ge(hid_hi_done, n + 1)
                eng.tensor_tensor(hid_lo[:, n % HID_RING, :], hid[:, n % 2, :], hid_hi[:, n % HID_RING, :].bitcast(F32),
                                  ALU.subtract).then_inc(hid_lo_done, 1)

            def l1_max(blk):
                b = blk // 2
                eng.wait_ge(l_full, blk + 1)
                eng.tensor_tensor(s1[:, blk, :, :], ps[:, CHAIN, 0:TPB * CTX].rearrange("p (t n) -> p t n", t=TPB),
                                  cb[:, 0:1, CTX * b:CTX * b + CTX].to_broadcast([P, TPB, CTX]), ALU.add).then_inc(l_added, 1)
                eng.wait_ge(l_added, blk + 1)
                eng.tensor_reduce(m1[:, blk, :], s1[:, blk, :, :], AX.X, ALU.max).then_inc(l_max, 1)
                eng.wait_ge(l_max, 2 * blk + 1)
                eng.tensor_scalar(nm1[:, blk, :], m1[:, blk, :], -L1_SCALE, None, ALU.mult).then_inc(l_max, 1)

            def l1_residual(blk):
                eng.wait_ge(l_exp, TPB * (blk + 1))
                link(eng.reciprocal(r1[:, blk, :], sum1[:, blk, :]))
                for t in range(TPB):
                    n = TPB * blk + t
                    eng.wait_ge(l_pv, n + 1)
                    eng.scalar_tensor_tensor(out=x[:, n, :], in0=ps[:, WIDE[t], 0:D], scalar=r1[:, blk, t:t + 1],
                                             in1=x[:, n, :], op0=ALU.mult, op1=ALU.add).then_inc(l_y, 1)

            def l1_root(blk):
                eng.wait_ge(l_sq, TPB * (blk + 1))
                for _ in root_steps(ss1[:, blk, :], rms[:, blk, :], ms[:, blk, :], half_ms[:, blk, :], 1.0 / D, RMS_EPS, l_root):
                    pass

            after_cross = chain(1, 1)
            for n in range(FC * BLOCKS + FF_LAG):
                if n < FC * BLOCKS:
                    hidden(n)
                if n + 2 < FC:
                    w1_low(n + 2)
                if 1 <= n <= FC * BLOCKS:
                    hid_low(n - 1)
                if n < FC:
                    advance(after_cross, FF_PIECES[n])
                blk, f = divmod(n, FC)
                if f == 4 and blk + 1 < BLOCKS:
                    x_low(blk + 1)
                blk, f = divmod(n - FF_LAG, FC)
                if n >= FF_LAG and f == FC - 1:
                    for t in range(TPB):
                        add(2, TPB * blk + t)
                blk, i = x3_step(n)
                if i == 2:
                    l1_max(blk)

            last = BLOCKS - 1
            l1_residual(0)
            l1_max(last)
            l1_residual(1)
            l1_root(0)
            l1_residual(2)
            l1_root(1)
            l1_residual(last)
            l1_root(2)
            l1_root(last)
            eng.wait_ge(l_root, BLOCKS)
            for t in range(TPB):
                y = x[:, TPB * last + t, :]
                eng.scalar_tensor_tensor(out=y, in0=y, scalar=rms[:, last, t:t + 1],
                                         in1=rows[:, ROW_W, :], op0=ALU.mult, op1=ALU.mult).then_inc(l_last, 1)


def kernel(**inputs):
    import numpy as np
    import concourse.bacc as bacc
    from concourse.bass_utils import run_bass_kernel_spmd

    v = {k: np.asarray(t) for k, t in inputs.items()}
    l0 = {k[len("L0_xattn_"):]: t for k, t in v.items() if k.startswith("L0_xattn_")}
    l1 = {k[len("L1_xattn_"):]: t for k, t in v.items() if k.startswith("L1_xattn_")}

    def by_feature(w):
        return w.reshape(D, NC, P // DH, DH).transpose(0, 1, 3, 2).reshape(D, D)

    def columns(t):
        return t.reshape(-1, P).T

    arrays = {
        "x": v["x"],
        "ctxT": v["ctx_1024"].transpose(2, 0, 1).reshape(D, B * CTX),
        "cols": np.concatenate(
            [columns(l0[n]) for n in ("ln1_s", "ln1_b", "ln2_s", "ln2_b", "ln3_s", "ln3_b", "bff1")]
            + [columns(l1[n]) for n in ("bq", "bk", "bv")], axis=1),
        "rows": np.stack([l0["bo1"], l0["bo2"], l0["bff2"], l1["norm_w"], l1["bfc"]]),
        "Wq": l1["Wq"], "WkT": l1["Wk"].T, "WvT": l1["Wv"].T, "WfcT": l1["Wfc"].T,
    }
    arrays.update({n: l0[n] for n in ("Wo1", "Wo2", "Wff1", "Wff2")})
    for n in ("Wq1", "Wq2"):
        arrays[n] = by_feature(l0[n])
    for n in ("Wkv1", "Wkv2"):
        arrays[n] = np.concatenate([by_feature(l0[n][:, :D]), l0[n][:, D:]], axis=1)
    arrays = {f"in_{n}": np.ascontiguousarray(t) for n, t in arrays.items()}

    nc = bacc.Bacc("TRN2", target_bir_lowering=False, num_devices=1)
    aps = {n[3:]: nc.dram_tensor(n, t.shape, mybir.dt.from_np(t.dtype), kind="ExternalInput").ap()
           for n, t in arrays.items()}
    aps["out"] = nc.dram_tensor("out", (B, S, D), F32, kind="ExternalOutput").ap()
    build(nc, aps)
    result = run_bass_kernel_spmd(nc, [arrays], core_ids=[0])
    return result.results[0]["out"]
```
